# Optimizing a Trainium2 kernel written in Bass

```python
import numpy as np
import jax
import jax.numpy as jnp

def _softmax(x, axis=-1):
    return jax.nn.softmax(x, axis=axis)

def _gelu(x):
    return jax.nn.gelu(x, approximate=True)

def _silu(x):
    return jax.nn.silu(x)

def _sigmoid(x):
    return jax.nn.sigmoid(x)

def _layernorm(x, axis=-1, eps=1e-05):
    m = jnp.mean(x, axis=axis, keepdims=True)
    v = jnp.var(x, axis=axis, keepdims=True)
    return (x - m) / jnp.sqrt(v + eps)

def _scatter_add(tgt, idx, src, axis=0):
    return tgt.at[idx].add(src)

def _segment_sum(src, seg, n):
    return jax.ops.segment_sum(src, seg, n)
kernel_name = 'mk_early_fusion_d2_tok_img512_r4_91f8c4'

def setup_inputs(seed: int=0):
    np.random.seed(seed)
    _w = jnp.asarray

    def _rec_inputs():
        import jax
        import jax.numpy as jnp
        _rk = jax.random.key(seed)
        x = -0.000147625 + 0.999875 * jax.random.normal(jax.random.fold_in(_rk, 1), (64, 3, 224, 224), jnp.float32)
        txt = 0.00355565 + 0.408319 * jax.random.normal(jax.random.fold_in(_rk, 2), (64, 77, 128), jnp.float32)
        return (x, txt)
    x, txt = _rec_inputs()

    def _L0_tok_setup():
        import jax, jax.numpy as jnp
        import numpy as np
        N_PATCHES = 8
        PATCH = 28
        C = 3
        IN_D = C * PATCH * PATCH
        HID = 128
        SEQ = N_PATCHES * N_PATCHES + 1

        def _positional_embedding(seq_len, dim):
            i = np.arange(seq_len)[:, None].astype(np.float32)
            j = np.arange(dim)[None, :].astype(np.float32)
            ang = i / np.power(100000.0, j / dim)
            pe = np.where(j % 2 == 0, np.sin(ang), np.cos(ang))
            return jnp.asarray(pe, dtype=jnp.float32)
        key = jax.random.key(seed)
        k1, k2, k3, k4 = jax.random.split(key, 4)
        B = 64
        X = jax.random.normal(k1, (B, C, 224, 224), dtype=jnp.float32)
        bound = 1.0 / np.sqrt(IN_D)
        W = jax.random.uniform(k2, (HID, IN_D), minval=-bound, maxval=bound, dtype=jnp.float32)
        b = jax.random.uniform(k3, (HID,), minval=-bound, maxval=bound, dtype=jnp.float32)
        class_token = jax.random.uniform(k4, (1, HID), dtype=jnp.float32)
        pos_embed = _positional_embedding(SEQ, HID)
        return {'X': X, 'W': W, 'b': b, 'class_token': class_token, 'pos_embed': pos_embed}
    _L0_tok_all = _L0_tok_setup()
    _L0_tok_in = {k: v for k, v in _L0_tok_all.items() if k in ('W', 'b', 'class_token', 'pos_embed')}
    del _L0_tok_all

    def _L0_attn_setup():
        import jax, jax.numpy as jnp
        import numpy as np
        H, KVH, HD, DN, DR = (8, 2, 64, 32, 32)
        EPS = 1e-06
        ROPE_BASE = 500000.0

        def _rms(x, w):
            return w * (x * jax.lax.rsqrt(jnp.mean(x * x, axis=-1, keepdims=True) + EPS))

        def _rope_tables(T):
            inv_freq = 1.0 / ROPE_BASE ** (np.arange(0, DR, 2, dtype=np.float32) / DR)
            freqs = np.outer(np.arange(T, dtype=np.float32), inv_freq)
            emb = np.concatenate([freqs, freqs], axis=-1)
            return (jnp.asarray(np.cos(emb)), jnp.asarray(np.sin(emb)))

        def _apply_rope(x, cos, sin):
            x1, x2 = jnp.split(x, 2, axis=-1)
            rot = jnp.concatenate([-x2, x1], axis=-1)
            return x * cos[None, None] + rot * sin[None, None]
        key = jax.random.key(seed)
        ks = jax.random.split(key, 10)
        std = 0.02
        mup = (256.0 / 512.0) ** 0.5
        return {'x': jax.random.normal(ks[0], (4, 512, 128), jnp.float32), 'W_DQ': jax.random.normal(ks[1], (128, 64), jnp.float32) * std, 'W_UQ': jax.random.normal(ks[2], (64, H * DN), jnp.float32) * std, 'W_QR': jax.random.normal(ks[3], (64, H * DR), jnp.float32) * std, 'W_DKV': jax.random.normal(ks[4], (128, 128), jnp.float32) * std, 'W_UK': jax.random.normal(ks[5], (128, KVH * DN), jnp.float32) * std, 'W_UV': jax.random.normal(ks[6], (128, KVH * HD), jnp.float32) * std, 'W_KR': jax.random.normal(ks[7], (128, KVH * DR), jnp.float32) * std, 'W_VR': jax.random.normal(ks[8], (128, H * HD), jnp.float32) * std * mup, 'W_O': jax.random.normal(ks[9], (H * HD, 128), jnp.float32) * std * mup, 'q_ln_w': jnp.ones((64,), jnp.float32), 'kv_ln_w': jnp.ones((128,), jnp.float32), 'q_head_norm_w': jnp.ones((HD,), jnp.float32), 'k_head_norm_w': jnp.ones((HD,), jnp.float32)}
    _L0_attn_all = _L0_attn_setup()
    _L0_attn_in = {k: v for k, v in _L0_attn_all.items() if k in ('W_DQ', 'W_UQ', 'W_QR', 'W_DKV', 'W_UK', 'W_UV', 'W_KR', 'W_VR', 'W_O', 'q_ln_w', 'kv_ln_w', 'q_head_norm_w', 'k_head_norm_w')}
    del _L0_attn_all

    def _L0_ffn_setup():
        import jax, jax.numpy as jnp
        import numpy as np
        B, S, D, H, E = (4, 512, 128, 8, 8)
        FF = 4 * D
        HD = D // H
        EPS = 1e-05

        def _layernorm(x, g, b):
            mu = jnp.mean(x, axis=-1, keepdims=True)
            var = jnp.mean((x - mu) ** 2, axis=-1, keepdims=True)
            return (x - mu) * jax.lax.rsqrt(var + EPS) * g + b
        key = jax.random.key(seed)
        ks = jax.random.split(key, 16)
        s = 0.02
        return {'x': jax.random.normal(ks[0], (B, S, D), dtype=jnp.float32), 'ln1_g': jnp.ones((D,), jnp.float32), 'ln1_b': jnp.zeros((D,), jnp.float32), 'Wq': jax.random.normal(ks[1], (D, D), jnp.float32) * s, 'bq': jnp.zeros((D,), jnp.float32), 'Wk': jax.random.normal(ks[2], (D, D), jnp.float32) * s, 'bk': jnp.zeros((D,), jnp.float32), 'Wv': jax.random.normal(ks[3], (D, D), jnp.float32) * s, 'bv': jnp.zeros((D,), jnp.float32), 'Wo': jax.random.normal(ks[4], (D, D), jnp.float32) * s, 'bo': jnp.zeros((D,), jnp.float32), 'gate_W': jax.random.normal(ks[5], (D, E), jnp.float32) * s, 'gate_b': jnp.zeros((E,), jnp.float32), 'W1': jax.random.normal(ks[6], (E, D, FF), jnp.float32) * s, 'b1': jnp.zeros((E, FF), jnp.float32), 'W2': jax.random.normal(ks[7], (E, FF, D), jnp.float32) * s, 'b2': jnp.zeros((E, D), jnp.float32)}
    _L0_ffn_all = _L0_ffn_setup()
    _L0_ffn_in = {k: v for k, v in _L0_ffn_all.items() if k in ('ln1_g', 'ln1_b', 'Wq', 'bq', 'Wk', 'bk', 'Wv', 'bv', 'Wo', 'bo', 'gate_W', 'gate_b', 'W1', 'b1', 'W2', 'b2')}
    del _L0_ffn_all

    def _L1_attn_setup():
        import jax, jax.numpy as jnp
        import numpy as np
        DIM = 128
        MAX_LEN = 128
        SHARED = 128
        EXPAND = DIM * 2
        PROJ = 2 * EXPAND + SHARED
        EPS = 1e-06
        BATCH = 32

        def _rope(x):
            b, n, m = x.shape
            half = m // 2
            pos = jnp.arange(n, dtype=x.dtype)
            inv_freq = 10000.0 ** (-jnp.arange(half, dtype=x.dtype) / half)
            sinusoid = pos[:, None] * inv_freq[None, :]
            sin = jnp.sin(sinusoid)[None]
            cos = jnp.cos(sinusoid)[None]
            x1, x2 = jnp.split(x, 2, axis=-1)
            return jnp.concatenate([x1 * cos - x2 * sin, x2 * cos + x1 * sin], axis=-1)
        key = jax.random.key(seed)
        ks = jax.random.split(key, 5)
        x = jax.random.normal(ks[0], (BATCH, MAX_LEN, DIM), jnp.float32)
        W1 = jax.random.normal(ks[1], (DIM, PROJ), jnp.float32) * 0.02
        b1 = jnp.zeros((PROJ,), jnp.float32)
        W2 = jax.random.normal(ks[2], (EXPAND, DIM), jnp.float32) * 0.02
        b2 = jnp.zeros((DIM,), jnp.float32)
        gamma = jax.random.normal(ks[3], (2, SHARED), jnp.float32) * 0.02
        beta = jnp.zeros((2, SHARED), jnp.float32)
        norm_scale = jnp.ones((), jnp.float32)
        return dict(x=x, W1=W1, b1=b1, W2=W2, b2=b2, gamma=gamma, beta=beta, norm_scale=norm_scale)
    _L1_attn_all = _L1_attn_setup()
    _L1_attn_in = {k: v for k, v in _L1_attn_all.items() if k in ('W1', 'b1', 'W2', 'b2', 'gamma', 'beta', 'norm_scale')}
    del _L1_attn_all

    def _L1_ffn_setup():
        import jax, jax.numpy as jnp
        import numpy as np
        NUM_TILES = 64
        TPC = 8
        GRID = 16
        EPS = 1e-05
        key = jax.random.key(seed)
        ks = jax.random.split(key, 6)
        B, S, D, T, DH, G = (2, 256, 128, NUM_TILES, 128, GRID)
        x = jax.random.normal(ks[0], (B, S, D), dtype=jnp.float32)
        gamma = jnp.ones((D,), jnp.float32)
        beta = jnp.zeros((D,), jnp.float32)
        Wd = jax.random.normal(ks[1], (T, DH, D), dtype=jnp.float32) * 0.02
        spline_bases = jax.random.normal(ks[2], (T, DH, G), dtype=jnp.float32) * 0.1
        spline_slopes = jax.random.normal(ks[3], (T, DH, G), dtype=jnp.float32) * 0.1
        Wu = jax.random.normal(ks[4], (T, D, DH), dtype=jnp.float32) * 0.02
        scale = jnp.full((T,), 0.1, jnp.float32)
        return {'x': x, 'gamma': gamma, 'beta': beta, 'Wd': Wd, 'spline_bases': spline_bases, 'spline_slopes': spline_slopes, 'Wu': Wu, 'scale': scale}
    _L1_ffn_all = _L1_ffn_setup()
    _L1_ffn_in = {k: v for k, v in _L1_ffn_all.items() if k in ('gamma', 'beta', 'Wd', 'spline_bases', 'spline_slopes', 'Wu', 'scale')}
    del _L1_ffn_all
    return {'x': x, 'txt': txt, 'L0_tok_W': _L0_tok_in['W'], 'L0_tok_b': _L0_tok_in['b'], 'L0_tok_class_token': _L0_tok_in['class_token'], 'L0_tok_pos_embed': _L0_tok_in['pos_embed'], 'L0_attn_W_DQ': _L0_attn_in['W_DQ'], 'L0_attn_W_UQ': _L0_attn_in['W_UQ'], 'L0_attn_W_QR': _L0_attn_in['W_QR'], 'L0_attn_W_DKV': _L0_attn_in['W_DKV'], 'L0_attn_W_UK': _L0_attn_in['W_UK'], 'L0_attn_W_UV': _L0_attn_in['W_UV'], 'L0_attn_W_KR': _L0_attn_in['W_KR'], 'L0_attn_W_VR': _L0_attn_in['W_VR'], 'L0_attn_W_O': _L0_attn_in['W_O'], 'L0_attn_q_ln_w': _L0_attn_in['q_ln_w'], 'L0_attn_kv_ln_w': _L0_attn_in['kv_ln_w'], 'L0_attn_q_head_norm_w': _L0_attn_in['q_head_norm_w'], 'L0_attn_k_head_norm_w': _L0_attn_in['k_head_norm_w'], 'L0_ffn_ln1_g': _L0_ffn_in['ln1_g'], 'L0_ffn_ln1_b': _L0_ffn_in['ln1_b'], 'L0_ffn_Wq': _L0_ffn_in['Wq'], 'L0_ffn_bq': _L0_ffn_in['bq'], 'L0_ffn_Wk': _L0_ffn_in['Wk'], 'L0_ffn_bk': _L0_ffn_in['bk'], 'L0_ffn_Wv': _L0_ffn_in['Wv'], 'L0_ffn_bv': _L0_ffn_in['bv'], 'L0_ffn_Wo': _L0_ffn_in['Wo'], 'L0_ffn_bo': _L0_ffn_in['bo'], 'L0_ffn_gate_W': _L0_ffn_in['gate_W'], 'L0_ffn_gate_b': _L0_ffn_in['gate_b'], 'L0_ffn_W1': _L0_ffn_in['W1'], 'L0_ffn_b1': _L0_ffn_in['b1'], 'L0_ffn_W2': _L0_ffn_in['W2'], 'L0_ffn_b2': _L0_ffn_in['b2'], 'L1_attn_W1': _L1_attn_in['W1'], 'L1_attn_b1': _L1_attn_in['b1'], 'L1_attn_W2': _L1_attn_in['W2'], 'L1_attn_b2': _L1_attn_in['b2'], 'L1_attn_gamma': _L1_attn_in['gamma'], 'L1_attn_beta': _L1_attn_in['beta'], 'L1_attn_norm_scale': _L1_attn_in['norm_scale'], 'L1_ffn_gamma': _L1_ffn_in['gamma'], 'L1_ffn_beta': _L1_ffn_in['beta'], 'L1_ffn_Wd': _L1_ffn_in['Wd'], 'L1_ffn_spline_bases': _L1_ffn_in['spline_bases'], 'L1_ffn_spline_slopes': _L1_ffn_in['spline_slopes'], 'L1_ffn_Wu': _L1_ffn_in['Wu'], 'L1_ffn_scale': _L1_ffn_in['scale']}

def reference(x, txt, L0_tok_W, L0_tok_b, L0_tok_class_token, L0_tok_pos_embed, L0_attn_W_DQ, L0_attn_W_UQ, L0_attn_W_QR, L0_attn_W_DKV, L0_attn_W_UK, L0_attn_W_UV, L0_attn_W_KR, L0_attn_W_VR, L0_attn_W_O, L0_attn_q_ln_w, L0_attn_kv_ln_w, L0_attn_q_head_norm_w, L0_attn_k_head_norm_w, L0_ffn_ln1_g, L0_ffn_ln1_b, L0_ffn_Wq, L0_ffn_bq, L0_ffn_Wk, L0_ffn_bk, L0_ffn_Wv, L0_ffn_bv, L0_ffn_Wo, L0_ffn_bo, L0_ffn_gate_W, L0_ffn_gate_b, L0_ffn_W1, L0_ffn_b1, L0_ffn_W2, L0_ffn_b2, L1_attn_W1, L1_attn_b1, L1_attn_W2, L1_attn_b2, L1_attn_gamma, L1_attn_beta, L1_attn_norm_scale, L1_ffn_gamma, L1_ffn_beta, L1_ffn_Wd, L1_ffn_spline_bases, L1_ffn_spline_slopes, L1_ffn_Wu, L1_ffn_scale):
    import jax
    import jax.numpy as jnp

    def _L0_tok_ref(X, W, b, class_token, pos_embed):
        import jax, jax.numpy as jnp
        import numpy as np
        N_PATCHES = 8
        PATCH = 28
        C = 3
        IN_D = C * PATCH * PATCH
        HID = 128
        SEQ = N_PATCHES * N_PATCHES + 1

        def _positional_embedding(seq_len, dim):
            i = np.arange(seq_len)[:, None].astype(np.float32)
            j = np.arange(dim)[None, :].astype(np.float32)
            ang = i / np.power(100000.0, j / dim)
            pe = np.where(j % 2 == 0, np.sin(ang), np.cos(ang))
            return jnp.asarray(pe, dtype=jnp.float32)
        B = X.shape[0]
        patches = X.reshape(B, C, N_PATCHES, PATCH, N_PATCHES, PATCH)
        patches = patches.transpose(0, 2, 4, 1, 3, 5).reshape(B, N_PATCHES * N_PATCHES, IN_D)
        tokens = jnp.einsum('bpi,hi->bph', patches, W) + b
        cls = jnp.broadcast_to(class_token[None, :, :], (B, 1, HID))
        tokens = jnp.concatenate([cls, tokens], axis=1)
        return tokens * pos_embed[None, :, :]

    def _L0_attn_ref(x, W_DQ, W_UQ, W_QR, W_DKV, W_UK, W_UV, W_KR, W_VR, W_O, q_ln_w, kv_ln_w, q_head_norm_w, k_head_norm_w):
        import jax, jax.numpy as jnp
        import numpy as np
        H, KVH, HD, DN, DR = (8, 2, 64, 32, 32)
        EPS = 1e-06
        ROPE_BASE = 500000.0

        def _rms(x, w):
            return w * (x * jax.lax.rsqrt(jnp.mean(x * x, axis=-1, keepdims=True) + EPS))

        def _rope_tables(T):
            inv_freq = 1.0 / ROPE_BASE ** (np.arange(0, DR, 2, dtype=np.float32) / DR)
            freqs = np.outer(np.arange(T, dtype=np.float32), inv_freq)
            emb = np.concatenate([freqs, freqs], axis=-1)
            return (jnp.asarray(np.cos(emb)), jnp.asarray(np.sin(emb)))

        def _apply_rope(x, cos, sin):
            x1, x2 = jnp.split(x, 2, axis=-1)
            rot = jnp.concatenate([-x2, x1], axis=-1)
            return x * cos[None, None] + rot * sin[None, None]
        B, T, D = x.shape
        cos, sin = _rope_tables(T)
        c_q = _rms(x @ W_DQ, q_ln_w)
        q_nope = (c_q @ W_UQ).reshape(B, T, H, DN).transpose(0, 2, 1, 3)
        q_rope = (c_q @ W_QR).reshape(B, T, H, DR).transpose(0, 2, 1, 3)
        c_kv = _rms(x @ W_DKV, kv_ln_w)
        k_nope = (c_kv @ W_UK).reshape(B, T, KVH, DN).transpose(0, 2, 1, 3)
        v = (c_kv @ W_UV).reshape(B, T, KVH, HD).transpose(0, 2, 1, 3)
        k_rope = (x @ W_KR).reshape(B, T, KVH, DR).transpose(0, 2, 1, 3)
        q_rope = _apply_rope(q_rope, cos, sin)
        k_rope = _apply_rope(k_rope, cos, sin)
        q = jnp.concatenate([q_nope, q_rope], axis=-1)
        k = jnp.concatenate([k_nope, k_rope], axis=-1)
        q = _rms(q, q_head_norm_w)
        k = _rms(k, k_head_norm_w)
        g = H // KVH
        k = jnp.repeat(k, g, axis=1)
        v = jnp.repeat(v, g, axis=1)
        scores = jnp.einsum('bhqd,bhkd->bhqk', q, k) * HD ** (-0.5)
        mask = jnp.tril(jnp.ones((T, T), dtype=bool))
        scores = jnp.where(mask, scores, -jnp.inf)
        attn_w = jax.nn.softmax(scores.astype(jnp.float32), axis=-1).astype(q.dtype)
        attn_out = jnp.einsum('bhqk,bhkd->bhqd', attn_w, v)
        v_res = (x @ W_VR).reshape(B, T, H, HD).transpose(0, 2, 1, 3)
        attn_out = attn_out + v_res
        out = attn_out.transpose(0, 2, 1, 3).reshape(B, T, H * HD)
        return out @ W_O

    def _L0_ffn_ref(x, ln1_g, ln1_b, Wq, bq, Wk, bk, Wv, bv, Wo, bo, gate_W, gate_b, W1, b1, W2, b2):
        import jax, jax.numpy as jnp
        import numpy as np
        B, S, D, H, E = (4, 512, 128, 8, 8)
        FF = 4 * D
        HD = D // H
        EPS = 1e-05

        def _layernorm(x, g, b):
            mu = jnp.mean(x, axis=-1, keepdims=True)
            var = jnp.mean((x - mu) ** 2, axis=-1, keepdims=True)
            return (x - mu) * jax.lax.rsqrt(var + EPS) * g + b
        b, s, d = x.shape
        q = (x @ Wq + bq).reshape(b, s, H, HD)
        k = (x @ Wk + bk).reshape(b, s, H, HD)
        v = (x @ Wv + bv).reshape(b, s, H, HD)
        scores = jnp.einsum('bqhd,bkhd->bhqk', q, k) / jnp.sqrt(jnp.float32(HD))
        attn = jax.nn.softmax(scores, axis=-1)
        o = jnp.einsum('bhqk,bkhd->bqhd', attn, v).reshape(b, s, d) @ Wo + bo
        h = _layernorm(x + o, ln1_g, ln1_b)
        t = h.reshape(b * s, d)
        probs = jax.nn.softmax(t @ gate_W + gate_b, axis=-1)
        idx = jnp.argmax(probs, axis=-1)
        gw = jnp.max(probs, axis=-1)
        hid = jax.nn.gelu(jnp.einsum('nd,edf->enf', t, W1) + b1[:, None, :])
        out_all = jnp.einsum('enf,efd->end', hid, W2) + b2[:, None, :]
        onehot = jax.nn.one_hot(idx, E, dtype=t.dtype)
        out = jnp.einsum('ne,end->nd', onehot, out_all)
        out = out * gw[:, None]
        return out.reshape(b, s, d)

    def _L1_attn_ref(x, W1, b1, W2, b2, gamma, beta, norm_scale):
        import jax, jax.numpy as jnp
        import numpy as np
        DIM = 128
        MAX_LEN = 128
        SHARED = 128
        EXPAND = DIM * 2
        PROJ = 2 * EXPAND + SHARED
        EPS = 1e-06
        BATCH = 32

        def _rope(x):
            b, n, m = x.shape
            half = m // 2
            pos = jnp.arange(n, dtype=x.dtype)
            inv_freq = 10000.0 ** (-jnp.arange(half, dtype=x.dtype) / half)
            sinusoid = pos[:, None] * inv_freq[None, :]
            sin = jnp.sin(sinusoid)[None]
            cos = jnp.cos(sinusoid)[None]
            x1, x2 = jnp.split(x, 2, axis=-1)
            return jnp.concatenate([x1 * cos - x2 * sin, x2 * cos + x1 * sin], axis=-1)
        shortcut = x
        ms = jnp.mean(jnp.square(x), axis=-1, keepdims=True)
        h = x * jax.lax.rsqrt(ms + EPS) * norm_scale
        uv = jax.nn.silu(h @ W1 + b1)
        u, v, base = jnp.split(uv, [EXPAND, 2 * EXPAND], axis=-1)
        qk_base = base[:, :, None, :] * gamma + beta
        q = qk_base[:, :, 0]
        k = qk_base[:, :, 1]
        qk = jnp.einsum('bnd,bmd->bnm', q, k) / MAX_LEN
        qk = _rope(qk)
        kernel = jnp.square(jax.nn.relu(qk))
        out = u * jnp.einsum('bnm,bme->bne', kernel, v)
        return out @ W2 + b2 + shortcut

    def _L1_ffn_ref(x, gamma, beta, Wd, spline_bases, spline_slopes, Wu, scale):
        import jax, jax.numpy as jnp
        import numpy as np
        NUM_TILES = 64
        TPC = 8
        GRID = 16
        EPS = 1e-05
        B, S, D = x.shape
        T, DH, _ = Wd.shape
        C = T // TPC
        N = B * S
        mu = x.mean(-1, keepdims=True)
        var = ((x - mu) ** 2).mean(-1, keepdims=True)
        xn = (x - mu) * jax.lax.rsqrt(var + EPS) * gamma + beta
        xf = xn.reshape(N, D)
        tile_sigs = jnp.sign(Wd.mean(axis=1))
        cluster_sigs = jnp.sign(tile_sigs.reshape(C, TPC, D).mean(1))
        in_sigs = jnp.sign(xf)
        best_c = jnp.argmax(in_sigs @ cluster_sigs.T, axis=-1)
        tile_scores = (in_sigs @ tile_sigs.T).reshape(N, C, TPC)
        sc = jnp.take_along_axis(tile_scores, best_c[:, None, None], axis=1)[:, 0, :]
        local_best = jnp.argmax(sc, axis=-1)
        tidx = best_c * TPC + local_best
        h = jnp.einsum('nd,nhd->nh', xf, Wd[tidx])
        hn = jax.nn.sigmoid(h)
        idx = jnp.clip((hn * GRID).astype(jnp.int32), 0, GRID - 1)
        base = jnp.take_along_axis(spline_bases[tidx], idx[..., None], axis=-1)[..., 0]
        slope = jnp.take_along_axis(spline_slopes[tidx], idx[..., None], axis=-1)[..., 0]
        local_pos = hn * GRID - idx.astype(h.dtype)
        hs = base + slope * local_pos
        y = jnp.einsum('nh,ndh->nd', hs, Wu[tidx]) * scale[tidx][:, None]
        return x + y.reshape(B, S, D)
    h = _L0_tok_ref(x, L0_tok_W, L0_tok_b, L0_tok_class_token, L0_tok_pos_embed)
    h = jnp.concatenate([h, txt], axis=1)
    h = h + _L0_attn_ref(_layernorm(h, axis=-1), L0_attn_W_DQ, L0_attn_W_UQ, L0_attn_W_QR, L0_attn_W_DKV, L0_attn_W_UK, L0_attn_W_UV, L0_attn_W_KR, L0_attn_W_VR, L0_attn_W_O, L0_attn_q_ln_w, L0_attn_kv_ln_w, L0_attn_q_head_norm_w, L0_attn_k_head_norm_w)
    h = h + _L0_ffn_ref(_layernorm(h, axis=-1), L0_ffn_ln1_g, L0_ffn_ln1_b, L0_ffn_Wq, L0_ffn_bq, L0_ffn_Wk, L0_ffn_bk, L0_ffn_Wv, L0_ffn_bv, L0_ffn_Wo, L0_ffn_bo, L0_ffn_gate_W, L0_ffn_gate_b, L0_ffn_W1, L0_ffn_b1, L0_ffn_W2, L0_ffn_b2)
    h = h + _L1_attn_ref(_layernorm(h, axis=-1), L1_attn_W1, L1_attn_b1, L1_attn_W2, L1_attn_b2, L1_attn_gamma, L1_attn_beta, L1_attn_norm_scale)
    h = h + _L1_ffn_ref(_layernorm(h, axis=-1), L1_ffn_gamma, L1_ffn_beta, L1_ffn_Wd, L1_ffn_spline_bases, L1_ffn_spline_slopes, L1_ffn_Wu, L1_ffn_scale)
    return h

_drawn_inputs = setup_inputs


def setup_inputs(seed=0):
    import zlib

    import numpy as np

    out = dict(_drawn_inputs(seed))
    spreads = {'L0_attn_q_ln_w': (1.0, 0.6),
     'L0_attn_kv_ln_w': (1.0, 0.6),
     'L0_attn_q_head_norm_w': (1.0, 0.6),
     'L0_attn_k_head_norm_w': (1.0, 0.6),
     'L0_ffn_ln1_g': (1.0, 0.6),
     'L0_ffn_ln1_b': (0.0, 0.545),
     'L0_ffn_bq': (0.0, 0.8),
     'L0_ffn_bk': (0.0, 0.8),
     'L0_ffn_bv': (0.0, 0.8),
     'L0_ffn_bo': (0.0, 0.632),
     'L0_ffn_gate_b': (0.0, 0.1),
     'L0_ffn_b1': (0.0, 0.741),
     'L0_ffn_b2': (0.0, 0.1),
     'L1_attn_b1': (0.0, 0.8),
     'L1_attn_b2': (0.0, 0.1),
     'L1_attn_beta': (0.0, 0.8),
     'L1_ffn_gamma': (1.0, 0.6),
     'L1_ffn_beta': (0.0, 0.8),
     'L1_ffn_scale': (0.10000000149011612, 0.6)}
    factors = {'L0_tok_b': 3.639,
     'L0_ffn_Wq': 8.0,
     'L0_ffn_Wk': 8.0,
     'L0_ffn_Wv': 8.0,
     'L0_ffn_Wo': 7.71,
     'L1_attn_W1': 8.0,
     'L1_attn_W2': 8.0,
     'L1_attn_gamma': 8.0,
     'L1_ffn_Wd': 8.0,
     'L1_ffn_spline_bases': 8.0,
     'L1_ffn_spline_slopes': 8.0,
     'L1_ffn_Wu': 8.0}
    for name, (base, spread) in spreads.items():
        noise = np.random.default_rng([zlib.crc32(name.encode()), seed]).standard_normal(out[name].shape)
        drawn = base * np.exp(spread * noise) if base else spread * noise
        out[name] = jnp.asarray(drawn.astype(out[name].dtype))
    for name, factor in factors.items():
        out[name] = (out[name] * factor).astype(out[name].dtype)
    return out
```

```python
from contextlib import ExitStack

import numpy as np

import concourse.bass as bass
from concourse import mybir

F32 = mybir.dt.float32
BF16 = mybir.dt.bfloat16
I32 = mybir.dt.int32
U8 = mybir.dt.uint8
ALU = mybir.AluOpType
ACT = mybir.ActivationFunctionType
AX = mybir.AxisListType

B, T, D = 64, 142, 128
TH = T // 2
N = B * T
NT = N // 128
PATCHES, PATCH, CH = 64, 28, 3
KP = 112
KC = CH * PATCH * PATCH // KP
XG = 8
H, KVH, HD, DR = 8, 2, 64, 32
G = H // KVH
CR = 114
NCH = 5
RW = NCH * CR
E0, FF = 8, 512
T1, DH, GRID, CL = 64, 128, 16, 8
NB0 = NT + E0 - 1
NB1 = NT + T1 - 1
W0C = FF + FF + FF // 128 + D
W1C = 2 * 128 + 2 * GRID + 1
EPS_LN, EPS_RMS = 1e-5, 1e-6
L = 2
NEG = -1e30


L0_CONSTS = ("ident", "wlat", "qln", "kvln", "wkv", "cosk", "sink", "wqa", "wqp", "cosq", "sinq", "qhn", "khn",
             "half_sum", "identb", "maskb", "wvrT", "wo2", "wq", "wk", "wv", "bq", "bk", "bv", "bo", "hmask",
             "wproj", "lng", "lnb")


L1_CONSTS = ("ident", "w1", "b1c", "b1v", "gb", "cosT", "sinT", "w2", "b2", "ns", "gamma", "beta")


class Net:

    def __init__(self, nc, ctx, io):
        self.nc, self.ctx, self.io = nc, ctx, io
        self.sems = {}

    def sb(self, ctx, name, shape, dt=F32):
        return ctx.enter_context(self.nc.sbuf_tensor(name, shape, dt))

    def sem(self, name):
        if name not in self.sems:
            self.sems[name] = self.nc.alloc_semaphore(name=name)
        return self.sems[name]

    def end_phase(self):
        self.nc.all_engine_barrier()
        self.nc.clear_and_free_semaphores(list(self.sems.values()))
        self.nc.all_engine_barrier()
        self.sems = {}


def halves(ap):
    return ap.rearrange("o (u p) d -> p (o u) d", u=2)


def patch_tokens(net):
    nc, io, ps, sem = net.nc, net.io, net.ps, net.sem
    with ExitStack() as ctx:
        wt = net.sb(ctx, "pt_w", [KP, KC, D])
        bcol = net.sb(ctx, "pt_b", [D, 1])
        posT = net.sb(ctx, "pt_posT", [D, PATCHES])
        cls = net.sb(ctx, "pt_cls", [B, 2, D])
        ident = net.sb(ctx, "pt_ident", [128, 128])
        x = net.sb(ctx, "pt_x", [KP, 2, 3, 7, 512])
        tokT = net.sb(ctx, "pt_tokT", [D, 2, 512])
        tok = net.sb(ctx, "pt_tok", [128, 2, 4, D])
        h0 = io["h0"]
        x_loaded = [[sem(f"pt_x_loaded_{g}{s}") for s in range(3)] for g in range(2)]
        consts_loaded, x_used = sem("pt_consts_loaded"), sem("pt_x_used")
        tokT_ready = sem("pt_tokT_ready")
        transposed, tok_ready = sem("pt_transposed"), sem("pt_tok_ready")
        tok_stored = [sem("pt_tok_stored_0"), sem("pt_tok_stored_1")]
        cls_ready, rows_stored = sem("pt_cls_ready"), sem("pt_rows_stored")
        zero_ready = sem("pt_zero_ready")
        zeros = net.sb(ctx, "pt_zeros", [128, 2048])
        block = ctx.enter_context(nc.Block())

        @block.sync
        def _(sp):
            sp.dma_start(wt[:], io["tok_w"]).then_inc(consts_loaded, 16)
            for g in range(2):
                for s in range(3):
                    sp.dma_start(x[:, g, s], io["x"][g, s]).then_inc(x_loaded[g][s], 16)
            with sp.Fori(1, B // XG // 2) as it:
                for g in range(2):
                    for s in range(3):
                        sp.wait_ge(x_used, 6 * it + (3 * g + s + 1 - 6))
                        sp.dma_start(x[:, g, s], io["x"][bass.ds(2 * it + g, 1), s].rearrange(
                            "o p k n -> (o p) k n")).then_inc(x_loaded[g][s], 16)

        @block.gpsimd
        def _(pool):
            nc.gpsimd.memset(zeros[:], 0.0).then_inc(zero_ready, 1)

        @block.scalar
        def _(act):
            for dst, src in ((bcol[:], io["tok_b"]), (posT[:], io["tok_posT"]), (cls[:, 0], io["tok_cls"]),
                             (cls[:, 1], io["tok_pos0"]), (ident[:], io["ident"])):
                act.dma_start(dst, src).then_inc(consts_loaded, 16)
            act.dma_start(h0[:, 1 + PATCHES:, :], io["txt"]).then_inc(rows_stored, 16)
            act.wait_ge(cls_ready, 1)
            act.dma_start(h0[:, 0, :], cls[:, 0]).then_inc(rows_stored, 16)
            act.wait_ge(zero_ready, 1)
            nz = 0
            for name in ("sorted0", "sorted1"):
                flat = io[name].rearrange("(p r) d -> p (r d)", p=128)
                for c in range(0, flat.shape[1], 2048):
                    w = min(2048, flat.shape[1] - c)
                    act.dma_start(flat[:, c:c + w], zeros[:, :w]).then_inc(rows_stored, 16)
                    nz += 1
            act.sem_inc(tok_ready, 2)
            with act.Fori(0, B // XG // 2) as it:
                for g in range(2):
                    act.wait_ge(transposed, 2 * it + g + 1)
                    nc.scalar.activation(tok[:, g], ps[1][:, 2 + g, :].rearrange("p (a d) -> p a d", a=4),
                                         ACT.Copy).then_inc(tok_ready, 1)
                    act.wait_ge(tok_ready, 2 * it + g + 3)
                    for i in range(2):
                        dst = h0[bass.ds(16 * it + 8 * g, 8), 1:1 + PATCHES, :].rearrange(
                            "(a i) p d -> i p a d", i=2)
                        act.dma_start(dst[i], tok[64 * i:64 * i + 64, g]).then_inc(tok_stored[g], 16)
                for g in range(2):
                    act.wait_ge(tok_stored[g], 32 * it + 32)
            act.wait_ge(rows_stored, 16 * (2 + nz))

        @block.vector
        def _(dve):
            dve.wait_ge(consts_loaded, 96)
            nc.vector.tensor_tensor(cls[:, 0], cls[:, 0], cls[:, 1], ALU.mult).then_inc(cls_ready, 1)
            with dve.Fori(0, B // XG // 2) as it:
                for g in range(2):
                    dve.wait_ge(x_used, 6 * it + 3 * g + 3)
                    nc.vector.scalar_tensor_tensor(
                        tokT[:, g].rearrange("p (b n) -> p b n", b=XG), ps[0][:, g, :].rearrange("p (b n) -> p b n", b=XG),
                        bcol[:], posT[:].unsqueeze(1).broadcast_to([D, XG, PATCHES]), ALU.add, ALU.mult).then_inc(tokT_ready, 1)

        @block.tensor
        def _(pe):
            pe.wait_ge(consts_loaded, 96)
            with pe.Fori(0, B // XG // 2) as it:
                for g in range(2):
                    for s in range(3):
                        pe.wait_ge(x_loaded[g][s], 16 * it + 16)
                        for k in range(7):
                            mm = nc.tensor.matmul(ps[0][:, g, :], wt[:, 7 * s + k], x[:, g, s, k],
                                                  start=(s + k == 0), stop=(s == 2 and k == 6))
                        mm.then_inc(x_used, 1)
                    pe.wait_ge(tokT_ready, 2 * it + g + 1)
                    pe.wait_ge(tok_ready, 2 * it + g + 1)
                    for a in range(4):
                        mm = nc.tensor.transpose(ps[1][:, 2 + g, 128 * a:128 * a + 128], tokT[:, g, 128 * a:128 * a + 128], ident[:])
                    mm.then_inc(transposed, 1)



def blocks_of(i):
    return i // 3, (i % 3) * T


def layer0(net):
    nc, io, ps, sem = net.nc, net.io, net.ps, net.sem
    with ExitStack() as ctx:
        def sb(name, shape, dt=F32):
            return net.sb(ctx, "l0_" + name, shape, dt)

        consts = {}
        for name in L0_CONSTS:
            src = io["c0_" + name]
            consts[name] = sb("c_" + name, list(src.shape), src.dtype)
        ident, identb, maskb = consts["ident"], consts["identb"], consts["maskb"]
        wvro = sb("wvro", [D, D])
        wqk = sb("wqk", [D, 1])
        h = sb("h", [TH, L, 2, D])
        stats = sb("stats", [TH, L, 2, 6])
        mv = sb("mv", [TH, L, 2, 2])
        rstd = sb("rstd", [TH, L, 2])
        xn = sb("xn", [TH, L, 2, D])
        xT = sb("xT", [D, L, T])
        junk = sb("junk", [TH, L, 4, D])
        cms = sb("cms", [TH, L, 4])
        crs = sb("crs", [TH, L, 4])
        cn = sb("cn", [TH, L, 2, 192])
        cqT = sb("cqT", [64, L, T])
        ckvT = sb("ckvT", [D, L, T])
        kt = sb("kt", [TH, L, 2, KVH, HD])
        kr2 = sb("kr2", [TH, L, 2, KVH * DR])
        ksq = sb("ksq", [TH, L, 4, HD])
        kss = sb("kss", [TH, L, 4])
        krs = sb("krs", [TH, L, 4])
        kd = sb("kd", [TH, L, 4, 2 * HD])
        kT = sb("kT", [D, L, KVH * T])
        v = sb("v", [TH, L, 2, KVH, HD + 1])
        q = sb("q", [D, L, RW])
        q1 = sb("q1", [D, L, G * T])
        qsq = sb("qsq", [D, L, RW])
        rq = sb("rq", [CR, L, NCH * KVH])
        nb = sb("nb", [CR, L, KVH, NCH])
        P = sb("P", [CR, L, 2 * NCH, T])
        PT = sb("PT", [TH, L, 2, 2 * RW])
        rsum = sb("rsum", [CR, L, NCH, KVH])
        o = sb("o", [CR, L, NCH, KVH, HD])
        oT = sb("oT", [D, L, RW])
        h1 = sb("h1", [TH, L, 2, D])
        xmb = sb("xmb", [TH, L, 2, D])
        qbd = sb("qbd", [D, L, 2 * RW])
        k2T = sb("k2T", [D, L, T])
        v2 = sb("v2", [TH, L, 2, H, 17])
        rsum2 = sb("rsum2", [TH, L, 2, H])
        o2 = sb("o2", [TH, L, 2, D])
        o2T = sb("o2T", [D, L, T])
        z = sb("z", [TH, L, 2, D])
        t = sb("t", [TH, L, 2, D])
        neg_half = sb("neg_half", [CR, 16])

        h_loaded = [sem("l0_h_loaded_0"), sem("l0_h_loaded_1")]
        h1_stored = [sem("l0_h1_stored_0"), sem("l0_h1_stored_1")]
        t_stored = [sem("l0_t_stored_0"), sem("l0_t_stored_1")]
        consts_loaded = sem("l0_consts_loaded")

        def s(name):
            return sem("l0_" + name)

        block = ctx.enter_context(nc.Block())
        STEPS = B // L

        def need(eng, it, l, *names):
            for n in names:
                eng.wait_ge(s(n), L * it + l + 1)

        def settle(eng):
            eng.sem_inc(s("settled"), 1)

        @block.sync
        def _(sp):
            for name in L0_CONSTS:
                sp.dma_start(consts[name][:], io["c0_" + name]).then_inc(consts_loaded, 16)
            for l in range(L):
                sp.sem_inc(h1_stored[l], 16)
                sp.sem_inc(t_stored[l], 16)

            def image(it, l):
                return bass.ds(L * it + l, 1)

            def load(it, l):
                sp.dma_start(h[:, l], halves(io["h0"][image(it, l)])).then_inc(h_loaded[l], 16)

            def store_h1(it, l):
                need(sp, it, l, "h1_ready")
                sp.dma_start(halves(io["h1"][image(it, l)]), h1[:, l]).then_inc(h1_stored[l], 16)

            def store_t(it, l):
                need(sp, it, l, "t_ready")
                sp.dma_start(halves(io["t"][image(it, l)]), t[:, l]).then_inc(t_stored[l], 16)

            for l in range(L):
                load(0, l)
            with sp.Fori(0, STEPS - 1) as it:
                for l in range(L):
                    store_h1(it, l)
                    load(it + 1, l)
                for l in range(L):
                    store_t(it, l)
            for l in range(L):
                store_h1(STEPS - 1, l)
                store_t(STEPS - 1, l)
            for l in range(L):
                sp.wait_ge(h1_stored[l], 16 * STEPS + 16)
                sp.wait_ge(t_stored[l], 16 * STEPS + 16)

        @block.gpsimd
        def _(pool):
            gp = nc.gpsimd
            gp.memset(neg_half[:], -0.5).then_inc(s("neg_half_ready"), 1)
            gp.memset(q[:, :, G * T:], 0.0).then_inc(s("pad_ready"), 1)
            gp.memset(qbd[:, :, H * T:], 0.0).then_inc(s("pad_ready"), 1)
            for l in range(L):
                gp.memset(v[:, l, :, :, HD:], 1.0).then_inc(s("pad_ready"), 1)
                gp.memset(v2[:, l, :, :, 16:], 1.0).then_inc(s("pad_ready"), 1)
            pool.wait_ge(s("neg_half_ready"), 1)

            def power(it, l, src, dst, n, before, after, scale, eps):
                rows = src.shape[0]
                need(pool, it, l, before)
                settle(pool)
                gp.tensor_scalar(dst, src, scale, eps, ALU.mult, ALU.add).then_inc(s(after + "_sum"), 1)
                need(pool, it, l, after + "_sum")
                gp.tensor_tensor(dst, dst, neg_half[:rows, :n], ALU.pow).then_inc(s(after), 1)

            with pool.Fori(0, STEPS) as it:
                for l in range(L):
                    power(it, l, mv[:, l, :, 1], rstd[:, l], 2, "ln_a", "rstd_a", 1.0, EPS_LN)
                for l in range(L):
                    power(it, l, cms[:, l], crs[:, l], 4, "cms", "crs", 1.0, EPS_RMS)
                for l in range(L):
                    power(it, l, kss[:, l], krs[:, l], 4, "kss", "krs", 1.0 / HD, EPS_RMS)
                for l in range(L):
                    power(it, l, rq[:, l], rq[:, l], 10, "qss", "rq", 1.0, HD * EPS_RMS)
                for l in range(L):
                    need(pool, it, l, "max_a")
                    gp.tensor_tensor(nb[:, l], nb[:, l], rq[:, l].rearrange("p (c k) -> p k c", k=KVH),
                                     ALU.mult).then_inc(s("nb_a"), 1)
                for l in range(L):
                    power(it, l, mv[:, l, :, 1], rstd[:, l], 2, "ln_b", "rstd_b", 1.0, EPS_LN)
                for l in range(L):
                    need(pool, it, l, "xn_b")
                    gp.tensor_tensor(xmb[:, l], xn[:, l], consts["bo"][:], ALU.add).then_inc(s("xmb"), 1)
                for l in range(L):
                    power(it, l, mv[:, l, :, 1], rstd[:, l], 2, "ln_c", "rstd_c", 1.0, EPS_LN)
                for l in range(L):
                    need(pool, it, l, "zn")
                    pool.wait_ge(t_stored[l], 16 * it + 16)
                    gp.tensor_tensor(t[:, l], z[:, l], consts["lng"][:], ALU.mult).then_inc(s("t_scaled"), 1)
                for l in range(L):
                    need(pool, it, l, "t_scaled")
                    gp.tensor_tensor(t[:, l], t[:, l], consts["lnb"][:], ALU.add).then_inc(s("t_ready"), 1)

        def layer_norm(dve, it, l, src, dst, tag):
            for u in range(2):
                nc.vector.bn_stats(stats[:, l, u], src[:, l, u]).then_inc(s("bn_" + tag), 1)
            dve.wait_ge(s("bn_" + tag), 2 * L * it + 2 * (l + 1))
            settle(dve)
            for u in range(2):
                ins = nc.vector.bn_aggr(mv[:, l, u], stats[:, l, u])
            ins.then_inc(s("ln_" + tag), 1)

        def normalise(dve, it, l, src, dst, tag, done):
            need(dve, it, l, "ln_" + tag, "rstd_" + tag)
            for u in range(2):
                ins = nc.vector.tensor_scalar(dst[:, l, u], src[:, l, u], mv[:, l, u, 0:1], rstd[:, l, u:u + 1],
                                              ALU.subtract, ALU.mult)
            ins.then_inc(s(done), 1)

        def score_max(it, l, tag):
            for n, b0, c0 in ((3, 0, 0), (2, 1, 3)):
                src = ps[l][:CR].rearrange("p (a b) c -> p a b c", a=2)[:, :, b0, :n * T].rearrange(
                    "p a (i k) -> p a i k", k=T)
                ins = nc.vector.tensor_reduce(nb[:, l, :, c0:c0 + n], src, AX.X, ALU.max, negate=True)
            ins.then_inc(s("max_" + tag), 1)

        def copies(op, l, khalf, act=False):
            for n, b0, c0 in ((3, 0, 0), (2, 1, 3)):
                src = ps[l][:TH].rearrange("p (a b) c -> p a b c", a=2)[:, :, b0, :n * CR]
                dst = PT[:, l, khalf].rearrange("p (a n) -> p a n", a=2)[:, :, c0 * CR:(c0 + n) * CR]
                ins = op(dst, src, ACT.Copy) if act else op(dst, src)
            return ins

        @block.vector
        def _(dve):
            v_ = nc.vector
            dve.wait_ge(consts_loaded, 16 * len(L0_CONSTS))
            dve.wait_ge(s("wvro_done"), 1)
            v_.tensor_copy(wvro[:], ps[0][:, 0, :D]).then_inc(s("wvro_ready"), 1)
            v_.tensor_tensor(wqk[:], consts["qhn"][:], consts["khn"][:], ALU.mult).then_inc(s("wqk_ready"), 1)
            dve.wait_ge(s("wqk_ready"), 1)
            dve.wait_ge(s("pad_ready"), 6)
            with dve.Fori(0, STEPS) as it:
                for l in range(L):
                    dve.wait_ge(h_loaded[l], 16 * it + 16)
                    layer_norm(dve, it, l, h, xn, "a")
                for l in range(L):
                    normalise(dve, it, l, h, xn, "a", "xn_a")
                for l in range(L):
                    need(dve, it, l, "crs", "lat_done")
                    for u in range(2):
                        v_.tensor_scalar(cn[:, l, u, :64], ps[l][:TH, 1 + u, :64], crs[:, l, 2 * u:2 * u + 1], None, ALU.mult)
                        ins = v_.tensor_scalar(cn[:, l, u, 64:], ps[l][:TH, 1 + u, 64:192], crs[:, l, 2 * u + 1:2 * u + 2], None, ALU.mult)
                    ins.then_inc(s("cn"), 1)
                    v_.tensor_tensor(kt[:, l, :, :, DR:], ps[l][:TH, 1:3, 192:256].rearrange("p u (k d) -> p u k d", k=KVH),
                                     consts["cosk"][:].rearrange("p u (k d) -> p u k d", k=KVH), ALU.mult).then_inc(s("kr1"), 1)
                    v_.tensor_tensor(kr2[:, l], ps[l][:TH, 1:3, 256:320], consts["sink"][:], ALU.mult).then_inc(s("kr2"), 1)
                    need(dve, it, l, "kr1", "kr2")
                    v_.tensor_tensor(kt[:, l, :, :, DR:], kt[:, l, :, :, DR:], kr2[:, l].rearrange("p u (k d) -> p u k d", k=KVH),
                                     ALU.add).then_inc(s("kr"), 1)
                for l in range(L):
                    need(dve, it, l, "cT_done")
                    v_.tensor_scalar(cqT[:, l], ps[l][:64, 0, :T], consts["qln"][:], None, ALU.mult)
                    v_.tensor_scalar(ckvT[:, l], ps[l][:, 0, T:2 * T], consts["kvln"][:], None, ALU.mult).then_inc(s("cT"), 1)
                for l in range(L):
                    need(dve, it, l, "kv_done")
                    kv = ps[l][:TH, 3, :384].rearrange("p (u n) -> p u n", u=2)
                    v_.tensor_copy(kt[:, l, :, :, :DR], kv[:, :, :64].rearrange("p u (k d) -> p u k d", k=KVH)).then_inc(s("kt"), 1)
                    v_.tensor_copy(v[:, l, :, :, :HD], kv[:, :, 64:].rearrange("p u (k d) -> p u k d", k=KVH)).then_inc(s("v"), 1)
                    need(dve, it, l, "kt", "kr")
                    k4 = kt[:, l].rearrange("p u k d -> p (u k) d")
                    v_.tensor_tensor(ksq[:, l], k4, k4, ALU.mult).then_inc(s("ksq"), 1)
                    need(dve, it, l, "ksq")
                    v_.tensor_reduce(kss[:, l], ksq[:, l], AX.X, ALU.add).then_inc(s("kss"), 1)
                for l in range(L):
                    need(dve, it, l, "q_done")
                    qa = ps[l][:, 0:2, :2 * T].rearrange("p b (c n) -> p b c n", n=T)
                    qp = ps[l][:, 2:4, :2 * T].rearrange("p b (c n) -> p b c n", n=T)
                    cosq = consts["cosq"][:].unsqueeze(1).unsqueeze(1).broadcast_to([D, 2, 2, T])
                    sinq = consts["sinq"][:].unsqueeze(1).unsqueeze(1).broadcast_to([D, 2, 2, T])
                    q1v = q1[:, l].rearrange("p (b c n) -> p b c n", b=2, n=T)
                    v_.tensor_tensor(q1v, qa, cosq, ALU.mult).then_inc(s("q1"), 1)
                    v_.tensor_tensor(qp, qp, sinq, ALU.mult).then_inc(s("q2"), 1)
                    need(dve, it, l, "q1", "q2")
                    v_.tensor_tensor(q[:, l, :G * T].rearrange("p (b c n) -> p b c n", b=2, n=T), q1v, qp, ALU.add).then_inc(s("q"), 1)
                for l in range(L):
                    need(dve, it, l, "krs")
                    for j in range(4):
                        ins = v_.tensor_scalar(kd[:, l, j].rearrange("p (a d) -> p a d", a=2),
                                               kt[:, l, j // 2, j % 2].unsqueeze(1).broadcast_to([TH, 2, HD]),
                                               krs[:, l, j:j + 1], None, ALU.mult)
                    ins.then_inc(s("kd"), 1)
                for l in range(L):
                    need(dve, it, l, "kT_done")
                    v_.tensor_scalar(kT[:, l], ps[l][:, 1, :2 * T], wqk[:], None, ALU.mult).then_inc(s("kT"), 1)
                    need(dve, it, l, "qss_done")
                    v_.tensor_copy(rq[:, l], ps[l][:CR, 0, :10]).then_inc(s("qss"), 1)
                for l in range(L):
                    need(dve, it, l, "s_done_a", "rq")
                    score_max(it, l, "a")
                for l in range(L):
                    need(dve, it, l, "pt_done_a1")
                    copies(v_.tensor_copy, l, 1).then_inc(s("PT_a1"), 1)
                for l in range(L):
                    need(dve, it, l, "o_done")
                    for n, b, c0 in ((3, 0, 0), (2, 1, 3)):
                        src = ps[l][:CR, b, :n * 130].rearrange("p (c k e) -> p c k e", k=KVH, e=65)
                        ins = v_.reciprocal(rsum[:, l, c0:c0 + n], src[:, :, :, 64])
                    ins.then_inc(s("rsum"), 1)
                    need(dve, it, l, "rsum")
                    for n, b, c0 in ((3, 0, 0), (2, 1, 3)):
                        src = ps[l][:CR, b, :n * 130].rearrange("p (c k e) -> p c k e", k=KVH, e=65)
                        ins = v_.tensor_tensor(o[:, l, c0:c0 + n], src[:, :, :, :64],
                                               rsum[:, l, c0:c0 + n].unsqueeze(3).broadcast_to([CR, n, KVH, HD]), ALU.mult)
                    ins.then_inc(s("o"), 1)
                for l in range(L):
                    need(dve, it, l, "out_done_a")
                    dve.wait_ge(h1_stored[l], 16 * it + 16)
                    v_.tensor_tensor(h1[:, l], ps[l][:TH, 0, :2 * D].rearrange("p (u d) -> p u d", u=2), h[:, l], ALU.add).then_inc(s("h1_ready"), 1)
                    need(dve, it, l, "h1_ready")
                    layer_norm(dve, it, l, h1, xn, "b")
                for l in range(L):
                    normalise(dve, it, l, h1, xn, "b", "xn_b")
                for l in range(L):
                    need(dve, it, l, "qk2_done")
                    v_.scalar_tensor_tensor(qbd[:, l, :H * T].rearrange("p (h n) -> p h n", h=H),
                                            ps[l][:, 1, :T].unsqueeze(1).broadcast_to([D, H, T]), consts["bq"][:],
                                            consts["hmask"][:].unsqueeze(2).broadcast_to([D, H, T]), ALU.add, ALU.mult).then_inc(s("qbd"), 1)
                    v_.tensor_scalar(k2T[:, l], ps[l][:, 1, T:2 * T], consts["bk"][:], None, ALU.add).then_inc(s("k2T"), 1)
                    need(dve, it, l, "v2_done")
                    v_.tensor_tensor(v2[:, l, :, :, :16], ps[l][:TH, 2, :2 * D].rearrange("p (u h e) -> p u h e", u=2, e=16),
                                     consts["bv"][:].rearrange("p u (h e) -> p u h e", e=16), ALU.add).then_inc(s("v2"), 1)
                for l in range(L):
                    need(dve, it, l, "s_done_b")
                    score_max(it, l, "b")
                for l in range(L):
                    need(dve, it, l, "pt_done_b1")
                    copies(v_.tensor_copy, l, 1).then_inc(s("PT_b1"), 1)
                for l in range(L):
                    need(dve, it, l, "o2_done")
                    src = ps[l][:TH, 0, :2 * H * 17].rearrange("p (u h e) -> p u h e", u=2, e=17)
                    v_.reciprocal(rsum2[:, l], src[:, :, :, 16]).then_inc(s("rsum2"), 1)
                    need(dve, it, l, "rsum2")
                    v_.tensor_tensor(o2[:, l].rearrange("p u (h e) -> p u h e", e=16), src[:, :, :, :16],
                                     rsum2[:, l].unsqueeze(3).broadcast_to([TH, 2, H, 16]), ALU.mult).then_inc(s("o2"), 1)
                for l in range(L):
                    need(dve, it, l, "proj_done", "xmb")
                    v_.tensor_tensor(z[:, l], ps[l][:TH, 2, :2 * D].rearrange("p (u d) -> p u d", u=2), xmb[:, l], ALU.add).then_inc(s("z"), 1)
                    need(dve, it, l, "z")
                    layer_norm(dve, it, l, z, z, "c")
                for l in range(L):
                    normalise(dve, it, l, z, z, "c", "zn")

        @block.scalar
        def _(act):
            a_ = nc.scalar.activation
            act.wait_ge(consts_loaded, 16 * len(L0_CONSTS))
            with act.Fori(0, STEPS) as it:
                for l in range(L):
                    need(act, it, l, "xt_done_a")
                    a_(xT[:, l], ps[l][:, 0, :T], ACT.Copy).then_inc(s("xT_a"), 1)
                for l in range(L):
                    need(act, it, l, "lat_done")
                    for u in range(2):
                        a_(junk[:, l, 2 * u, :64], ps[l][:TH, 1 + u, :64], ACT.Square, scale=64 ** -0.5, accum_out=cms[:, l, 2 * u:2 * u + 1])
                        ins = a_(junk[:, l, 2 * u + 1], ps[l][:TH, 1 + u, 64:192], ACT.Square, scale=128 ** -0.5, accum_out=cms[:, l, 2 * u + 1:2 * u + 2])
                    ins.then_inc(s("cms"), 1)
                for l in range(L):
                    need(act, it, l, "q")
                    a_(qsq[:, l], q[:, l], ACT.Square).then_inc(s("qsq"), 1)
                for l in range(L):
                    need(act, it, l, "nb_a")
                    for a in range(2):
                        for i in range(NCH):
                            b, c = blocks_of(i)
                            ins = a_(P[:, l, NCH * a + i], ps[l][:CR, 2 * a + b, c:c + T], ACT.Exp,
                                     bias=nb[:, l, a, i:i + 1], scale=rq[:, l, 2 * i + a:2 * i + a + 1])
                    ins.then_inc(s("P_a"), 1)
                for l in range(L):
                    need(act, it, l, "pt_done_a0")
                    copies(a_, l, 0, True).then_inc(s("PT_a0"), 1)
                for l in range(L):
                    need(act, it, l, "ot_done")
                    a_(oT[:, l, :3 * CR], ps[l][:, 2, :3 * CR], ACT.Copy)
                    a_(oT[:, l, 3 * CR:], ps[l][:, 3, :2 * CR], ACT.Copy).then_inc(s("oT"), 1)
                for l in range(L):
                    need(act, it, l, "xt_done_b")
                    a_(xT[:, l], ps[l][:, 3, :T], ACT.Copy).then_inc(s("xT_b"), 1)
                for l in range(L):
                    need(act, it, l, "max_b")
                    for a in range(2):
                        for i in range(NCH):
                            b, c = blocks_of(i)
                            ins = a_(P[:, l, NCH * a + i], ps[l][:CR, 2 * a + b, c:c + T], ACT.Exp, bias=nb[:, l, a, i:i + 1])
                    ins.then_inc(s("P_b"), 1)
                for l in range(L):
                    need(act, it, l, "pt_done_b0")
                    copies(a_, l, 0, True).then_inc(s("PT_b0"), 1)
                for l in range(L):
                    need(act, it, l, "o2t_done")
                    a_(o2T[:, l], ps[l][:, 1, :T], ACT.Copy).then_inc(s("o2T"), 1)

        @block.tensor
        def _(pe):
            mm, tr = nc.tensor.matmul, nc.tensor.transpose

            def transposes_P(it, l, khalf, tag):
                for a in range(2):
                    for i in range(NCH):
                        b = i // 3
                        ins = tr(ps[l][:TH, 2 * a + b, CR * (i % 3):CR * (i % 3) + CR],
                                 P[:, l, NCH * a + i, TH * khalf:TH * khalf + TH], ident[:CR, :CR])
                ins.then_inc(s(f"pt_done_{tag}{khalf}"), 1)

            pe.wait_ge(consts_loaded, 16 * len(L0_CONSTS))
            for c in range(4):
                ins = mm(ps[0][:, 0, :D], consts["wvrT"][:, c], consts["wo2"][:, c], start=(c == 0), stop=(c == 3))
            ins.then_inc(s("wvro_done"), 1)
            pe.wait_ge(s("wvro_ready"), 1)
            with pe.Fori(0, STEPS) as it:
                for l in range(L):
                    need(pe, it, l, "xn_a")
                    for u in range(2):
                        ins = tr(ps[l][:, 0, TH * u:TH * u + TH], xn[:, l, u], ident[:TH, :TH])
                    ins.then_inc(s("xt_done_a"), 1)
                for l in range(L):
                    need(pe, it, l, "xT_a")
                    for u in range(2):
                        ins = mm(ps[l][:TH, 1 + u, :320], xT[:, l, TH * u:TH * u + TH], consts["wlat"][:], start=True, stop=True)
                    ins.then_inc(s("lat_done"), 1)
                for l in range(L):
                    need(pe, it, l, "cn")
                    settle(pe)
                    for u in range(2):
                        tr(ps[l][:64, 0, TH * u:TH * u + TH], cn[:, l, u, :64], ident[:TH, :TH])
                        ins = tr(ps[l][:, 0, T + TH * u:T + TH * u + TH], cn[:, l, u, 64:], ident[:TH, :TH])
                    ins.then_inc(s("cT_done"), 1)
                for l in range(L):
                    need(pe, it, l, "cT")
                    for u in range(2):
                        ins = mm(ps[l][:TH, 3, 192 * u:192 * u + 192], ckvT[:, l, TH * u:TH * u + TH], consts["wkv"][:], start=True, stop=True)
                    ins.then_inc(s("kv_done"), 1)
                for l in range(L):
                    need(pe, it, l, "kr", "v", "kt")
                    for w, b0 in (("wqa", 0), ("wqp", 2)):
                        for c in range(4):
                            ins = mm(ps[l][:, b0 + c // 2, T * (c % 2):T * (c % 2) + T], consts[w][:, c], cqT[:, l], start=True, stop=True)
                    ins.then_inc(s("q_done"), 1)
                for l in range(L):
                    need(pe, it, l, "q", "kd")
                    for j in range(4):
                        u, k = j // 2, j % 2
                        ins = tr(ps[l][:, 1, T * k + TH * u:T * k + TH * u + TH], kd[:, l, j], ident[:TH, :TH])
                    ins.then_inc(s("kT_done"), 1)
                    need(pe, it, l, "qsq")
                    settle(pe)
                    for i in range(NCH):
                        ins = mm(ps[l][:CR, 0, 2 * i:2 * i + 2], qsq[:, l, CR * i:CR * i + CR], consts["half_sum"][:], start=True, stop=True)
                    ins.then_inc(s("qss_done"), 1)
                for l in range(L):
                    need(pe, it, l, "kT", "qss")
                    settle(pe)
                    for a in range(2):
                        for i in range(NCH):
                            b, c = blocks_of(i)
                            mm(ps[l][:CR, 2 * a + b, c:c + T], q[HD * a:HD * a + HD, l, CR * i:CR * i + CR],
                               kT[HD * a:HD * a + HD, l, T * a:T * a + T], start=(i in (0, 3)), stop=False, skip_group_check=True)
                    for a in range(2):
                        for n, b, c0 in ((3, 0, 0), (2, 1, 3)):
                            ins = mm(ps[l][:CR, 2 * a + b, :n * T], identb[:CR, :CR], maskb[:, c0:c0 + n], start=False, stop=True, skip_group_check=True)
                    ins.then_inc(s("s_done_a"), 1)
                for l in range(L):
                    need(pe, it, l, "P_a")
                    transposes_P(it, l, 0, "a")
                for l in range(L):
                    need(pe, it, l, "PT_a0")
                    transposes_P(it, l, 1, "a")
                for l in range(L):
                    need(pe, it, l, "PT_a1")
                    for i in range(NCH):
                        b = i // 3
                        for k in range(KVH):
                            for u in range(2):
                                c = 130 * (i % 3) + 65 * k
                                ins = mm(ps[l][:CR, b, c:c + 65], PT[:, l, u, RW * k + CR * i:RW * k + CR * i + CR],
                                         v[:, l, u, k], start=(u == 0), stop=(u == 1))
                    ins.then_inc(s("o_done"), 1)
                for l in range(L):
                    need(pe, it, l, "o")
                    for i in range(NCH):
                        ins = tr(ps[l][:, 2 + i // 3, CR * (i % 3):CR * (i % 3) + CR], o[:, l, i].rearrange("p k e -> p (k e)"), ident[:CR, :CR])
                    ins.then_inc(s("ot_done"), 1)
                for l in range(L):
                    need(pe, it, l, "oT")
                    for u in range(2):
                        out = ps[l][:TH, 0, D * u:D * u + D]
                        mm(out, xT[:, l, TH * u:TH * u + TH], wvro[:], start=True, stop=False)
                        for g in range(G):
                            ins = mm(out, oT[:, l, T * g + TH * u:T * g + TH * u + TH], consts["wo2"][:, g], start=False, stop=(g == G - 1))
                    ins.then_inc(s("out_done_a"), 1)
                for l in range(L):
                    need(pe, it, l, "xn_b")
                    for u in range(2):
                        ins = tr(ps[l][:, 3, TH * u:TH * u + TH], xn[:, l, u], ident[:TH, :TH])
                    ins.then_inc(s("xt_done_b"), 1)
                for l in range(L):
                    need(pe, it, l, "xT_b")
                    mm(ps[l][:, 1, :T], consts["wq"][:], xT[:, l], start=True, stop=True)
                    mm(ps[l][:, 1, T:2 * T], consts["wk"][:], xT[:, l], start=True, stop=True).then_inc(s("qk2_done"), 1)
                    for u in range(2):
                        ins = mm(ps[l][:TH, 2, D * u:D * u + D], xT[:, l, TH * u:TH * u + TH], consts["wv"][:], start=True, stop=True)
                    ins.then_inc(s("v2_done"), 1)
                for l in range(L):
                    need(pe, it, l, "qbd", "k2T", "v2")
                    for a in range(2):
                        for i in range(NCH):
                            b, c = blocks_of(i)
                            ins = mm(ps[l][:CR, 2 * a + b, c:c + T], qbd[:, l, RW * a + CR * i:RW * a + CR * i + CR], k2T[:, l], start=True, stop=True)
                    ins.then_inc(s("s_done_b"), 1)
                for l in range(L):
                    need(pe, it, l, "P_b")
                    transposes_P(it, l, 0, "b")
                for l in range(L):
                    need(pe, it, l, "PT_b0")
                    transposes_P(it, l, 1, "b")
                for l in range(L):
                    need(pe, it, l, "PT_b1")
                    settle(pe)
                    for u in range(2):
                        for hh in range(H):
                            c = 136 * u + 17 * hh
                            for k in range(2):
                                ins = mm(ps[l][:TH, 0, c:c + 17], PT[:, l, k, T * hh + TH * u:T * hh + TH * u + TH],
                                         v2[:, l, k, hh], start=(k == 0), stop=(k == 1))
                    ins.then_inc(s("o2_done"), 1)
                for l in range(L):
                    need(pe, it, l, "o2")
                    for u in range(2):
                        ins = tr(ps[l][:, 1, TH * u:TH * u + TH], o2[:, l, u], ident[:TH, :TH])
                    ins.then_inc(s("o2t_done"), 1)
                for l in range(L):
                    need(pe, it, l, "o2T")
                    for u in range(2):
                        ins = mm(ps[l][:TH, 2, D * u:D * u + D], o2T[:, l, TH * u:TH * u + TH], consts["wproj"][:], start=True, stop=True)
                    ins.then_inc(s("proj_done"), 1)



def block_rows(ap, j):
    return ap.rearrange("(j p) d -> j p d", p=128)[bass.ds(j, 1)].rearrange("o p d -> (o p) d")


def route(net, tag, ne, nb, source, score_consts, score_stage, wide_gate):
    nc, io, ps, sem = net.nc, net.io, net.ps, net.sem
    with ExitStack() as ctx:
        def sb(name, shape, dt=F32):
            return net.sb(ctx, f"{tag}_" + name, shape, dt)

        def s(name):
            return sem(f"{tag}_" + name)

        r = {}
        names = score_consts + ("ident", "upper", "onesb", "scan", "jcol")
        consts = {}
        for name in names:
            src = io[f"c{tag}_" + name]
            consts[name] = sb("c_" + name, list(src.shape), src.dtype)
        nconst = 16 * len(names)
        ident = consts["ident"]
        x = sb("x", [128, L, D])
        xT = sb("xT", [D, L, 128], F32 if wide_gate else BF16)
        onehot = sb("onehot", [128, L, ne], BF16)
        onehot_all = sb("onehot_all", [128, NT, ne], BF16)
        acc = sb("acc", [128, L, ne], BF16)
        res = sb("res", [128, L, 2])
        res_all = sb("res_all", [128, NT, 2])
        weighted = sb("weighted", [128, L, ne])
        blocks_f = sb("blocks_f", [ne, 1])
        blocks_i = sb("blocks_i", [ne, 2], I32)
        blocks_b = sb("blocks_b", [ne, 128], BF16)
        ends = sb("ends", [128, 2 * ne])
        eb_f = sb("eb_f", [128, 2])
        eb_i = sb("eb_i", [128, 2], I32)
        eb_junk = sb("eb_junk", [128, 2, ne])
        base_of = sb("base_of", [128, NT, ne])
        slot_f = sb("slot_f", [128, NT])
        gate = sb("gate", [128, NT])
        rows_f = sb("rows_f", [NT, 2, 128])
        slots = net.slots
        slot_col = sb("slot_col", [128, L], I32)
        x_loaded = [s(f"x_loaded_{l}") for l in range(L)]
        x_again = [s(f"x_again_{l}") for l in range(L)]
        scattered = [s(f"scattered_{l}") for l in range(L)]
        env = dict(net=net, sb=sb, s=s, consts=consts, x=x, xT=xT, onehot=onehot, res=res, x_loaded=x_loaded)

        def need(eng, base, l, *which):
            for n in which:
                eng.wait_ge(s(n), base + (l + 1))

        env["need"] = need
        score = score_stage(env)

        def per_block(eng, body):
            with eng.Fori(0, NT // L) as it:
                body(L * it, range(L))
            body(NT - NT % L, range(NT % L))

        block = ctx.enter_context(nc.Block())

        @block.sync
        def _(sp):
            for name in names:
                sp.dma_start(consts[name][:], io[f"c{tag}_" + name]).then_inc(s("consts_loaded"), 16)
            score.get("sync", lambda e: None)(sp)

            def load(base, lanes):
                for l in lanes:
                    sp.wait_ge(s("x_free"), base + (l + 1))
                    sp.dma_start(x[:, l], block_rows(source, base + l)).then_inc(x_loaded[l], 16)

            per_block(sp, load)
            sp.wait_ge(s("eb_ready"), 1)
            sp.dma_start(io["eb"], eb_i[:]).then_inc(s("tables_stored"), 16)
            sp.wait_ge(s("rows_ready"), 1)
            sp.dma_start(io["slot_gate"].rearrange("g (j p) -> j g p", p=128), rows_f[:]).then_inc(s("tables_stored"), 16)

            def load_again(base, lanes):
                for l in lanes:
                    sp.wait_ge(s("x_scattered"), base + (l + 1))
                    sp.dma_start(x[:, l], block_rows(source, base + l)).then_inc(x_again[l], 16)

            per_block(sp, load_again)
            sp.wait_ge(s("tables_stored"), 32)

        @block.tensor
        def _(pe):
            mm, tr = nc.tensor.matmul, nc.tensor.transpose
            pe.wait_ge(s("consts_loaded"), nconst)
            score.get("pe_setup", lambda e: None)(pe)
            pe.sem_inc(s("x_free"), L)

            def body(base, lanes):
                for l in lanes:
                    pe.wait_ge(x_loaded[l], 8 * base + 16)
                    tr(ps[l][:, 0, :128], x[:, l], ident[:]).then_inc(s("x_free"), 1)
                score["pe"](pe, base, lanes)
                for l in lanes:
                    need(pe, base, l, "onehot", "acc")
                    mm(ps[l][:, 2, :ne], consts["upper"][:], onehot[:, l], start=True, stop=False)
                    mm(ps[l][:, 2, :ne], consts["onesb"][:], acc[:, l], start=False, stop=True).then_inc(s("rank_done"), 1)

            per_block(pe, body)
            pe.wait_ge(s("acc"), NT + 1)
            mm(ps[0][:ne, 0, :1], acc[:, NT % L], consts["onesb"][:, :1], start=True, stop=True).then_inc(s("count_done"), 1)
            pe.wait_ge(s("blocks_b"), 1)
            mm(ps[0][:, 1, :2 * ne], blocks_b[:], consts["scan"][:], start=True, stop=True).then_inc(s("ends_done"), 1)
            pe.wait_ge(s("slot_f"), 1)
            tr(ps[0][:NT, 2, :128], slot_f[:], ident[:])
            tr(ps[0][:NT, 2, 128:256], gate[:], ident[:]).then_inc(s("rows_done"), 1)

        @block.vector
        def _(dve):
            v_ = nc.vector
            dve.wait_ge(s("consts_loaded"), nconst)
            v_.memset(acc[:], 0.0).then_inc(s("acc"), 1)
            if not wide_gate:
                v_.memset(res[:], 1.0).then_inc(s("res_set"), 1)
                dve.wait_ge(s("res_set"), 1)
            score.get("dve_setup", lambda e: None)(dve)

            def body(base, lanes):
                score["dve"](dve, base, lanes)
                for l in lanes:
                    need(dve, base, l, "onehot", "acc", "rank_done")
                    v_.tensor_tensor(acc[:, (l + 1) % L], acc[:, l], onehot[:, l], ALU.add).then_inc(s("acc"), 1)
                    v_.tensor_copy(onehot_all[:, bass.ds(base + l, 1)].rearrange("p o e -> p (o e)"), onehot[:, l])
                    v_.scalar_tensor_tensor(weighted[:, l], ps[l][:, 2, :ne], 1.0, onehot[:, l], ALU.mult, ALU.mult,
                                            accum_out=res[:, l, 0:1]).then_inc(s("rank"), 1)
                    need(dve, base, l, "rank")
                    v_.tensor_copy(res_all[:, bass.ds(base + l, 1)].rearrange("p o e -> p (o e)"), res[:, l]).then_inc(s("res_kept"), 1)

            per_block(dve, body)
            dve.wait_ge(s("count_done"), 1)
            v_.tensor_scalar(blocks_i[:, 0:1], ps[0][:ne, 0, :1], 127.0, None, ALU.add).then_inc(s("b1"), 1)
            dve.wait_ge(s("b1"), 1)
            v_.tensor_scalar(blocks_i[:, 1:2], blocks_i[:, 0:1], 7, None, ALU.arith_shift_right).then_inc(s("b2"), 1)
            dve.wait_ge(s("b2"), 1)
            v_.tensor_copy(blocks_f[:], blocks_i[:, 1:2]).then_inc(s("b3"), 1)
            dve.wait_ge(s("b3"), 1)
            v_.tensor_scalar(blocks_b[:], consts["onesb"][:ne], blocks_f[:], None, ALU.mult).then_inc(s("blocks_b"), 1)
            dve.wait_ge(s("ends_done"), 1)
            v_.tensor_copy(ends[:], ps[0][:, 1, :2 * ne]).then_inc(s("ends"), 1)
            dve.wait_ge(s("ends"), 1)
            for i in range(2):
                ins = v_.tensor_scalar(eb_junk[:, i], ends[:, :ne], consts["jcol"][:, i:i + 1], None, ALU.is_le, ALU.add,
                                       accum_out=eb_f[:, i:i + 1])
            ins.then_inc(s("eb_f"), 1)
            dve.wait_ge(s("eb_f"), 1)
            v_.tensor_scalar(eb_i[:], eb_f[:], float(ne - 1), None, ALU.min).then_inc(s("eb_ready"), 1)
            dve.wait_ge(s("res_kept"), NT)
            v_.tensor_tensor(base_of[:], onehot_all[:], ends[:, ne:].unsqueeze(1).broadcast_to([128, NT, ne]), ALU.mult).then_inc(s("base_of"), 1)
            dve.wait_ge(s("base_of"), 1)
            v_.tensor_reduce(slot_f[:], base_of[:], AX.X, ALU.add).then_inc(s("base_sum"), 1)
            v_.reciprocal(gate[:], res_all[:, :, 1])
            dve.wait_ge(s("base_sum"), 1)
            v_.tensor_tensor(slot_f[:], slot_f[:], res_all[:, :, 0], ALU.add).then_inc(s("slot_f"), 1)
            dve.wait_ge(s("slot_f"), 1)
            v_.tensor_copy(slots[:], slot_f[:]).then_inc(s("slots"), 1)
            dve.wait_ge(s("rows_done"), 1)
            v_.tensor_copy(rows_f[:], ps[0][:NT, 2, :256].rearrange("p (g n) -> p g n", g=2)).then_inc(s("rows_ready"), 1)

        @block.scalar
        def _(act):
            act.wait_ge(s("consts_loaded"), nconst)
            if "act" in score:
                per_block(act, lambda base, lanes: score["act"](act, base, lanes))

        @block.gpsimd
        def _(pool):
            pool.sem_inc(s("x_scattered"), L)
            pool.wait_ge(s("slots"), 1)

            def scatter(base, lanes):
                for l in lanes:
                    nc.gpsimd.tensor_copy(slot_col[:, l:l + 1], slots[:, bass.ds(base + l, 1)]).then_inc(s("slot_col"), 1)
                for l in lanes:
                    need(pool, base, l, "slot_col")
                    pool.wait_ge(x_again[l], 8 * base + 16)
                    pool.sem_inc(s("settled"), 1)
                    nc.gpsimd.indirect_dma_start(io[f"sorted{tag[-1]}"], bass.IndirectOffsetOnAxis(slot_col[:, l:l + 1], 0),
                                                 x[:, l], None).then_inc(scattered[l], 16)
                for l in lanes:
                    pool.wait_ge(scattered[l], 8 * base + 16)
                    pool.sem_inc(s("x_scattered"), 1)

            per_block(pool, scatter)


def gate_scores(env):
    net, sb, s, need = env["net"], env["sb"], env["s"], env["need"]
    nc, ps, consts = net.nc, net.ps, env["consts"]
    xT, onehot, res = env["xT"], env["onehot"], env["res"]
    lg, nmx, ex, first, mx2 = sb("lg", [128, L, E0]), sb("nmx", [128, L]), sb("ex", [128, L, E0]), sb("first", [128, L, E0]), sb("mx2", [128, L])

    def pe(eng, base, lanes):
        for l in lanes:
            need(eng, base, l, "xT")
            eng.sem_inc(s("settled"), 1)
            nc.tensor.matmul(ps[l][:, 1, :E0], xT[:, l], consts["gw"][:], start=True, stop=True).then_inc(s("scores_done"), 1)

    def act(eng, base, lanes):
        for l in lanes:
            eng.wait_ge(s("x_free"), base + (l + 1 + L))
            nc.scalar.activation(xT[:, l], ps[l][:, 0, :128], ACT.Copy).then_inc(s("xT"), 1)
        for l in lanes:
            need(eng, base, l, "lg0")
            nc.scalar.activation(ex[:, l], lg[:, l], ACT.Exp, accum_out=res[:, l, 1:2]).then_inc(s("gate_sum"), 1)

    def dve(eng, base, lanes):
        v_ = nc.vector
        for l in lanes:
            need(eng, base, l, "scores_done")
            v_.tensor_tensor(lg[:, l], ps[l][:, 1, :E0], consts["gb"][:], ALU.add).then_inc(s("lg"), 1)
            need(eng, base, l, "lg")
            v_.tensor_reduce(nmx[:, l:l + 1], lg[:, l], AX.X, ALU.max, negate=True).then_inc(s("nmx"), 1)
            need(eng, base, l, "nmx")
            v_.tensor_scalar(lg[:, l], lg[:, l], nmx[:, l:l + 1], None, ALU.add).then_inc(s("lg0"), 1)
            need(eng, base, l, "lg0")
            v_.scalar_tensor_tensor(first[:, l], lg[:, l], 0.0, consts["order"][:], ALU.is_equal, ALU.mult).then_inc(s("first"), 1)
            need(eng, base, l, "first")
            v_.tensor_reduce(mx2[:, l:l + 1], first[:, l], AX.X, ALU.max).then_inc(s("mx2"), 1)
            need(eng, base, l, "mx2", "gate_sum")
            v_.tensor_scalar(onehot[:, l], first[:, l], mx2[:, l:l + 1], None, ALU.is_equal).then_inc(s("onehot"), 1)

    return {"pe": pe, "act": act, "dve": dve}


def route_experts(net):
    route(net, "r0", E0, NB0, net.io["t"].rearrange("b t d -> (b t) d"), ("gw", "gb", "order"), gate_scores, True)


def sign_scores(env):
    net, sb, s, need = env["net"], env["sb"], env["s"], env["need"]
    nc, ps, consts = net.nc, net.ps, env["consts"]
    xT, onehot = env["xT"], env["onehot"]
    wd = sb("wd", [D, T1, DH])
    sums, pos = sb("sums", [D, T1]), sb("pos", [D, T1])
    nsig = sb("nsig", [D, T1])
    csum, cpos, csig = sb("csum", [D, CL]), sb("cpos", [D, CL]), sb("csig", [D, CL])
    sig = sb("sig", [D, CL + T1], BF16)
    xpos = sb("xpos", [D, L, 128])
    key, mx = sb("key", [128, L, CL + T1]), sb("mx", [128, L, 2])
    big = sb("big", [128, L, CL])

    def sync(eng):
        eng.dma_start(wd[:], net.io["wdT"]).then_inc(s("wd_loaded"), 16)

    def dve_setup(eng):
        v_ = nc.vector
        eng.wait_ge(s("wd_loaded"), 16)
        v_.tensor_reduce(sums[:], wd[:], AX.X, ALU.add).then_inc(s("sums"), 1)
        eng.wait_ge(s("sums"), 1)
        v_.tensor_scalar(pos[:], sums[:], 0.0, None, ALU.is_gt).then_inc(s("pos"), 1)
        eng.wait_ge(s("pos"), 1)
        v_.scalar_tensor_tensor(nsig[:], sums[:], 0.0, pos[:], ALU.is_lt, ALU.subtract).then_inc(s("nsig"), 1)
        eng.wait_ge(s("nsig"), 1)
        v_.tensor_scalar(sig[:, CL:], nsig[:], float(T1), None, ALU.mult)
        v_.tensor_reduce(csum[:], nsig[:].rearrange("p (c t) -> p c t", c=CL), AX.X, ALU.add).then_inc(s("csum"), 1)
        eng.wait_ge(s("csum"), 1)
        v_.tensor_scalar(cpos[:], csum[:], 0.0, None, ALU.is_lt).then_inc(s("cpos"), 1)
        eng.wait_ge(s("cpos"), 1)
        v_.scalar_tensor_tensor(csig[:], csum[:], 0.0, cpos[:], ALU.is_gt, ALU.subtract).then_inc(s("csig"), 1)
        eng.wait_ge(s("csig"), 1)
        v_.tensor_scalar(sig[:, :CL], csig[:], float(CL), None, ALU.mult).then_inc(s("sig"), 1)

    def pe_setup(eng):
        eng.wait_ge(s("sig"), 1)

    def pe(eng, base, lanes):
        for l in lanes:
            need(eng, base, l, "xT")
            nc.tensor.matmul(ps[l][:, 1, :CL + T1], xT[:, l], sig[:], start=True, stop=True).then_inc(s("scores_done"), 1)

    def dve(eng, base, lanes):
        v_ = nc.vector
        for l in lanes:
            eng.wait_ge(s("x_free"), base + (l + 1 + L))
            v_.tensor_scalar(xpos[:, l], ps[l][:, 0, :128], 0.0, None, ALU.is_gt).then_inc(s("xpos"), 1)
            need(eng, base, l, "xpos")
            v_.scalar_tensor_tensor(xT[:, l], ps[l][:, 0, :128], 0.0, xpos[:, l], ALU.is_lt, ALU.subtract).then_inc(s("xT"), 1)
        for l in lanes:
            need(eng, base, l, "scores_done")
            v_.tensor_tensor(key[:, l], ps[l][:, 1, :CL + T1], consts["order"][:], ALU.add).then_inc(s("key"), 1)
            need(eng, base, l, "key")
            v_.tensor_reduce(mx[:, l, 0:1], key[:, l, :CL], AX.X, ALU.max).then_inc(s("mx_c"), 1)
            need(eng, base, l, "mx_c")
            v_.tensor_scalar(big[:, l], key[:, l, :CL], mx[:, l, 0:1], float(1 << 15), ALU.is_equal, ALU.mult).then_inc(s("big"), 1)
            need(eng, base, l, "big")
            kt = key[:, l, CL:].rearrange("p (c t) -> p c t", c=CL)
            v_.tensor_tensor(kt, kt, big[:, l].unsqueeze(2).broadcast_to([128, CL, T1 // CL]), ALU.add).then_inc(s("key_t"), 1)
            need(eng, base, l, "key_t")
            v_.tensor_reduce(mx[:, l, 1:2], key[:, l, CL:], AX.X, ALU.max).then_inc(s("mx_t"), 1)
            need(eng, base, l, "mx_t")
            v_.tensor_scalar(onehot[:, l], key[:, l, CL:], mx[:, l, 1:2], None, ALU.is_equal).then_inc(s("onehot"), 1)

    return {"sync": sync, "dve_setup": dve_setup, "pe_setup": pe_setup, "pe": pe, "dve": dve}


def route_tiles(net):
    route(net, "r1", T1, NB1, net.io["xf"].rearrange("b t d -> (b t) d"), ("order",), sign_scores, False)


def sorted_blocks(net, tag, nb, width, emit):
    nc, io, ps, sem = net.nc, net.io, net.ps, net.sem
    S = 2 * L
    with ExitStack() as ctx:
        def sb(name, shape, dt=F32):
            return net.sb(ctx, f"{tag}_" + name, shape, dt)

        def s(name):
            return sem(f"{tag}_" + name)

        eb = sb("eb", [1, 256], I32)
        ident = sb("ident", [128, 128])
        x = sb("x", [128, S, D])
        w = sb("w", [128, S, width])
        xT = sb("xT", [D, L, 128])
        y = sb("y", [128, S, D])
        loaded = [s(f"loaded_{i}") for i in range(S)]
        y_stored = [s(f"y_stored_{i}") for i in range(S)]

        def need(eng, base, l, *which):
            for n in which:
                eng.wait_ge(s(n), base + (l + 1))

        def per_block(eng, body):
            with eng.Fori(0, nb // S) as it:
                for a in range(2):
                    body(S * it + L * a, L * a, it)
            if nb % S:
                body(nb - nb % S, 0, nb // S)

        env = dict(net=net, sb=sb, s=s, need=need, x=x, w=w, xT=xT, y=y, y_stored=y_stored)
        parts = emit(env)
        block = ctx.enter_context(nc.Block())

        @block.sync
        def _(sp):
            sp.dma_start(ident[:], io["ident"]).then_inc(s("ident_loaded"), 16)
            sp.dma_start(eb[:], io["eb"].rearrange("p g -> (p g)").unsqueeze(0)).then_inc(s("eb_loaded"), 16)
            parts.get("sync", lambda e: None)(sp)
            sp.wait_ge(s("eb_loaded"), 16)
            for i in range(S):
                sp.sem_inc(y_stored[i], 16)

            def load(base, slot0):
                for l in range(L):
                    e = sp.value_load(eb[0:1, bass.ds(base + l, 1)], min_val=0, max_val=io[f"{tag}_w"].shape[0] - 1)
                    sp.dma_start(w[:, slot0 + l], io[f"{tag}_w"][bass.ds(e, 1)].rearrange("o p n -> (o p) n")).then_inc(loaded[slot0 + l], 16)
                    sp.dma_start(x[:, slot0 + l], block_rows(io[f"sorted{tag[-1]}"], base + l)).then_inc(loaded[slot0 + l], 16)

            def store(base, slot0):
                for l in range(L):
                    need(sp, base, l, "y_ready")
                    sp.dma_start(block_rows(io[f"y{tag[-1]}"], base + l), y[:, slot0 + l]).then_inc(y_stored[slot0 + l], 16)

            load(0, 0)
            load(L, L)
            last = nb - 3 * L
            with sp.Fori(0, last // S) as it:
                for a in range(2):
                    store(S * it + L * a, L * a)
                    load(S * it + L * a + S, L * a)
            store(last, 0)
            load(last + S, 0)
            store(last + L, L)
            store(last + S, 0)
            for i in range(S):
                sp.wait_ge(y_stored[i], 16 * (nb // S + (i < nb % S)) + 16)

        @block.gpsimd
        def _(pool):
            parts.get("pool_setup", lambda e: None)(pool)

            def body(base, slot0, it):
                for l in range(L):
                    pool.wait_ge(loaded[slot0 + l], 32 * it + 32)
                parts["pool"](pool, base, slot0)

            if "pool" in parts:
                per_block(pool, body)

        @block.tensor
        def _(pe):
            pe.wait_ge(s("ident_loaded"), 16)

            def body(base, slot0, it):
                for l in range(L):
                    pe.wait_ge(loaded[slot0 + l], 32 * it + 32)
                    nc.tensor.transpose(ps[l][:, 0, :128], x[:, slot0 + l], ident[:]).then_inc(s("x_transposed"), 1)
                parts["pe"](pe, base, slot0)

            per_block(pe, body)

        @block.vector
        def _(dve):
            parts.get("dve_setup", lambda e: None)(dve)

            def body(base, slot0, it):
                for l in range(L):
                    need(dve, base, l, "x_transposed")
                    nc.vector.tensor_copy(xT[:, l], ps[l][:, 0, :128]).then_inc(s("xT"), 1)
                parts["dve"](dve, base, slot0, it)

            per_block(dve, body)

        @block.scalar
        def _(act):
            per_block(act, lambda base, slot0, it: parts["act"](act, base, slot0, it))


def expert_parts(env):
    net, sb, s, need = env["net"], env["sb"], env["s"], env["need"]
    nc, ps, w, xT, y, y_stored = net.nc, net.ps, env["w"], env["xT"], env["y"], env["y_stored"]
    C = FF // 128
    hid = sb("hid", [128, L, C, 128])

    def pe(eng, base, slot0):
        mm = nc.tensor.matmul
        for l in range(L):
            need(eng, base, l, "xT")
            for c in range(C):
                ins = mm(ps[l][:, 1, 128 * c:128 * c + 128], w[:, slot0 + l, 128 * c:128 * c + 128], xT[:, l], start=True, stop=True)
            ins.then_inc(s("up_done"), 1)
        for l in range(L):
            need(eng, base, l, "hid")
            for c in range(C):
                ins = mm(ps[l][:, 2, :D], hid[:, l, c], w[:, slot0 + l, FF + 128 * c:FF + 128 * c + 128], start=(c == 0), stop=(c == C - 1))
            ins.then_inc(s("down_done"), 1)

    def act(eng, base, slot0, it):
        for l in range(L):
            need(eng, base, l, "up_done")
            for c in range(C):
                ins = nc.scalar.activation(hid[:, l, c], ps[l][:, 1, 128 * c:128 * c + 128], ACT.Gelu_apprx_tanh,
                                           bias=w[:, slot0 + l, 2 * FF + c:2 * FF + c + 1])
            ins.then_inc(s("hid"), 1)

    def dve(eng, base, slot0, it):
        for l in range(L):
            eng.wait_ge(y_stored[slot0 + l], 16 * it + 16)
            need(eng, base, l, "down_done")
            nc.vector.tensor_tensor(y[:, slot0 + l], ps[l][:, 2, :D], w[:, slot0 + l, 2 * FF + C:], ALU.add).then_inc(s("y_ready"), 1)

    return {"pe": pe, "act": act, "dve": dve}


def experts(net):
    sorted_blocks(net, "f0", NB0, W0C, expert_parts)


def spline_parts(env):
    net, sb, s, need = env["net"], env["sb"], env["s"], env["need"]
    nc, ps, w, xT, y, y_stored = net.nc, net.ps, env["w"], env["xT"], env["y"], env["y_stored"]
    hn = sb("hn", [DH, L, 128])
    hs = sb("hs", [DH, L, 128])
    mask = sb("mask", [DH, L, GRID - 1, 128], U8)
    late = sb("late", [DH, L, 3, 128])
    slope = sb("slope", [DH, L, GRID])
    shift = sb("shift", [DH, L, GRID])
    gidx = sb("gidx", [DH, GRID])
    BASE, SLOPE = 2 * 128, 2 * 128 + GRID

    def sync(eng):
        eng.dma_start(gidx[:], net.io["gidx"]).then_inc(s("gidx_loaded"), 16)

    def pool_setup(eng):
        eng.wait_ge(s("gidx_loaded"), 16)
        eng.sem_inc(s("tables_used"), L)

    def pool(eng, base, slot0):
        gp = nc.gpsimd
        for l in range(L):
            need(eng, base, l, "tables_used")
            gp.tensor_tensor(shift[:, l], w[:, slot0 + l, SLOPE:SLOPE + GRID], gidx[:], ALU.mult).then_inc(s("gslope"), 1)
            eng.sem_inc(s("settled"), 1)
            gp.tensor_scalar(slope[:, l], w[:, slot0 + l, SLOPE:SLOPE + GRID], float(GRID), 0.0, ALU.mult, ALU.add)
            need(eng, base, l, "gslope")
            gp.tensor_tensor(shift[:, l], w[:, slot0 + l, BASE:BASE + GRID], shift[:, l], ALU.subtract).then_inc(s("tables"), 1)

    def piece(l, g):
        return ps[l][:, 1 + (g - 1) // 4, 128 * ((g - 1) % 4):128 * ((g - 1) % 4) + 128] if g <= 12 else late[:, l, g - 13]

    def act(eng, base, slot0, it):
        a_ = nc.scalar.activation
        for l in range(L):
            need(eng, base, l, "h_done")
            a_(hn[:, l], ps[l][:, 0, 128:256], ACT.Sigmoid).then_inc(s("hn"), 1)
        for l in range(L):
            need(eng, base, l, "hn", "tables")
            for g in range(GRID):
                dst = hs[:, l] if g == 0 else piece(l, g)
                ins = a_(dst, hn[:, l], ACT.Identity, scale=slope[:, l, g:g + 1], bias=shift[:, l, g:g + 1])
                if g in (4, 8, 12):
                    ins.then_inc(s("pieces"), 1)
            ins.then_inc(s("tables_used"), 1)
            eng.sem_inc(s("settled"), 1)

    def dve(eng, base, slot0, it):
        v_ = nc.vector
        for l in range(L):
            need(eng, base, l, "hn")
            for g in range(1, GRID):
                ins = v_.tensor_scalar(mask[:, l, g - 1], hn[:, l], g / GRID, None, ALU.is_ge)
            ins.then_inc(s("masks"), 1)
        for l in range(L):
            need(eng, base, l, "masks")
        for g in range(1, GRID):
            if g > 1:
                eng.wait_ge(s("copied"), (GRID - 1) * base + L * (g - 1))
            if g in (1, 5, 9):
                eng.wait_ge(s("pieces"), 3 * base + (3 * (L - 1) + 1 + g // 4))
            if g == 13:
                eng.wait_ge(s("tables_used"), base + 2 * L)
            eng.sem_inc(s("settled"), 1)
            for l in range(L):
                ins = v_.copy_predicated(hs[:, l], mask[:, l, g - 1], piece(l, g))
                ins.then_inc(s("copied"), 1)
        for l in range(L):
            eng.wait_ge(y_stored[slot0 + l], 16 * it + 16)
            need(eng, base, l, "y_done")
            v_.tensor_scalar(y[:, slot0 + l], ps[l][:, 1, :D], w[:, slot0 + l, W1C - 1:W1C], None, ALU.mult).then_inc(s("y_ready"), 1)

    def pe(eng, base, slot0):
        mm = nc.tensor.matmul
        for l in range(L):
            need(eng, base, l, "xT")
            mm(ps[l][:, 0, 128:256], w[:, slot0 + l, :128], xT[:, l], start=True, stop=True).then_inc(s("h_done"), 1)
        for l in range(L):
            eng.wait_ge(s("copied"), (GRID - 1) * base + (L * (GRID - 2) + l + 1))
            mm(ps[l][:, 1, :D], hs[:, l], w[:, slot0 + l, 128:256], start=True, stop=True).then_inc(s("y_done"), 1)

    return {"sync": sync, "pool_setup": pool_setup, "pool": pool, "act": act, "dve": dve, "pe": pe}


def spline_tiles(net):
    sorted_blocks(net, "f1", NB1, W1C, spline_parts)



def layer1(net):
    nc, io, ps, sem = net.nc, net.io, net.ps, net.sem
    EX = 2 * D
    with ExitStack() as ctx:
        def sb(name, shape, dt=F32):
            return net.sb(ctx, "l1_" + name, shape, dt)

        def s(name):
            return sem("l1_" + name)

        consts = {}
        for name in L1_CONSTS:
            src = io["c2_" + name]
            consts[name] = sb("c_" + name, list(src.shape), src.dtype)
        ident = consts["ident"]
        rows = sb("rows", [128, 2, TH])
        slot_i = sb("slot_i", [TH, 128], I32)
        gate = sb("gate", [TH, 128])
        cols = sb("cols", [TH, L, 2], I32)
        gcols = sb("gcols", [TH, L, 2])
        neg_half = sb("neg_half", [TH, 2])
        h1 = sb("h1", [TH, L, 2, D])
        y = sb("y", [TH, L, 2, D])
        h2 = sb("h2", [TH, L, 2, D])
        stats = sb("stats", [TH, L, 2, 6])
        mv = sb("mv", [TH, L, 2, 2])
        rstd = sb("rstd", [TH, L, 2])
        x = sb("x", [TH, L, 2, D])
        junk = sb("junk", [TH, L, 2, D])
        ms = sb("ms", [TH, L, 2])
        rms = sb("rms", [TH, L, 2])
        hb = sb("hb", [TH, L, 2, D])
        xr = sb("xr", [TH, L, 2, D])
        xrT = sb("xrT", [D, L, T])
        uT = sb("uT", [D, L, 2, T])
        bT = sb("bT", [D, L, T])
        qT, kT = sb("qT", [D, L, T]), sb("kT", [D, L, T])
        vb = sb("vb", [TH, L, 2, EX])
        v = sb("v", [TH, L, 2, EX])
        r1, r2 = sb("r1", [TH, L, 2, T]), sb("r2", [TH, L, 2, T])
        rot = sb("rot", [TH, L, 2, T])
        kern = sb("kern", [TH, L, 2, T])
        uo = sb("uo", [D, L, 2, T])
        h3 = sb("h3", [TH, L, 2, D])
        x2 = sb("x2", [TH, L, 2, D])
        r3 = sb("r3", [TH, L, 2, D])
        xf = sb("xf", [TH, L, 2, D])
        loaded = [s(f"h1_loaded_{l}") for l in range(L)]
        gathered = [s(f"gathered_{l}") for l in range(L)]
        r3_stored = [s(f"r3_stored_{l}") for l in range(L)]
        xf_stored = [s(f"xf_stored_{l}") for l in range(L)]
        STEPS = B // L
        nconst = 16 * len(L1_CONSTS)

        def need(eng, it, l, *names):
            for n in names:
                eng.wait_ge(s(n), L * it + l + 1)

        def settle(eng):
            eng.sem_inc(s("settled"), 1)

        block = ctx.enter_context(nc.Block())

        @block.sync
        def _(sp):
            for name in L1_CONSTS:
                sp.dma_start(consts[name][:], io["c2_" + name]).then_inc(s("consts_loaded"), 16)
            sp.dma_start(rows[:], io["slot_gate"].rearrange("g (r p) -> r g p", p=TH)).then_inc(s("rows_loaded"), 16)
            for l in range(L):
                sp.sem_inc(r3_stored[l], 16)
                sp.sem_inc(xf_stored[l], 16)

            def image(it, l):
                return bass.ds(L * it + l, 1)

            def load(it, l):
                sp.dma_start(h1[:, l], halves(io["h1"][image(it, l)])).then_inc(loaded[l], 16)

            def store(it, l, name, ready, tile, stored):
                need(sp, it, l, ready)
                sp.dma_start(halves(io[name][image(it, l)]), tile[:, l]).then_inc(stored[l], 16)

            for l in range(L):
                load(0, l)
            with sp.Fori(0, STEPS - 1) as it:
                for l in range(L):
                    need(sp, it, l, "h2")
                    load(it + 1, l)
                for l in range(L):
                    store(it, l, "r3", "r3", r3, r3_stored)
                for l in range(L):
                    store(it, l, "xf", "xf", xf, xf_stored)
            for l in range(L):
                store(STEPS - 1, l, "r3", "r3", r3, r3_stored)
                store(STEPS - 1, l, "xf", "xf", xf, xf_stored)
            for l in range(L):
                sp.wait_ge(r3_stored[l], 16 * STEPS + 16)
                sp.wait_ge(xf_stored[l], 16 * STEPS + 16)

        @block.gpsimd
        def _(pool):
            gp = nc.gpsimd
            gp.memset(neg_half[:], -0.5).then_inc(s("neg_half_ready"), 1)
            pool.wait_ge(s("neg_half_ready"), 1)
            pool.wait_ge(s("slot_i"), 1)
            pool.wait_ge(s("gate"), 1)

            def gather(it, l):
                pair = bass.ds(2 * (L * it + l), 2)
                gp.tensor_copy(cols[:, l], slot_i[:, pair]).then_inc(s("cols"), 1)
                gp.tensor_copy(gcols[:, l], gate[:, pair]).then_inc(s("gcols"), 1)
                need(pool, it, l, "cols")
                settle(pool)
                for u in range(2):
                    gp.indirect_dma_start(y[:, l, u], None, io["y0"], bass.IndirectOffsetOnAxis(cols[:, l, u:u + 1], 0)).then_inc(gathered[l], 16)

            def power(it, l, src, dst, before, after, eps):
                need(pool, it, l, before)
                settle(pool)
                gp.tensor_scalar(dst, src, 1.0, eps, ALU.mult, ALU.add).then_inc(s(after + "_sum"), 1)
                need(pool, it, l, after + "_sum")
                gp.tensor_tensor(dst, dst, neg_half[:], ALU.pow).then_inc(s(after), 1)

            def steps(it, last):
                for l in range(L):
                    power(it, l, mv[:, l, :, 1], rstd[:, l], "ln_a", "rstd_a", EPS_LN)
                for l in range(L):
                    power(it, l, ms[:, l], rms[:, l], "ms", "rms", EPS_RMS)
                if not last:
                    for l in range(L):
                        gather(it + 1, l)
                for l in range(L):
                    need(pool, it, l, "x")
                    gp.tensor_tensor(hb[:, l], h2[:, l], x[:, l], ALU.add).then_inc(s("hx"), 1)
                for l in range(L):
                    need(pool, it, l, "hx")
                    gp.tensor_tensor(hb[:, l], hb[:, l], consts["b2"][:], ALU.add).then_inc(s("hb"), 1)
                for l in range(L):
                    power(it, l, mv[:, l, :, 1], rstd[:, l], "ln_b", "rstd_b", EPS_LN)
                for l in range(L):
                    need(pool, it, l, "x2")
                    pool.wait_ge(r3_stored[l], 16 * it + 16)
                    gp.tensor_tensor(r3[:, l], h3[:, l], x2[:, l], ALU.add).then_inc(s("r3"), 1)
                for l in range(L):
                    power(it, l, mv[:, l, :, 1], rstd[:, l], "ln_c", "rstd_c", EPS_LN)
                for l in range(L):
                    need(pool, it, l, "x3")
                    pool.wait_ge(xf_stored[l], 16 * it + 16)
                    gp.tensor_tensor(xf[:, l], x2[:, l], consts["gamma"][:], ALU.mult).then_inc(s("xg"), 1)
                for l in range(L):
                    need(pool, it, l, "xg")
                    gp.tensor_tensor(xf[:, l], xf[:, l], consts["beta"][:], ALU.add).then_inc(s("xf"), 1)

            for l in range(L):
                gather(0, l)
            with pool.Fori(0, STEPS - 1) as it:
                steps(it, False)
            steps(STEPS - 1, True)

        def layer_norm(dve, it, l, src, tag):
            for u in range(2):
                nc.vector.bn_stats(stats[:, l, u], src[:, l, u]).then_inc(s("bn_" + tag), 1)
            dve.wait_ge(s("bn_" + tag), 2 * L * it + 2 * (l + 1))
            settle(dve)
            for u in range(2):
                ins = nc.vector.bn_aggr(mv[:, l, u], stats[:, l, u])
            ins.then_inc(s("ln_" + tag), 1)

        def normalise(dve, it, l, src, dst, tag, done):
            need(dve, it, l, "ln_" + tag, "rstd_" + tag)
            for u in range(2):
                ins = nc.vector.tensor_scalar(dst[:, l, u], src[:, l, u], mv[:, l, u, 0:1], rstd[:, l, u:u + 1],
                                              ALU.subtract, ALU.mult)
            ins.then_inc(s(done), 1)

        @block.vector
        def _(dve):
            v_ = nc.vector
            dve.wait_ge(s("consts_loaded"), nconst)
            dve.wait_ge(s("rows_transposed"), 1)
            v_.tensor_copy(slot_i[:], ps[0][:TH, 0, :128]).then_inc(s("slot_i"), 1)
            v_.tensor_copy(gate[:], ps[0][:TH, 0, 128:256]).then_inc(s("gate"), 1)
            with dve.Fori(0, STEPS) as it:
                for l in range(L):
                    dve.wait_ge(loaded[l], 16 * it + 16)
                    dve.wait_ge(gathered[l], 32 * it + 32)
                    need(dve, it, l, "gcols")
                    for u in range(2):
                        ins = v_.scalar_tensor_tensor(h2[:, l, u], y[:, l, u], gcols[:, l, u:u + 1], h1[:, l, u], ALU.mult, ALU.add)
                    ins.then_inc(s("h2"), 1)
                    need(dve, it, l, "h2")
                    layer_norm(dve, it, l, h2, "a")
                for l in range(L):
                    normalise(dve, it, l, h2, x, "a", "x")
                for l in range(L):
                    need(dve, it, l, "rms", "x")
                    for u in range(2):
                        ins = v_.tensor_scalar(xr[:, l, u], x[:, l, u], rms[:, l, u:u + 1], consts["ns"][:], ALU.mult, ALU.mult)
                    ins.then_inc(s("xr"), 1)
                for l in range(L):
                    need(dve, it, l, "v_done")
                    v_.tensor_tensor(vb[:, l], ps[l][:TH, 1, :].rearrange("p (u e) -> p u e", u=2), consts["b1v"][:], ALU.add).then_inc(s("vb"), 1)
                for l in range(L):
                    need(dve, it, l, "bT")
                    for j, dst in ((0, qT), (1, kT)):
                        ins = v_.tensor_scalar(dst[:, l], bT[:, l], consts["gb"][:, 2 * j:2 * j + 1], consts["gb"][:, 2 * j + 1:2 * j + 2], ALU.mult, ALU.add)
                    ins.then_inc(s("qk"), 1)
                for l in range(L):
                    need(dve, it, l, "s_done")
                    src = ps[l][:TH, 2, :2 * T].rearrange("p (u n) -> p u n", u=2)
                    v_.tensor_tensor(r1[:, l], src, consts["cosT"][:].unsqueeze(1).broadcast_to([TH, 2, T]), ALU.mult)
                    v_.tensor_tensor(r2[:, l], src, consts["sinT"][:].unsqueeze(1).broadcast_to([TH, 2, T]), ALU.mult).then_inc(s("r12"), 1)
                    need(dve, it, l, "r12")
                    v_.tensor_tensor(rot[:, l, 0], r1[:, l, 0], r2[:, l, 1], ALU.subtract)
                    v_.tensor_tensor(rot[:, l, 1], r1[:, l, 1], r2[:, l, 0], ALU.add).then_inc(s("rot"), 1)
                    need(dve, it, l, "rot")
                    v_.scalar_tensor_tensor(kern[:, l], rot[:, l], 0.0, rot[:, l], ALU.max, ALU.mult).then_inc(s("kern"), 1)
                for l in range(L):
                    need(dve, it, l, "o_done", "uT")
                    v_.tensor_tensor(uo[:, l], ps[l][:, 3, :2 * T].rearrange("p (c n) -> p c n", c=2), uT[:, l], ALU.mult).then_inc(s("uo"), 1)
                for l in range(L):
                    need(dve, it, l, "out_done", "hb")
                    v_.tensor_tensor(h3[:, l], ps[l][:TH, 0, :2 * D].rearrange("p (u d) -> p u d", u=2), hb[:, l], ALU.add).then_inc(s("h3"), 1)
                    need(dve, it, l, "h3")
                    layer_norm(dve, it, l, h3, "b")
                for l in range(L):
                    normalise(dve, it, l, h3, x2, "b", "x2")
                    need(dve, it, l, "x2")
                    layer_norm(dve, it, l, x2, "c")
                for l in range(L):
                    need(dve, it, l, "r3")
                    normalise(dve, it, l, x2, x2, "c", "x3")

        @block.scalar
        def _(act):
            a_ = nc.scalar.activation
            act.wait_ge(s("consts_loaded"), nconst)
            with act.Fori(0, STEPS) as it:
                for l in range(L):
                    need(act, it, l, "x")
                    for u in range(2):
                        ins = a_(junk[:, l, u], x[:, l, u], ACT.Square, scale=D ** -0.5, accum_out=ms[:, l, u:u + 1])
                    ins.then_inc(s("ms"), 1)
                for l in range(L):
                    need(act, it, l, "xr_transposed")
                    a_(xrT[:, l], ps[l][:, 0, :T], ACT.Copy).then_inc(s("xrT"), 1)
                for l in range(L):
                    need(act, it, l, "ub_done")
                    a_(bT[:, l], ps[l][:, 3, 2 * T:3 * T], ACT.Silu, bias=consts["b1c"][:, 2:3]).then_inc(s("bT"), 1)
                    for c in range(2):
                        ins = a_(uT[:, l, c], ps[l][:, 3, T * c:T * c + T], ACT.Silu, bias=consts["b1c"][:, c:c + 1])
                    ins.then_inc(s("uT"), 1)
                for l in range(L):
                    need(act, it, l, "vb")
                    a_(v[:, l], vb[:, l], ACT.Silu).then_inc(s("v"), 1)

        @block.tensor
        def _(pe):
            mm, tr = nc.tensor.matmul, nc.tensor.transpose
            pe.wait_ge(s("consts_loaded"), nconst)
            pe.wait_ge(s("rows_loaded"), 16)
            for g in range(2):
                ins = tr(ps[0][:TH, 0, 128 * g:128 * g + 128], rows[:, g], ident[:])
            ins.then_inc(s("rows_transposed"), 1)
            pe.wait_ge(s("gate"), 1)
            with pe.Fori(0, STEPS) as it:
                for l in range(L):
                    need(pe, it, l, "xr")
                    for u in range(2):
                        ins = tr(ps[l][:, 0, TH * u:TH * u + TH], xr[:, l, u], ident[:TH, :TH])
                    ins.then_inc(s("xr_transposed"), 1)
                for l in range(L):
                    need(pe, it, l, "xrT")
                    for c in (2, 0, 1):
                        ins = mm(ps[l][:, 3, T * c:T * c + T], consts["w1"][:, (2 * EX if c == 2 else D * c):(2 * EX if c == 2 else D * c) + D], xrT[:, l], start=True, stop=True)
                    ins.then_inc(s("ub_done"), 1)
                    for u in range(2):
                        ins = mm(ps[l][:TH, 1, EX * u:EX * u + EX], xrT[:, l, TH * u:TH * u + TH], consts["w1"][:, EX:2 * EX], start=True, stop=True)
                    ins.then_inc(s("v_done"), 1)
                for l in range(L):
                    need(pe, it, l, "qk")
                    for u in range(2):
                        ins = mm(ps[l][:TH, 2, T * u:T * u + T], kT[:, l, TH * u:TH * u + TH], qT[:, l], start=True, stop=True)
                    ins.then_inc(s("s_done"), 1)
                for l in range(L):
                    need(pe, it, l, "kern", "v", "uT")
                    for c in range(2):
                        for u in range(2):
                            ins = mm(ps[l][:, 3, T * c:T * c + T], v[:, l, u, D * c:D * c + D], kern[:, l, u], start=(u == 0), stop=(u == 1))
                    ins.then_inc(s("o_done"), 1)
                for l in range(L):
                    need(pe, it, l, "uo")
                    for u in range(2):
                        for c in range(2):
                            ins = mm(ps[l][:TH, 0, D * u:D * u + D], uo[:, l, c, TH * u:TH * u + TH], consts["w2"][:, c], start=(c == 0), stop=(c == 1))
                    ins.then_inc(s("out_done"), 1)


def gather_out(net):
    nc, io, sem, slots = net.nc, net.io, net.sem, net.slots
    with ExitStack() as ctx:
        def s(name):
            return sem("g_" + name)

        cols = net.sb(ctx, "g_cols", [128, L], I32)
        y = net.sb(ctx, "g_y", [128, L, D])
        r3 = net.sb(ctx, "g_r3", [128, L, D])
        out = net.sb(ctx, "g_out", [128, L, D])
        gathered = [s(f"gathered_{l}") for l in range(L)]
        r3_loaded = [s(f"r3_loaded_{l}") for l in range(L)]
        stored = [s(f"out_stored_{l}") for l in range(L)]
        r3_rows = io["r3"].rearrange("b t d -> (b t) d")
        out_rows = io["out"].rearrange("b t d -> (b t) d")
        block = ctx.enter_context(nc.Block())

        def per_block(eng, body):
            with eng.Fori(0, NT // L) as it:
                body(L * it, range(L))
            body(NT - NT % L, range(NT % L))

        @block.sync
        def _(sp):
            def body(base, lanes):
                for l in lanes:
                    sp.wait_ge(s("sum"), base + (l + 1))
                    sp.dma_start(r3[:, l], block_rows(r3_rows, base + l)).then_inc(r3_loaded[l], 16)

            per_block(sp, body)

        @block.gpsimd
        def _(pool):
            def body(base, lanes):
                for l in lanes:
                    pool.wait_ge(s("sum"), base + (l + 1))
                    pool.sem_inc(s("settled"), 1)
                    nc.gpsimd.tensor_copy(cols[:, l:l + 1], slots[:, bass.ds(base + l, 1)]).then_inc(s("cols"), 1)
                for l in lanes:
                    pool.wait_ge(s("cols"), base + (l + 1))
                    pool.sem_inc(s("settled"), 1)
                    nc.gpsimd.indirect_dma_start(y[:, l], None, io["y1"], bass.IndirectOffsetOnAxis(cols[:, l:l + 1], 0)).then_inc(gathered[l], 16)

            per_block(pool, body)

        @block.vector
        def _(dve):
            dve.sem_inc(s("sum"), L)

            def body(base, lanes):
                for l in lanes:
                    dve.wait_ge(gathered[l], 8 * base + 16)
                    dve.wait_ge(r3_loaded[l], 8 * base + 16)
                    dve.wait_ge(stored[l], 8 * base + 16)
                    nc.vector.tensor_tensor(out[:, l], y[:, l], r3[:, l], ALU.add).then_inc(s("sum"), 1)

            per_block(dve, body)

        @block.scalar
        def _(act):
            for l in range(L):
                act.sem_inc(stored[l], 16)

            def body(base, lanes):
                for l in lanes:
                    act.wait_ge(s("sum"), base + (l + 1 + L))
                    act.dma_start(block_rows(out_rows, base + l), out[:, l]).then_inc(stored[l], 16)

            per_block(act, body)
            for l in range(L):
                act.wait_ge(stored[l], 16 * ((NT - l + L - 1) // L) + 16)


def host_arrays(inp):
    f = np.float32
    c = np.ascontiguousarray
    a = {}
    x = inp["x"].reshape(B // XG // 2, 2, XG, CH, 8, PATCH, 8, PATCH)
    x = x.transpose(0, 1, 3, 5, 7, 2, 4, 6).reshape(B // XG, 3, 7, KP, XG * PATCHES)
    a["x"] = c(x.transpose(0, 1, 3, 2, 4))
    a["tok_w"] = c(inp["L0_tok_W"].T.reshape(KC, KP, D).transpose(1, 0, 2))
    a["tok_b"] = c(inp["L0_tok_b"].reshape(D, 1))
    pos = inp["L0_tok_pos_embed"]
    a["tok_posT"] = c(pos[1:].T)
    a["tok_cls"] = c(np.broadcast_to(inp["L0_tok_class_token"], (B, D)))
    a["tok_pos0"] = c(np.broadcast_to(pos[:1], (B, D)))
    a["txt"] = c(inp["txt"])
    a["ident"] = np.eye(128, dtype=f)

    ang = np.outer(np.arange(T, dtype=f), 1.0 / 500000.0 ** (np.arange(0, DR, 2, dtype=f) / DR))
    emb = np.concatenate([ang, ang], -1).astype(f)
    cos, sin = np.cos(emb).astype(f), np.sin(emb).astype(f)
    sin = sin * np.where(np.arange(DR) < DR // 2, -1, 1).astype(f)
    rot = np.r_[DR // 2:DR, 0:DR // 2]
    one_head = lambda r, n: np.concatenate([n, r], 1).T
    p = {}
    p["ident"] = np.eye(128, dtype=f)
    p["identb"] = np.eye(128, dtype=f).astype(np.dtype("bfloat16"))
    row = np.arange(RW).reshape(NCH, CR).T[:, :, None]
    key = np.arange(T)[None, None]
    hidden = (key > row % T) & (row < G * T)
    p["maskb"] = np.where(hidden, NEG, 0.0).astype(f).astype(np.dtype("bfloat16"))
    p["cosq"] = np.tile(one_head(cos, np.ones((T, HD - DR), f)), (2, 1))
    p["sinq"] = np.tile(one_head(sin, np.zeros((T, HD - DR), f)), (2, 1))
    p["cosk"] = np.tile(cos.reshape(2, TH, DR).transpose(1, 0, 2), (1, 1, KVH))
    p["sink"] = np.tile(sin.reshape(2, TH, DR).transpose(1, 0, 2), (1, 1, KVH))
    g = lambda n: inp["L0_attn_" + n]
    kr = g("W_KR").reshape(D, KVH, DR)
    p["wlat"] = np.concatenate([g("W_DQ"), g("W_DKV"), kr.reshape(D, -1), kr[:, :, rot].reshape(D, -1)], 1)
    p["wkv"] = np.concatenate([g("W_UK"), g("W_UV")], 1)
    uq, qr = g("W_UQ").reshape(64, H, HD - DR), g("W_QR").reshape(64, H, DR)
    pack = lambda n, r: np.concatenate([n, r], 2).reshape(64, KVH, G, HD).transpose(0, 2, 1, 3).reshape(64, G, 128)
    p["wqa"] = pack(uq, qr)
    p["wqp"] = pack(uq, qr[:, :, rot])
    p["qln"] = g("q_ln_w").reshape(64, 1)
    p["kvln"] = g("kv_ln_w").reshape(D, 1)
    p["qhn"] = np.tile(g("q_head_norm_w"), 2).reshape(D, 1)
    p["khn"] = np.tile(g("k_head_norm_w"), 2).reshape(D, 1)
    p["half_sum"] = np.kron(np.eye(2, dtype=f), np.ones((64, 1), f))
    p["wo2"] = g("W_O").reshape(KVH, G, HD, D).transpose(0, 2, 1, 3).reshape(D, G, D)
    p["wvrT"] = g("W_VR").T.reshape(KVH, G, HD, D).transpose(0, 2, 1, 3).reshape(D, G, D)
    g = lambda n: inp["L0_ffn_" + n]
    rows = lambda w: np.broadcast_to(w, (TH, 2, D))
    p["wq"], p["wk"], p["wv"], p["wproj"] = g("Wq"), g("Wk"), g("Wv"), g("Wo")
    p["bq"], p["bk"] = g("bq").reshape(D, 1), g("bk").reshape(D, 1)
    p["bv"], p["bo"], p["lng"], p["lnb"] = rows(g("bv")), rows(g("bo")), rows(g("ln1_g")), rows(g("ln1_b"))
    p["hmask"] = np.kron(np.eye(H, dtype=f), np.ones((16, 1), f)) * f(0.25)
    a.update({"c0_" + k: c(p[k]) for k in L0_CONSTS})

    bf = np.dtype("bfloat16")
    for tag, ne in (("cr0_", E0), ("cr1_", T1)):
        a[tag + "ident"] = np.eye(128, dtype=f)
        a[tag + "upper"] = np.triu(np.ones((128, 128), f), 1).astype(bf)
        a[tag + "onesb"] = np.ones((128, 128), bf)
        k, e = np.arange(ne)[:, None], np.arange(ne)[None]
        a[tag + "scan"] = np.concatenate([(k <= e) * 1.0, (k < e) * 128.0], 1).astype(bf)
        a[tag + "jcol"] = (2 * np.arange(128)[:, None] + np.arange(2)[None]).astype(f)
    a["cr0_gw"] = c(g("gate_W"))
    a["cr0_gb"] = c(np.broadcast_to(g("gate_b"), (128, E0)))
    a["cr0_order"] = c(np.broadcast_to(np.arange(E0, 0, -1, dtype=f), (128, E0)))
    a["cr1_order"] = c(np.broadcast_to(np.concatenate([np.arange(CL - 1, -1, -1), np.arange(T1 - 1, -1, -1)]).astype(f), (128, CL + T1)))

    a["f0_w"] = np.concatenate([
        g("W1"), g("W2").reshape(E0, FF // 128, 128, D).transpose(0, 2, 1, 3).reshape(E0, 128, FF),
        g("b1").reshape(E0, FF // 128, 128).transpose(0, 2, 1), np.broadcast_to(g("b2")[:, None], (E0, 128, D))], 2)

    g = lambda n: inp["L1_attn_" + n]
    p = {"ident": np.eye(128, dtype=f)}
    half = T // 2
    inv = (f(10000.0) ** (-np.arange(half, dtype=f) / f(half))).astype(f)
    ang = np.arange(T, dtype=f)[None] * inv[:, None]
    p["cosT"], p["sinT"] = np.cos(ang).astype(f) / 128, np.sin(ang).astype(f) / 128
    p["w1"] = g("W1")
    b1 = g("b1")
    p["b1c"] = np.stack([b1[:D], b1[D:2 * D], b1[4 * D:]], 1)
    p["b1v"] = np.broadcast_to(b1[2 * D:4 * D], (TH, 2, 2 * D))
    p["gb"] = np.stack([g("gamma")[0], g("beta")[0], g("gamma")[1], g("beta")[1]], 1)
    p["w2"] = g("W2").reshape(2, D, D).transpose(1, 0, 2)
    p["b2"] = rows(g("b2"))
    p["ns"] = np.broadcast_to(g("norm_scale"), (TH, 1))
    g = lambda n: inp["L1_ffn_" + n]
    p["gamma"], p["beta"] = rows(g("gamma")), rows(g("beta"))
    a.update({"c2_" + k: c(p[k]) for k in L1_CONSTS})
    a["wdT"] = c(g("Wd").transpose(2, 0, 1))
    a["f1_w"] = np.concatenate([g("Wd").transpose(0, 2, 1), g("Wu").transpose(0, 2, 1), g("spline_bases"), g("spline_slopes"),
                                np.broadcast_to(g("scale")[:, None, None], (T1, 128, 1))], 2)
    a["gidx"] = c(np.broadcast_to(np.arange(GRID, dtype=f), (DH, GRID)))
    return a


SCRATCH = {"r3": (B, T, D), "xf": (B, T, D), "y0": (NB0 * 128, D), "y1": (NB1 * 128, D), "slot_gate": (2, N), "h1": (B, T, D), "t": (B, T, D), "h0": (B, T, D), "sorted0": (NB0 * 128, D), "sorted1": (NB1 * 128, D)}


def build(nc, arrays, phases, debug=False, given=()):
    io = {}
    for k, v in arrays.items():
        io[k] = nc.dram_tensor(f"in_{k}", v.shape, mybir.dt.from_np(v.dtype), kind="ExternalInput").ap()
    for k, shape in SCRATCH.items():
        io[k] = nc.dram_tensor(k, shape, F32, **({"kind": "ExternalInput" if k in given else "ExternalOutput"} if debug else {})).ap()
    io["eb"] = nc.dram_tensor("eb", (128, 2), I32, **({"kind": "ExternalOutput"} if debug else {})).ap()
    io["out"] = nc.dram_tensor("out_0", (B, T, D), F32, kind="ExternalOutput").ap()
    with ExitStack() as ctx:
        net = Net(nc, ctx, io)
        net.ps = [ctx.enter_context(nc.psum_tensor(f"ps{l}", [128, 4, 512], F32)) for l in range(L)]
        net.slots = net.sb(ctx, "slots", [128, NT], I32)
        for phase in phases:
            phase(net)
            net.end_phase()


PHASES = (patch_tokens, layer0, route_experts, experts, layer1, route_tiles, spline_tiles, gather_out)


def kernel(**inputs):
    from concourse import bacc
    from concourse.bass_utils import run_bass_kernel_spmd

    arrays = host_arrays({k: np.asarray(v) for k, v in inputs.items()})
    nc = bacc.Bacc("TRN2", target_bir_lowering=False, num_devices=1)
    build(nc, arrays, PHASES)
    r = run_bass_kernel_spmd(nc, [{f"in_{k}": v for k, v in arrays.items()}], core_ids=[0])
    return r.results[0]["out_0"]
```

```python
from contextlib import ExitStack

import numpy as np

import concourse.bass as bass
from concourse import mybir

F32 = mybir.dt.float32
BF16 = mybir.dt.bfloat16
I32 = mybir.dt.int32
U8 = mybir.dt.uint8
ALU = mybir.AluOpType
ACT = mybir.ActivationFunctionType
AX = mybir.AxisListType

B, T, D = 64, 142, 128
TH = T // 2
N = B * T
NT = N // 128
PATCHES, PATCH, CH = 64, 28, 3
KP = 112
KC = CH * PATCH * PATCH // KP
XG = 8
H, KVH, HD, DR = 8, 2, 64, 32
G = H // KVH
CR = 114
NCH = 5
RW = NCH * CR
E0, FF = 8, 512
T1, DH, GRID, CL = 64, 128, 16, 8
NB0 = NT + E0 - 1
NB1 = -(-(NT + T1 - 1) // 4) * 4
W0C = FF + FF + FF // 128 + D
W1C = 2 * 128 + 2 * GRID + 1
EPS_LN, EPS_RMS = 1e-5, 1e-6
L = 2
LA = 4
NEG = -1e30


L0_CONSTS = ("ident", "wlat", "qln", "kvln", "wkv", "cosk", "sink", "wqa", "wqp", "cosq", "sinq", "qhn", "khn",
             "half_sum", "identb", "maskb", "wvrT", "wo2", "wq", "wk", "wv", "bq", "bk", "bv", "bo", "hmask",
             "wproj", "lng", "lnb")


L1_CONSTS = ("ident", "w1", "b1c", "b1v", "gb", "cosT", "sinT", "w2", "b2", "ns", "gamma", "beta")


class Net:

    def __init__(self, nc, ctx, io):
        self.nc, self.ctx, self.io = nc, ctx, io
        self.sems = {}

    def sb(self, ctx, name, shape, dt=F32):
        return ctx.enter_context(self.nc.sbuf_tensor(name, shape, dt))

    def psum(self, ctx, tag):
        return [ctx.enter_context(self.nc.psum_tensor(f"{tag}_ps{l}", [128, 4, 512], F32)) for l in range(L)]

    def sem(self, name):
        if name not in self.sems:
            self.sems[name] = self.nc.alloc_semaphore(name=name)
        return self.sems[name]

    def end_phase(self):
        self.nc.all_engine_barrier()
        self.nc.clear_and_free_semaphores(list(self.sems.values()))
        self.nc.all_engine_barrier()
        self.sems = {}


def halves(ap):
    return ap.rearrange("o (u p) d -> p (o u) d", u=2)


def patch_tokens(net):
    nc, io, sem = net.nc, net.io, net.sem
    with ExitStack() as ctx:
        ps = net.psum(ctx, "pt")
        wt = net.sb(ctx, "pt_w", [KP, KC, D])
        bcol = net.sb(ctx, "pt_b", [D, 1])
        posT = net.sb(ctx, "pt_posT", [D, PATCHES])
        cls = net.sb(ctx, "pt_cls", [B, 2, D])
        ident = net.sb(ctx, "pt_ident", [128, 128])
        x = net.sb(ctx, "pt_x", [KP, 2, 3, 7, 512])
        tokT = net.sb(ctx, "pt_tokT", [D, 2, 512])
        tok = net.sb(ctx, "pt_tok", [128, 2, 4, D])
        h0 = io["h0"]
        x_loaded = [[sem(f"pt_x_loaded_{g}{s}") for s in range(3)] for g in range(2)]
        consts_loaded, x_used = sem("pt_consts_loaded"), sem("pt_x_used")
        tokT_ready = sem("pt_tokT_ready")
        transposed, tok_ready = sem("pt_transposed"), sem("pt_tok_ready")
        tok_stored = [sem("pt_tok_stored_0"), sem("pt_tok_stored_1")]
        cls_ready, rows_stored = sem("pt_cls_ready"), sem("pt_rows_stored")
        zero_ready = sem("pt_zero_ready")
        zeros = net.sb(ctx, "pt_zeros", [128, 2048])
        block = ctx.enter_context(nc.Block())

        @block.sync
        def _(sp):
            sp.dma_start(wt[:], io["tok_w"]).then_inc(consts_loaded, 16)
            for g in range(2):
                for s in range(3):
                    sp.dma_start(x[:, g, s], io["x"][g, s]).then_inc(x_loaded[g][s], 16)
            with sp.Fori(1, B // XG // 2) as it:
                for g in range(2):
                    for s in range(3):
                        sp.wait_ge(x_used, 6 * it + (3 * g + s + 1 - 6))
                        sp.dma_start(x[:, g, s], io["x"][bass.ds(2 * it + g, 1), s].rearrange(
                            "o p k n -> (o p) k n")).then_inc(x_loaded[g][s], 16)

        @block.gpsimd
        def _(pool):
            nc.gpsimd.memset(zeros[:], 0.0).then_inc(zero_ready, 1)

        @block.scalar
        def _(act):
            for dst, src in ((bcol[:], io["tok_b"]), (posT[:], io["tok_posT"]), (cls[:, 0], io["tok_cls"]),
                             (cls[:, 1], io["tok_pos0"]), (ident[:], io["ident"])):
                act.dma_start(dst, src).then_inc(consts_loaded, 16)
            act.dma_start(h0[:, 1 + PATCHES:, :], io["txt"]).then_inc(rows_stored, 16)
            act.wait_ge(cls_ready, 1)
            act.dma_start(h0[:, 0, :], cls[:, 0]).then_inc(rows_stored, 16)
            act.wait_ge(zero_ready, 1)
            nz = 0
            for name in ("sorted0", "sorted1"):
                flat = io[name].rearrange("(p r) d -> p (r d)", p=128)
                for c in range(0, flat.shape[1], 2048):
                    w = min(2048, flat.shape[1] - c)
                    act.dma_start(flat[:, c:c + w], zeros[:, :w]).then_inc(rows_stored, 16)
                    nz += 1
            act.sem_inc(tok_ready, 2)
            with act.Fori(0, B // XG // 2) as it:
                for g in range(2):
                    act.wait_ge(transposed, 2 * it + g + 1)
                    nc.scalar.activation(tok[:, g], ps[1][:, 2 + g, :].rearrange("p (a d) -> p a d", a=4),
                                         ACT.Copy).then_inc(tok_ready, 1)
                    act.wait_ge(tok_ready, 2 * it + g + 3)
                    for i in range(2):
                        dst = h0[bass.ds(16 * it + 8 * g, 8), 1:1 + PATCHES, :].rearrange(
                            "(a i) p d -> i p a d", i=2)
                        act.dma_start(dst[i], tok[64 * i:64 * i + 64, g]).then_inc(tok_stored[g], 16)
                for g in range(2):
                    act.wait_ge(tok_stored[g], 32 * it + 32)
            act.wait_ge(rows_stored, 16 * (2 + nz))

        @block.vector
        def _(dve):
            dve.wait_ge(consts_loaded, 96)
            nc.vector.tensor_tensor(cls[:, 0], cls[:, 0], cls[:, 1], ALU.mult).then_inc(cls_ready, 1)
            with dve.Fori(0, B // XG // 2) as it:
                for g in range(2):
                    dve.wait_ge(x_used, 6 * it + 3 * g + 3)
                    nc.vector.scalar_tensor_tensor(
                        tokT[:, g].rearrange("p (b n) -> p b n", b=XG), ps[0][:, g, :].rearrange("p (b n) -> p b n", b=XG),
                        bcol[:], posT[:].unsqueeze(1).broadcast_to([D, XG, PATCHES]), ALU.add, ALU.mult).then_inc(tokT_ready, 1)

        @block.tensor
        def _(pe):
            pe.wait_ge(consts_loaded, 96)
            with pe.Fori(0, B // XG // 2) as it:
                for g in range(2):
                    for s in range(3):
                        pe.wait_ge(x_loaded[g][s], 16 * it + 16)
                        for k in range(7):
                            mm = nc.tensor.matmul(ps[0][:, g, :], wt[:, 7 * s + k], x[:, g, s, k],
                                                  start=(s + k == 0), stop=(s == 2 and k == 6))
                        mm.then_inc(x_used, 1)
                    pe.wait_ge(tokT_ready, 2 * it + g + 1)
                    pe.wait_ge(tok_ready, 2 * it + g + 1)
                    for a in range(4):
                        mm = nc.tensor.transpose(ps[1][:, 2 + g, 128 * a:128 * a + 128], tokT[:, g, 128 * a:128 * a + 128], ident[:])
                    mm.then_inc(transposed, 1)



def layer0(net):
    nc, io, sem = net.nc, net.io, net.sem
    LL = LA
    with ExitStack() as ctx:
        def sb(name, shape, dt=F32):
            return net.sb(ctx, "l0_" + name, shape, dt)

        ps = [ctx.enter_context(nc.psum_tensor(f"l0_ps{l}", [128, 2, 512], F32)) for l in range(LL)]
        X, Y = 0, 1
        consts = {}
        for name in L0_CONSTS:
            src = io["c0_" + name]
            consts[name] = sb("c_" + name, list(src.shape), src.dtype)
        ident, identb, maskb = consts["ident"], consts["identb"], consts["maskb"]
        wvro = sb("wvro", [D, D])
        wqk = sb("wqk", [D, 1])
        bo2 = sb("bo2", [TH, D])
        h = sb("h", [TH, LL, 2, D])
        stats = sb("stats", [TH, LL, 2, 6])
        mv = sb("mv", [TH, LL, 2, 2])
        rstd = sb("rstd", [TH, LL, 2])
        xn = sb("xn", [TH, LL, 2, D])
        xT = sb("xT", [D, LL, T])
        cms = sb("cms", [TH, LL, 2, 2])
        crs = sb("crs", [TH, LL, 2, 2])
        cn = sb("cn", [TH, LL, 2, 192])
        cqT = sb("cqT", [64, LL, T])
        ckvT = sb("ckvT", [D, LL, T])
        kt = sb("kt", [TH, LL, 2, KVH, HD])
        kr2 = sb("kr2", [TH, LL, 2, KVH * DR])
        ksq = sb("ksq", [TH, LL, 4, HD])
        kss = sb("kss", [TH, LL, 4])
        krs = sb("krs", [TH, LL, 4])
        kT = sb("kT", [D, LL, T])
        v = sb("v", [TH, LL, 2, KVH * HD])
        q = sb("q", [D, LL, RW])
        q1 = sb("q1", [D, LL, 2 * T])
        qsq = sb("qsq", [D, LL, RW])
        rq = sb("rq", [CR, LL, NCH, KVH])
        nb = sb("nb", [CR, LL, KVH, NCH])
        P = sb("P", [CR, LL, NCH, T])
        PT = sb("PT", [TH, LL, 2, 2 * RW])
        h1 = sb("h1", [TH, LL, 2, D])
        xmb = sb("xmb", [TH, LL, 2, D])
        q2T = sb("q2T", [D, LL, T])
        qbd = sb("qbd", [D, LL, 2 * RW])
        k2T = sb("k2T", [D, LL, T])
        v2 = sb("v2", [TH, LL, 2, H, D + 16])
        rsum = sb("rsum", [CR, LL, 2, NCH])
        z = sb("z", [TH, LL, 2, D])
        t = sb("t", [TH, LL, 2, D])
        oT = qsq
        o2T = q2T
        neg_half = sb("neg_half", [CR, 10])

        h_loaded = [sem(f"l0_h_loaded_{l}") for l in range(LL)]
        h1_stored = [sem(f"l0_h1_stored_{l}") for l in range(LL)]
        t_stored = [sem(f"l0_t_stored_{l}") for l in range(LL)]
        consts_loaded = sem("l0_consts_loaded")

        def s(name):
            return sem("l0_" + name)

        block = ctx.enter_context(nc.Block())
        STEPS = B // LL
        PARTS = ((X, 0, 3), (Y, 3, 2))

        def need(eng, it, l, *names):
            for n in names:
                eng.wait_ge(s(n), LL * it + l + 1)

        def settle(eng):
            eng.sem_inc(s("settled"), 1)

        FIRST, SECOND = (0, 1), (2, 3)

        def in_turns(eng, first, second):
            def merge(*halves_):
                at = [[next(p), n, p] for n, p in enumerate(halves_)]
                while at:
                    now = min(at, key=lambda e: e[:2])
                    now[0] = next(now[2], None)
                    at = [e for e in at if e[0] is not None]

            merge(first(0, FIRST))
            merge(second(0, FIRST), first(0, SECOND))
            with eng.Fori(1, STEPS) as it:
                merge(first(it, FIRST), second(it - 1, SECOND))
                merge(second(it, FIRST), first(it, SECOND))
            merge(second(STEPS - 1, SECOND))

        @block.sync
        def _(sp):
            for name in L0_CONSTS:
                sp.dma_start(consts[name][:], io["c0_" + name]).then_inc(consts_loaded, 16)
            for l in range(LL):
                sp.sem_inc(h1_stored[l], 16)
                sp.sem_inc(t_stored[l], 16)

            def image(it, l):
                return bass.ds(LL * it + l, 1)

            def load(it, l):
                sp.dma_start(h[:, l], halves(io["h0"][image(it, l)])).then_inc(h_loaded[l], 16)

            def store_h1(it, l):
                need(sp, it, l, "h1_ready")
                sp.dma_start(halves(io["h1"][image(it, l)]), h1[:, l]).then_inc(h1_stored[l], 16)

            def store_t(it, l):
                need(sp, it, l, "t_ready")
                sp.dma_start(halves(io["t"][image(it, l)]), t[:, l]).then_inc(t_stored[l], 16)

            def h1_then_t(it, lanes, loads):
                for l in lanes:
                    store_h1(it, l)
                    if loads:
                        load(it + 1, l)
                for l in lanes:
                    store_t(it, l)

            for l in range(LL):
                load(0, l)
            h1_then_t(0, FIRST, True)
            with sp.Fori(1, STEPS - 1) as it:
                h1_then_t(it - 1, SECOND, True)
                h1_then_t(it, FIRST, True)
            h1_then_t(STEPS - 2, SECOND, True)
            h1_then_t(STEPS - 1, FIRST, False)
            h1_then_t(STEPS - 1, SECOND, False)
            for l in range(LL):
                sp.wait_ge(h1_stored[l], 16 * STEPS + 16)
                sp.wait_ge(t_stored[l], 16 * STEPS + 16)

        @block.gpsimd
        def _(pool):
            gp = nc.gpsimd
            gp.memset(neg_half[:], -0.5).then_inc(s("neg_half_ready"), 1)
            gp.memset(q[:, :, G * T:], 0.0).then_inc(s("pad_ready"), 1)
            gp.memset(qsq[:, :, G * T:], 0.0).then_inc(s("pad_ready"), 1)
            gp.memset(qbd[:, :, H * T:], 0.0).then_inc(s("pad_ready"), 1)
            for l in range(LL):
                gp.memset(v2[:, l], 0.0).then_inc(s("pad_ready"), 1)
            pool.wait_ge(s("neg_half_ready"), 1)
            pool.wait_ge(consts_loaded, 16 * len(L0_CONSTS))
            pool.wait_ge(s("bo2_ready"), 1)

            def power(it, l, src, dst, n, before, after, scale, eps):
                rows = src.shape[0]
                need(pool, it, l, before)
                settle(pool)
                gp.tensor_scalar(dst, src, scale, eps, ALU.mult, ALU.add).then_inc(s(after + "_sum"), 1)
                need(pool, it, l, after + "_sum")
                gp.tensor_tensor(dst, dst, neg_half[:rows, :n], ALU.pow).then_inc(s(after), 1)

            def first(it, lanes):
                yield 1
                for l in lanes:
                    power(it, l, mv[:, l, :, 1], rstd[:, l], 2, "ln_a", "rstd_a", 1.0, EPS_LN)
                yield 7
                for l in lanes:
                    power(it, l, cms[:, l].rearrange("p a b -> p (a b)"), crs[:, l].rearrange("p a b -> p (a b)"), 4, "cms", "crs", 1.0, EPS_RMS)
                yield 16
                for l in lanes:
                    power(it, l, kss[:, l], krs[:, l], 4, "kss", "krs", 1.0 / HD, EPS_RMS)
                yield 21
                for l in lanes:
                    rq2 = rq[:, l].rearrange("p c k -> p (c k)")
                    power(it, l, rq2, rq2, 10, "qss", "rq", 1.0, HD * EPS_RMS)
                for a in range(2):
                    yield 24 + 10 * a
                    for l in lanes:
                        need(pool, it, l, f"max_a{a}", "rq")
                        gp.tensor_tensor(nb[:, l, a], nb[:, l, a], rq[:, l, :, a], ALU.mult).then_inc(s(f"nb_a{a}"), 1)
                    yield 27 + 10 * a
                    for l in lanes:
                        need(pool, it, l, f"rsum_a{a}")
                        gp.tensor_tensor(P[:, l], P[:, l], rsum[:, l, a].unsqueeze(2).broadcast_to([CR, NCH, T]), ALU.mult).then_inc(s(f"P_a{a}"), 1)

            def second(it, lanes):
                yield 6
                for l in lanes:
                    power(it, l, mv[:, l, :, 1], rstd[:, l], 2, "ln_b", "rstd_b", 1.0, EPS_LN)
                yield 17
                for l in lanes:
                    need(pool, it, l, "q2T")
                    gp.tensor_tensor(qbd[:, l, :H * T].rearrange("p (h n) -> p h n", h=H),
                                     q2T[:, l].unsqueeze(1).broadcast_to([D, H, T]),
                                     consts["hmask"][:].unsqueeze(2).broadcast_to([D, H, T]), ALU.mult).then_inc(s("qbd"), 1)
                yield 12
                for l in lanes:
                    need(pool, it, l, "xn_b")
                    gp.tensor_tensor(xmb[:, l], xn[:, l], bo2[:].unsqueeze(1).broadcast_to([TH, 2, D]), ALU.add).then_inc(s("xmb"), 1)
                yield 40
                for l in lanes:
                    power(it, l, mv[:, l, :, 1], rstd[:, l], 2, "ln_c", "rstd_c", 1.0, EPS_LN)
                yield 42
                for l in lanes:
                    need(pool, it, l, "zn")
                    pool.wait_ge(t_stored[l], 16 * it + 16)
                    gp.tensor_tensor(t[:, l], z[:, l], consts["lng"][:].unsqueeze(1).broadcast_to([TH, 2, D]), ALU.mult).then_inc(s("t_scaled"), 1)
                yield 42
                for l in lanes:
                    need(pool, it, l, "t_scaled")
                    gp.tensor_tensor(t[:, l], t[:, l], consts["lnb"][:].unsqueeze(1).broadcast_to([TH, 2, D]), ALU.add).then_inc(s("t_ready"), 1)

            in_turns(pool, first, second)

        def layer_norm(dve, it, l, src, tag):
            for u in range(2):
                nc.vector.bn_stats(stats[:, l, u], src[:, l, u]).then_inc(s("bn_" + tag), 1)
            dve.wait_ge(s("bn_" + tag), 2 * LL * it + 2 * (l + 1))
            settle(dve)
            for u in range(2):
                ins = nc.vector.bn_aggr(mv[:, l, u], stats[:, l, u])
            ins.then_inc(s("ln_" + tag), 1)

        def normalise(dve, it, l, src, dst, tag, done):
            need(dve, it, l, "ln_" + tag, "rstd_" + tag)
            for u in range(2):
                ins = nc.vector.tensor_scalar(dst[:, l, u], src[:, l, u], mv[:, l, u, 0:1], rstd[:, l, u:u + 1],
                                              ALU.subtract, ALU.mult)
            ins.then_inc(s(done), 1)

        def score_max(dve, it, l, tag, a):
            need(dve, it, l, f"s_done_{tag}{a}")
            for bank, c0, n in PARTS:
                ins = nc.vector.tensor_reduce(nb[:, l, a, c0:c0 + n], ps[l][:CR, bank, :n * T].rearrange("p (i k) -> p i k", k=T),
                                              AX.X, ALU.max, negate=True)
            ins.then_inc(s(f"max_{tag}{a}"), 1)

        def keep_PT(op, eng, it, l, tag, a, khalf, *func):
            need(eng, it, l, f"pt_done_{tag}{a}{khalf}")
            for bank, c0, n in PARTS:
                ins = op(PT[:, l, khalf, RW * a + CR * c0:RW * a + CR * (c0 + n)], ps[l][:TH, bank, :CR * n], *func)
            ins.then_inc(s(f"PT_{tag}{a}{khalf}"), 1)

        @block.vector
        def _(dve):
            v_ = nc.vector
            dve.wait_ge(consts_loaded, 16 * len(L0_CONSTS))
            dve.wait_ge(s("setup_done"), 2)
            v_.tensor_copy(wvro[:], ps[0][:, X, :D])
            v_.tensor_tensor(bo2[:], ps[0][:TH, Y, :D], consts["bo"][:], ALU.add).then_inc(s("bo2_ready"), 1)
            v_.tensor_tensor(wqk[:], consts["qhn"][:], consts["khn"][:], ALU.mult).then_inc(s("wqk_ready"), 1)
            dve.wait_ge(s("pad_ready"), 3 + LL)
            def first(it, lanes):
                yield 0
                for l in lanes:
                    dve.wait_ge(h_loaded[l], 16 * it + 16)
                    layer_norm(dve, it, l, h, "a")
                yield 2
                for l in lanes:
                    normalise(dve, it, l, h, xn, "a", "xn_a")
                yield 7
                for l in lanes:
                    need(dve, it, l, "cms")
                    kr1 = kt[:, l, :, :, DR:]
                    v_.tensor_tensor(kr1, ps[l][:TH, :, 192:256].rearrange("p u (k d) -> p u k d", k=KVH),
                                     consts["cosk"][:].rearrange("p u (k d) -> p u k d", k=KVH), ALU.mult).then_inc(s("kr1"), 1)
                    v_.tensor_tensor(kr2[:, l], ps[l][:TH, :, 256:320], consts["sink"][:], ALU.mult).then_inc(s("kr2"), 1)
                    need(dve, it, l, "kr1", "kr2")
                    v_.tensor_tensor(kr1, kr1, kr2[:, l].rearrange("p u (k d) -> p u k d", k=KVH), ALU.add).then_inc(s("kr"), 1)
                yield 8
                for l in lanes:
                    need(dve, it, l, "crs")
                    v_.tensor_tensor(cn[:, l, :, :64], ps[l][:TH, :, :64], crs[:, l, :, 0:1].broadcast_to([TH, 2, 64]), ALU.mult)
                    v_.tensor_tensor(cn[:, l, :, 64:], ps[l][:TH, :, 64:192], crs[:, l, :, 1:2].broadcast_to([TH, 2, 128]), ALU.mult).then_inc(s("cn"), 1)
                yield 13
                for l in lanes:
                    need(dve, it, l, "kv_kept", "kr")
                    k4 = kt[:, l].rearrange("p u k d -> p (u k) d")
                    v_.tensor_tensor(ksq[:, l], k4, k4, ALU.mult).then_inc(s("ksq"), 1)
                yield 13
                for l in lanes:
                    need(dve, it, l, "ksq")
                    v_.tensor_reduce(kss[:, l], ksq[:, l], AX.X, ALU.add).then_inc(s("kss"), 1)
                for r in range(2):
                    yield 14 + 3 * r
                    for l in lanes:
                        need(dve, it, l, f"q_done_{r}")
                        cosq = consts["cosq"][:].unsqueeze(1).broadcast_to([D, 2, T])
                        sinq = consts["sinq"][:].unsqueeze(1).broadcast_to([D, 2, T])
                        qp = ps[l][:, Y, :2 * T].rearrange("p (c n) -> p c n", n=T)
                        q1v = q1[:, l].rearrange("p (c n) -> p c n", n=T)
                        v_.tensor_tensor(q1v, ps[l][:, X, :2 * T].rearrange("p (c n) -> p c n", n=T), cosq, ALU.mult).then_inc(s(f"q1_{r}"), 1)
                        v_.tensor_tensor(qp, qp, sinq, ALU.mult).then_inc(s(f"q2_{r}"), 1)
                        need(dve, it, l, f"q1_{r}", f"q2_{r}")
                        v_.tensor_tensor(q[:, l, 2 * T * r:2 * T * r + 2 * T], ps[l][:, Y, :2 * T], q1[:, l], ALU.add).then_inc(s(f"q_{r}"), 1)
                yield 18
                for l in lanes:
                    need(dve, it, l, "krs")
                    k4 = kt[:, l].rearrange("p u k d -> p (u k) d")
                    v_.tensor_tensor(k4, k4, krs[:, l].unsqueeze(2).broadcast_to([TH, 4, HD]), ALU.mult).then_inc(s("kn"), 1)
                yield 20
                for l in lanes:
                    need(dve, it, l, "qss_done")
                    v_.tensor_copy(rq[:, l].rearrange("p c k -> p (c k)"), ps[l][:CR, Y, :10]).then_inc(s("qss"), 1)
                for a in range(2):
                    yield 23 + 10 * a
                    for l in lanes:
                        score_max(dve, it, l, "a", a)
                    yield 26 + 10 * a
                    for l in lanes:
                        need(dve, it, l, f"exp_a{a}")
                        v_.reciprocal(rsum[:, l, a], rsum[:, l, a]).then_inc(s(f"rsum_a{a}"), 1)
                    yield 31 + 10 * a
                    for l in lanes:
                        keep_PT(v_.tensor_copy, dve, it, l, "a", a, 1)

            def second(it, lanes):
                yield 5
                for l in lanes:
                    need(dve, it, l, "out_done")
                    dve.wait_ge(h1_stored[l], 16 * it + 16)
                    v_.tensor_tensor(h1[:, l], ps[l][:TH, X, :2 * D].rearrange("p (u d) -> p u d", u=2), h[:, l], ALU.add).then_inc(s("h1_ready"), 1)
                    need(dve, it, l, "h1_ready")
                    layer_norm(dve, it, l, h1, "b")
                yield 8
                for l in lanes:
                    normalise(dve, it, l, h1, xn, "b", "xn_b")
                for a in range(2):
                    yield 20 + 8 * a
                    for l in lanes:
                        score_max(dve, it, l, "b", a)
                    yield 22 + 8 * a
                    for l in lanes:
                        need(dve, it, l, f"exp_b{a}")
                        v_.reciprocal(rsum[:, l, a], rsum[:, l, a]).then_inc(s(f"rsum_b{a}"), 1)
                        need(dve, it, l, f"rsum_b{a}")
                        v_.tensor_tensor(P[:, l], P[:, l], rsum[:, l, a].unsqueeze(2).broadcast_to([CR, NCH, T]), ALU.mult).then_inc(s(f"P_b{a}"), 1)
                    yield 26 + 8 * a
                    for l in lanes:
                        keep_PT(v_.tensor_copy, dve, it, l, "b", a, 1)
                yield 39
                for l in lanes:
                    need(dve, it, l, "proj_done", "xmb")
                    v_.tensor_tensor(z[:, l], ps[l][:TH, X, :2 * D].rearrange("p (u d) -> p u d", u=2), xmb[:, l], ALU.add).then_inc(s("z"), 1)
                    need(dve, it, l, "z")
                    layer_norm(dve, it, l, z, "c")
                yield 41
                for l in lanes:
                    normalise(dve, it, l, z, z, "c", "zn")

            in_turns(dve, first, second)

        @block.scalar
        def _(act):
            a_ = nc.scalar.activation
            act.wait_ge(consts_loaded, 16 * len(L0_CONSTS))
            act.wait_ge(s("pad_ready"), 3 + LL)
            act.wait_ge(s("wqk_ready"), 1)
            def first(it, lanes):
                yield 4
                for l in lanes:
                    need(act, it, l, "xt_done_a")
                    a_(xT[:, l], ps[l][:, X, :T], ACT.Copy).then_inc(s("xT_a"), 1)
                yield 6
                for l in lanes:
                    need(act, it, l, "lat_done")
                    for u in range(2):
                        for j, (c0, n) in enumerate(((0, 64), (64, 128))):
                            ins = a_(cn[:, l, u, c0:c0 + n], ps[l][:TH, u, c0:c0 + n], ACT.Square, scale=n ** -0.5,
                                     accum_out=cms[:, l, u, j:j + 1])
                    ins.then_inc(s("cms"), 1)
                yield 10
                for l in lanes:
                    need(act, it, l, "cT_done")
                    a_(cqT[:, l], ps[l][:64, X, :T], ACT.Copy, scale=consts["qln"][:])
                    a_(ckvT[:, l], ps[l][:, X, T:2 * T], ACT.Copy, scale=consts["kvln"][:]).then_inc(s("cT"), 1)
                yield 12
                for l in lanes:
                    need(act, it, l, "kv_done")
                    kv = ps[l][:TH, Y, :384].rearrange("p (u n) -> p u n", u=2)
                    a_(kt[:, l, :, :, :DR], kv[:, :, :64].rearrange("p u (k d) -> p u k d", k=KVH), ACT.Copy)
                    a_(v[:, l], kv[:, :, 64:], ACT.Copy).then_inc(s("kv_kept"), 1)
                for r in range(2):
                    yield 15 + 3 * r
                    for l in lanes:
                        need(act, it, l, f"q_{r}")
                        a_(qsq[:, l, 2 * T * r:2 * T * r + 2 * T], q[:, l, 2 * T * r:2 * T * r + 2 * T], ACT.Square).then_inc(s(f"qsq_{r}"), 1)
                yield 20
                for l in lanes:
                    need(act, it, l, "kT_done")
                    a_(kT[:, l], ps[l][:, X, :T], ACT.Copy, scale=wqk[:]).then_inc(s("kT"), 1)
                for a in range(2):
                    yield 25 + 10 * a
                    for l in lanes:
                        need(act, it, l, f"nb_a{a}")
                        for bank, c0, n in PARTS:
                            for i in range(n):
                                ins = a_(P[:, l, c0 + i], ps[l][:CR, bank, T * i:T * i + T], ACT.Exp,
                                         bias=nb[:, l, a, c0 + i:c0 + i + 1], scale=rq[:, l, c0 + i, a:a + 1],
                                         accum_out=rsum[:, l, a, c0 + i:c0 + i + 1])
                        ins.then_inc(s(f"exp_a{a}"), 1)
                    yield 29 + 10 * a
                    for l in lanes:
                        keep_PT(a_, act, it, l, "a", a, 0, ACT.Copy)

            def second(it, lanes):
                yield 2
                for l in lanes:
                    need(act, it, l, "o_done")
                    for r in range(2):
                        ins = a_(oT[:, l, 2 * T * r:2 * T * r + 2 * T], ps[l][:, r, :2 * T], ACT.Copy)
                    ins.then_inc(s("oT"), 1)
                yield 11
                for l in lanes:
                    need(act, it, l, "xt_done_b")
                    a_(xT[:, l], ps[l][:, Y, :T], ACT.Copy).then_inc(s("xT_b"), 1)
                yield 15
                for l in lanes:
                    need(act, it, l, "qk2_done")
                    a_(q2T[:, l], ps[l][:, X, :T], ACT.Identity, bias=consts["bq"][:]).then_inc(s("q2T"), 1)
                    a_(k2T[:, l], ps[l][:, X, T:2 * T], ACT.Identity, bias=consts["bk"][:]).then_inc(s("k2T"), 1)
                yield 15
                for l in lanes:
                    need(act, it, l, "v2_done")
                    a_(v2[:, l, :, :, :16], ps[l][:TH, Y, :2 * D].rearrange("p (u h e) -> p u h e", u=2, e=16), ACT.Copy).then_inc(s("v2"), 1)
                for a in range(2):
                    yield 21 + 8 * a
                    for l in lanes:
                        need(act, it, l, f"max_b{a}")
                        for bank, c0, n in PARTS:
                            for i in range(n):
                                ins = a_(P[:, l, c0 + i], ps[l][:CR, bank, T * i:T * i + T], ACT.Exp, bias=nb[:, l, a, c0 + i:c0 + i + 1],
                                         accum_out=rsum[:, l, a, c0 + i:c0 + i + 1])
                        ins.then_inc(s(f"exp_b{a}"), 1)
                    yield 24 + 8 * a
                    for l in lanes:
                        keep_PT(a_, act, it, l, "b", a, 0, ACT.Copy)
                yield 37
                for l in lanes:
                    need(act, it, l, "o2_done")
                    a_(o2T[:, l], ps[l][:, Y, :T], ACT.Copy).then_inc(s("o2T"), 1)

            in_turns(act, first, second)

        @block.tensor
        def _(pe):
            mm, tr = nc.tensor.matmul, nc.tensor.transpose

            def scores(it, l, tag, a, keys, queries, masked):
                for bank, c0, n in PARTS:
                    for i in range(n):
                        ins = mm(ps[l][:CR, bank, T * i:T * i + T], queries(c0 + i), keys,
                                 start=(i == 0 or not masked), stop=not masked, skip_group_check=masked)
                if masked:
                    for bank, c0, n in PARTS:
                        ins = mm(ps[l][:CR, bank, :n * T], identb[:CR, :CR], maskb[:, c0:c0 + n], start=False, stop=True, skip_group_check=True)
                ins.then_inc(s(f"s_done_{tag}{a}"), 1)

            def transposes_P(it, l, tag, a, khalf):
                for bank, c0, n in PARTS:
                    for i in range(n):
                        ins = tr(ps[l][:TH, bank, CR * i:CR * i + CR], P[:, l, c0 + i, TH * khalf:TH * khalf + TH], ident[:CR, :CR])
                ins.then_inc(s(f"pt_done_{tag}{a}{khalf}"), 1)

            def attend(it, lanes, tag, turn, scores_of, before):
                for a in range(2):
                    yield turn[a]
                    for l in lanes:
                        need(pe, it, l, *(before if a == 0 else (f"PT_{tag}01",)))
                        settle(pe)
                        scores_of(l, a)
                    yield turn[a] + (6 if tag == "a" else 4)
                    for l in lanes:
                        need(pe, it, l, f"P_{tag}{a}")
                        transposes_P(it, l, tag, a, 0)
                    yield turn[a] + (8 if tag == "a" else 6)
                    for l in lanes:
                        need(pe, it, l, f"PT_{tag}{a}0")
                        transposes_P(it, l, tag, a, 1)

            pe.wait_ge(consts_loaded, 16 * len(L0_CONSTS))
            for c in range(4):
                ins = mm(ps[0][:, X, :D], consts["wvrT"][:, c], consts["wo2"][:, c], start=(c == 0), stop=(c == 3))
            ins.then_inc(s("setup_done"), 1)
            mm(ps[0][:TH, Y, :D], consts["bv"][:], consts["wproj"][:], start=True, stop=True).then_inc(s("setup_done"), 1)
            pe.wait_ge(s("bo2_ready"), 1)
            pe.wait_ge(s("pad_ready"), 3 + LL)
            def first(it, lanes):
                yield 3
                for l in lanes:
                    need(pe, it, l, "xn_a")
                    for u in range(2):
                        ins = tr(ps[l][:, X, TH * u:TH * u + TH], xn[:, l, u], ident[:TH, :TH])
                    ins.then_inc(s("xt_done_a"), 1)
                yield 5
                for l in lanes:
                    need(pe, it, l, "xT_a")
                    for u in range(2):
                        ins = mm(ps[l][:TH, u, :320], xT[:, l, TH * u:TH * u + TH], consts["wlat"][:], start=True, stop=True)
                    ins.then_inc(s("lat_done"), 1)
                yield 9
                for l in lanes:
                    need(pe, it, l, "cn", "kr")
                    settle(pe)
                    for u in range(2):
                        tr(ps[l][:64, X, TH * u:TH * u + TH], cn[:, l, u, :64], ident[:TH, :TH])
                        ins = tr(ps[l][:, X, T + TH * u:T + TH * u + TH], cn[:, l, u, 64:], ident[:TH, :TH])
                    ins.then_inc(s("cT_done"), 1)
                yield 11
                for l in lanes:
                    need(pe, it, l, "cT")
                    for u in range(2):
                        ins = mm(ps[l][:TH, Y, 192 * u:192 * u + 192], ckvT[:, l, TH * u:TH * u + TH], consts["wkv"][:], start=True, stop=True)
                    ins.then_inc(s("kv_done"), 1)
                for r in range(2):
                    yield 13 + 3 * r
                    for l in lanes:
                        need(pe, it, l, "kv_kept" if r == 0 else "q_0")
                        for w, bank in (("wqa", X), ("wqp", Y)):
                            for c in range(2):
                                ins = mm(ps[l][:, bank, T * c:T * c + T], consts[w][:, 2 * r + c], cqT[:, l], start=True, stop=True)
                        ins.then_inc(s(f"q_done_{r}"), 1)
                yield 19
                for l in lanes:
                    need(pe, it, l, "q_1", "kn")
                    for u in range(2):
                        ins = tr(ps[l][:, X, TH * u:TH * u + TH], kt[:, l, u].rearrange("p k d -> p (k d)"), ident[:TH, :TH])
                    ins.then_inc(s("kT_done"), 1)
                yield 19
                for l in lanes:
                    need(pe, it, l, "qsq_1")
                    settle(pe)
                    for i in range(NCH):
                        ins = mm(ps[l][:CR, Y, 2 * i:2 * i + 2], qsq[:, l, CR * i:CR * i + CR], consts["half_sum"][:], start=True, stop=True)
                    ins.then_inc(s("qss_done"), 1)
                yield from attend(it, lanes, "a", (22, 32), lambda l, a: scores(it, l, "a", a, kT[HD * a:HD * a + HD, l],
                                                    lambda i: q[HD * a:HD * a + HD, l, CR * i:CR * i + CR], True), ("kT", "qss"))

            def second(it, lanes):
                yield 0
                for l in lanes:
                    need(pe, it, l, "PT_a11")
                    for r in range(2):
                        for k in range(KVH):
                            for u in range(2):
                                c = RW * k + 2 * T * r
                                ins = mm(ps[l][HD * k:HD * k + HD, r, :2 * T], v[:, l, u, HD * k:HD * k + HD], PT[:, l, u, c:c + 2 * T], start=(u == 0), stop=(u == 1))
                    ins.then_inc(s("o_done"), 1)
                yield 3
                for l in lanes:
                    need(pe, it, l, "oT")
                    for u in range(2):
                        out = ps[l][:TH, X, D * u:D * u + D]
                        mm(out, xT[:, l, TH * u:TH * u + TH], wvro[:], start=True, stop=False)
                        for g in range(G):
                            ins = mm(out, oT[:, l, T * g + TH * u:T * g + TH * u + TH], consts["wo2"][:, g], start=False, stop=(g == G - 1))
                    ins.then_inc(s("out_done"), 1)
                yield 10
                for l in lanes:
                    need(pe, it, l, "xn_b")
                    for u in range(2):
                        ins = tr(ps[l][:, Y, TH * u:TH * u + TH], xn[:, l, u], ident[:TH, :TH])
                    ins.then_inc(s("xt_done_b"), 1)
                yield 13
                for l in lanes:
                    need(pe, it, l, "xT_b")
                    mm(ps[l][:, X, :T], consts["wq"][:], xT[:, l], start=True, stop=True)
                    mm(ps[l][:, X, T:2 * T], consts["wk"][:], xT[:, l], start=True, stop=True).then_inc(s("qk2_done"), 1)
                    for u in range(2):
                        ins = mm(ps[l][:TH, Y, D * u:D * u + D], xT[:, l, TH * u:TH * u + TH], consts["wv"][:], start=True, stop=True)
                    ins.then_inc(s("v2_done"), 1)
                yield from attend(it, lanes, "b", (19, 27), lambda l, a: scores(it, l, "b", a, k2T[:, l],
                                                    lambda i: qbd[:, l, RW * a + CR * i:RW * a + CR * i + CR], False), ("qbd", "k2T", "v2"))
                yield 36
                for l in lanes:
                    need(pe, it, l, "PT_b11")
                    for n, (hh, u) in enumerate((hh, u) for hh in range(H) for u in range(2)):
                        wide = v2[:, l, u].rearrange("p h e -> p (h e)")
                        ins = mm(ps[l][:, Y, :T], wide[:, D * hh:D * hh + D], PT[:, l, u, T * hh:T * hh + T],
                                 start=(n == 0), stop=(n == 2 * H - 1))
                    ins.then_inc(s("o2_done"), 1)
                yield 38
                for l in lanes:
                    need(pe, it, l, "o2T")
                    for u in range(2):
                        ins = mm(ps[l][:TH, X, D * u:D * u + D], o2T[:, l, TH * u:TH * u + TH], consts["wproj"][:], start=True, stop=True)
                    ins.then_inc(s("proj_done"), 1)

            in_turns(pe, first, second)


def block_rows(ap, j):
    return ap.rearrange("(j p) d -> j p d", p=128)[bass.ds(j, 1)].rearrange("o p d -> (o p) d")


def route(net, tag, ne, nb, source, score_consts, score_stage, wide_gate):
    nc, io, sem = net.nc, net.io, net.sem
    with ExitStack() as ctx:
        ps = net.psum(ctx, tag)
        def sb(name, shape, dt=F32):
            return net.sb(ctx, f"{tag}_" + name, shape, dt)

        def s(name):
            return sem(f"{tag}_" + name)

        r = {}
        names = score_consts + ("ident", "upper", "onesb", "scan", "jcol")
        consts = {}
        for name in names:
            src = io[f"c{tag}_" + name]
            consts[name] = sb("c_" + name, list(src.shape), src.dtype)
        nconst = 16 * len(names)
        ident = consts["ident"]
        x = sb("x", [128, L, D])
        xT = sb("xT", [D, L, 128], F32 if wide_gate else BF16)
        onehot = sb("onehot", [128, L, ne], BF16)
        onehot_all = sb("onehot_all", [128, NT, ne], BF16)
        acc = sb("acc", [128, L, ne], BF16)
        res = sb("res", [128, L, 2])
        res_all = sb("res_all", [128, NT, 2])
        weighted = sb("weighted", [128, L, ne])
        blocks_f = sb("blocks_f", [ne, 1])
        blocks_i = sb("blocks_i", [ne, 2], I32)
        blocks_b = sb("blocks_b", [ne, 128], BF16)
        ends = sb("ends", [128, 2 * ne])
        eb_f = sb("eb_f", [128, 2])
        eb_i = sb("eb_i", [128, 2], I32)
        eb_junk = sb("eb_junk", [128, 2, ne])
        base_of = sb("base_of", [128, NT, ne])
        slot_f = sb("slot_f", [128, NT])
        gate = sb("gate", [128, NT])
        rows_f = sb("rows_f", [NT, 2, 128])
        slots = net.slots
        slot_col = sb("slot_col", [128, L], I32)
        x_loaded = [s(f"x_loaded_{l}") for l in range(L)]
        x_again = [s(f"x_again_{l}") for l in range(L)]
        scattered = [s(f"scattered_{l}") for l in range(L)]
        env = dict(net=net, ps=ps, sb=sb, s=s, consts=consts, x=x, xT=xT, onehot=onehot, res=res, x_loaded=x_loaded)

        def need(eng, base, l, *which):
            for n in which:
                eng.wait_ge(s(n), base + (l + 1))

        env["need"] = need
        score = score_stage(env)

        def per_block(eng, body):
            with eng.Fori(0, NT // L) as it:
                body(L * it, range(L))
            body(NT - NT % L, range(NT % L))

        block = ctx.enter_context(nc.Block())

        @block.sync
        def _(sp):
            for name in names:
                sp.dma_start(consts[name][:], io[f"c{tag}_" + name]).then_inc(s("consts_loaded"), 16)
            score.get("sync", lambda e: None)(sp)

            def load(base, lanes):
                for l in lanes:
                    sp.wait_ge(s("x_free"), base + (l + 1))
                    sp.dma_start(x[:, l], block_rows(source, base + l)).then_inc(x_loaded[l], 16)

            per_block(sp, load)
            sp.wait_ge(s("eb_ready"), 1)
            sp.dma_start(io["eb"], eb_i[:]).then_inc(s("tables_stored"), 16)
            sp.wait_ge(s("rows_ready"), 1)
            sp.dma_start(io["slot_gate"].rearrange("g (j p) -> j g p", p=128), rows_f[:]).then_inc(s("tables_stored"), 16)

            def load_again(base, lanes):
                for l in lanes:
                    sp.wait_ge(s("x_scattered"), base + (l + 1))
                    sp.dma_start(x[:, l], block_rows(source, base + l)).then_inc(x_again[l], 16)

            per_block(sp, load_again)
            sp.wait_ge(s("tables_stored"), 32)

        @block.tensor
        def _(pe):
            mm, tr = nc.tensor.matmul, nc.tensor.transpose
            pe.wait_ge(s("consts_loaded"), nconst)
            score.get("pe_setup", lambda e: None)(pe)
            pe.sem_inc(s("x_free"), L)

            def body(base, lanes):
                for l in lanes:
                    pe.wait_ge(x_loaded[l], 8 * base + 16)
                    tr(ps[l][:, 0, :128], x[:, l], ident[:]).then_inc(s("x_free"), 1)
                score["pe"](pe, base, lanes)
                for l in lanes:
                    need(pe, base, l, "onehot", "acc")
                    mm(ps[l][:, 2, :ne], consts["upper"][:], onehot[:, l], start=True, stop=False)
                    mm(ps[l][:, 2, :ne], consts["onesb"][:], acc[:, l], start=False, stop=True).then_inc(s("rank_done"), 1)

            per_block(pe, body)
            pe.wait_ge(s("acc"), NT + 1)
            mm(ps[0][:ne, 0, :1], acc[:, NT % L], consts["onesb"][:, :1], start=True, stop=True).then_inc(s("count_done"), 1)
            pe.wait_ge(s("blocks_b"), 1)
            mm(ps[0][:, 1, :2 * ne], blocks_b[:], consts["scan"][:], start=True, stop=True).then_inc(s("ends_done"), 1)
            pe.wait_ge(s("slot_f"), 1)
            tr(ps[0][:NT, 2, :128], slot_f[:], ident[:])
            tr(ps[0][:NT, 2, 128:256], gate[:], ident[:]).then_inc(s("rows_done"), 1)

        @block.vector
        def _(dve):
            v_ = nc.vector
            dve.wait_ge(s("consts_loaded"), nconst)
            v_.memset(acc[:], 0.0).then_inc(s("acc"), 1)
            if not wide_gate:
                v_.memset(res[:], 1.0).then_inc(s("res_set"), 1)
                dve.wait_ge(s("res_set"), 1)
            score.get("dve_setup", lambda e: None)(dve)

            def body(base, lanes):
                score["dve"](dve, base, lanes)
                for l in lanes:
                    need(dve, base, l, "onehot", "acc", "rank_done")
                    v_.tensor_tensor(acc[:, (l + 1) % L], acc[:, l], onehot[:, l], ALU.add).then_inc(s("acc"), 1)
                    v_.tensor_copy(onehot_all[:, bass.ds(base + l, 1)].rearrange("p o e -> p (o e)"), onehot[:, l])
                    v_.scalar_tensor_tensor(weighted[:, l], ps[l][:, 2, :ne], 1.0, onehot[:, l], ALU.mult, ALU.mult,
                                            accum_out=res[:, l, 0:1]).then_inc(s("rank"), 1)
                    need(dve, base, l, "rank")
                    v_.tensor_copy(res_all[:, bass.ds(base + l, 1)].rearrange("p o e -> p (o e)"), res[:, l]).then_inc(s("res_kept"), 1)

            per_block(dve, body)
            dve.wait_ge(s("count_done"), 1)
            v_.tensor_scalar(blocks_i[:, 0:1], ps[0][:ne, 0, :1], 127.0, None, ALU.add).then_inc(s("b1"), 1)
            dve.wait_ge(s("b1"), 1)
            v_.tensor_scalar(blocks_i[:, 1:2], blocks_i[:, 0:1], 7, None, ALU.arith_shift_right).then_inc(s("b2"), 1)
            dve.wait_ge(s("b2"), 1)
            v_.tensor_copy(blocks_f[:], blocks_i[:, 1:2]).then_inc(s("b3"), 1)
            dve.wait_ge(s("b3"), 1)
            v_.tensor_scalar(blocks_b[:], consts["onesb"][:ne], blocks_f[:], None, ALU.mult).then_inc(s("blocks_b"), 1)
            dve.wait_ge(s("ends_done"), 1)
            v_.tensor_copy(ends[:], ps[0][:, 1, :2 * ne]).then_inc(s("ends"), 1)
            dve.wait_ge(s("ends"), 1)
            for i in range(2):
                ins = v_.tensor_scalar(eb_junk[:, i], ends[:, :ne], consts["jcol"][:, i:i + 1], None, ALU.is_le, ALU.add,
                                       accum_out=eb_f[:, i:i + 1])
            ins.then_inc(s("eb_f"), 1)
            dve.wait_ge(s("eb_f"), 1)
            v_.tensor_scalar(eb_i[:], eb_f[:], float(ne - 1), None, ALU.min).then_inc(s("eb_ready"), 1)
            dve.wait_ge(s("res_kept"), NT)
            v_.tensor_tensor(base_of[:], onehot_all[:], ends[:, ne:].unsqueeze(1).broadcast_to([128, NT, ne]), ALU.mult).then_inc(s("base_of"), 1)
            dve.wait_ge(s("base_of"), 1)
            v_.tensor_reduce(slot_f[:], base_of[:], AX.X, ALU.add).then_inc(s("base_sum"), 1)
            v_.reciprocal(gate[:], res_all[:, :, 1])
            dve.wait_ge(s("base_sum"), 1)
            v_.tensor_tensor(slot_f[:], slot_f[:], res_all[:, :, 0], ALU.add).then_inc(s("slot_f"), 1)
            dve.wait_ge(s("slot_f"), 1)
            v_.tensor_copy(slots[:], slot_f[:]).then_inc(s("slots"), 1)
            dve.wait_ge(s("rows_done"), 1)
            v_.tensor_copy(rows_f[:], ps[0][:NT, 2, :256].rearrange("p (g n) -> p g n", g=2)).then_inc(s("rows_ready"), 1)

        @block.scalar
        def _(act):
            act.wait_ge(s("consts_loaded"), nconst)
            if "act" in score:
                per_block(act, lambda base, lanes: score["act"](act, base, lanes))

        @block.gpsimd
        def _(pool):
            pool.sem_inc(s("x_scattered"), L)
            pool.wait_ge(s("slots"), 1)

            def scatter(base, lanes):
                for l in lanes:
                    nc.gpsimd.tensor_copy(slot_col[:, l:l + 1], slots[:, bass.ds(base + l, 1)]).then_inc(s("slot_col"), 1)
                for l in lanes:
                    need(pool, base, l, "slot_col")
                    pool.wait_ge(x_again[l], 8 * base + 16)
                    pool.sem_inc(s("settled"), 1)
                    nc.gpsimd.indirect_dma_start(io[f"sorted{tag[-1]}"], bass.IndirectOffsetOnAxis(slot_col[:, l:l + 1], 0),
                                                 x[:, l], None).then_inc(scattered[l], 16)
                for l in lanes:
                    pool.wait_ge(scattered[l], 8 * base + 16)
                    pool.sem_inc(s("x_scattered"), 1)

            per_block(pool, scatter)


def gate_scores(env):
    net, sb, s, need = env["net"], env["sb"], env["s"], env["need"]
    nc, ps, consts = net.nc, env["ps"], env["consts"]
    xT, onehot, res = env["xT"], env["onehot"], env["res"]
    lg, nmx, ex, first, mx2 = sb("lg", [128, L, E0]), sb("nmx", [128, L]), sb("ex", [128, L, E0]), sb("first", [128, L, E0]), sb("mx2", [128, L])

    def pe(eng, base, lanes):
        for l in lanes:
            need(eng, base, l, "xT")
            eng.sem_inc(s("settled"), 1)
            nc.tensor.matmul(ps[l][:, 1, :E0], xT[:, l], consts["gw"][:], start=True, stop=True).then_inc(s("scores_done"), 1)

    def act(eng, base, lanes):
        for l in lanes:
            eng.wait_ge(s("x_free"), base + (l + 1 + L))
            nc.scalar.activation(xT[:, l], ps[l][:, 0, :128], ACT.Copy).then_inc(s("xT"), 1)
        for l in lanes:
            need(eng, base, l, "lg0")
            nc.scalar.activation(ex[:, l], lg[:, l], ACT.Exp, accum_out=res[:, l, 1:2]).then_inc(s("gate_sum"), 1)

    def dve(eng, base, lanes):
        v_ = nc.vector
        for l in lanes:
            need(eng, base, l, "scores_done")
            v_.tensor_tensor(lg[:, l], ps[l][:, 1, :E0], consts["gb"][:], ALU.add).then_inc(s("lg"), 1)
            need(eng, base, l, "lg")
            v_.tensor_reduce(nmx[:, l:l + 1], lg[:, l], AX.X, ALU.max, negate=True).then_inc(s("nmx"), 1)
            need(eng, base, l, "nmx")
            v_.tensor_scalar(lg[:, l], lg[:, l], nmx[:, l:l + 1], None, ALU.add).then_inc(s("lg0"), 1)
            need(eng, base, l, "lg0")
            v_.scalar_tensor_tensor(first[:, l], lg[:, l], 0.0, consts["order"][:], ALU.is_equal, ALU.mult).then_inc(s("first"), 1)
            need(eng, base, l, "first")
            v_.tensor_reduce(mx2[:, l:l + 1], first[:, l], AX.X, ALU.max).then_inc(s("mx2"), 1)
            need(eng, base, l, "mx2", "gate_sum")
            v_.tensor_scalar(onehot[:, l], first[:, l], mx2[:, l:l + 1], None, ALU.is_equal).then_inc(s("onehot"), 1)

    return {"pe": pe, "act": act, "dve": dve}


def route_experts(net):
    route(net, "r0", E0, NB0, net.io["t"].rearrange("b t d -> (b t) d"), ("gw", "gb", "order"), gate_scores, True)


def sign_scores(env):
    net, sb, s, need = env["net"], env["sb"], env["s"], env["need"]
    nc, ps, consts = net.nc, env["ps"], env["consts"]
    xT, onehot = env["xT"], env["onehot"]
    wd = sb("wd", [D, T1, DH])
    sums, pos = sb("sums", [D, T1]), sb("pos", [D, T1])
    nsig = sb("nsig", [D, T1])
    csum, cpos, csig = sb("csum", [D, CL]), sb("cpos", [D, CL]), sb("csig", [D, CL])
    sig = sb("sig", [D, CL + T1], BF16)
    xpos = sb("xpos", [D, L, 128])
    key, mx = sb("key", [128, L, CL + T1]), sb("mx", [128, L, 2])
    big = sb("big", [128, L, CL])

    def sync(eng):
        eng.dma_start(wd[:], net.io["wdT"]).then_inc(s("wd_loaded"), 16)

    def dve_setup(eng):
        v_ = nc.vector
        eng.wait_ge(s("wd_loaded"), 16)
        v_.tensor_reduce(sums[:], wd[:], AX.X, ALU.add).then_inc(s("sums"), 1)
        eng.wait_ge(s("sums"), 1)
        v_.tensor_scalar(pos[:], sums[:], 0.0, None, ALU.is_gt).then_inc(s("pos"), 1)
        eng.wait_ge(s("pos"), 1)
        v_.scalar_tensor_tensor(nsig[:], sums[:], 0.0, pos[:], ALU.is_lt, ALU.subtract).then_inc(s("nsig"), 1)
        eng.wait_ge(s("nsig"), 1)
        v_.tensor_scalar(sig[:, CL:], nsig[:], float(T1), None, ALU.mult)
        v_.tensor_reduce(csum[:], nsig[:].rearrange("p (c t) -> p c t", c=CL), AX.X, ALU.add).then_inc(s("csum"), 1)
        eng.wait_ge(s("csum"), 1)
        v_.tensor_scalar(cpos[:], csum[:], 0.0, None, ALU.is_lt).then_inc(s("cpos"), 1)
        eng.wait_ge(s("cpos"), 1)
        v_.scalar_tensor_tensor(csig[:], csum[:], 0.0, cpos[:], ALU.is_gt, ALU.subtract).then_inc(s("csig"), 1)
        eng.wait_ge(s("csig"), 1)
        v_.tensor_scalar(sig[:, :CL], csig[:], float(CL), None, ALU.mult).then_inc(s("sig"), 1)

    def pe_setup(eng):
        eng.wait_ge(s("sig"), 1)

    def pe(eng, base, lanes):
        for l in lanes:
            need(eng, base, l, "xT")
            nc.tensor.matmul(ps[l][:, 1, :CL + T1], xT[:, l], sig[:], start=True, stop=True).then_inc(s("scores_done"), 1)

    def dve(eng, base, lanes):
        v_ = nc.vector
        for l in lanes:
            eng.wait_ge(s("x_free"), base + (l + 1 + L))
            v_.tensor_scalar(xpos[:, l], ps[l][:, 0, :128], 0.0, None, ALU.is_gt).then_inc(s("xpos"), 1)
            need(eng, base, l, "xpos")
            v_.scalar_tensor_tensor(xT[:, l], ps[l][:, 0, :128], 0.0, xpos[:, l], ALU.is_lt, ALU.subtract).then_inc(s("xT"), 1)
        for l in lanes:
            need(eng, base, l, "scores_done")
            v_.tensor_tensor(key[:, l], ps[l][:, 1, :CL + T1], consts["order"][:], ALU.add).then_inc(s("key"), 1)
            need(eng, base, l, "key")
            v_.tensor_reduce(mx[:, l, 0:1], key[:, l, :CL], AX.X, ALU.max).then_inc(s("mx_c"), 1)
            need(eng, base, l, "mx_c")
            v_.tensor_scalar(big[:, l], key[:, l, :CL], mx[:, l, 0:1], float(1 << 15), ALU.is_equal, ALU.mult).then_inc(s("big"), 1)
            need(eng, base, l, "big")
            kt = key[:, l, CL:].rearrange("p (c t) -> p c t", c=CL)
            v_.tensor_tensor(kt, kt, big[:, l].unsqueeze(2).broadcast_to([128, CL, T1 // CL]), ALU.add).then_inc(s("key_t"), 1)
            need(eng, base, l, "key_t")
            v_.tensor_reduce(mx[:, l, 1:2], key[:, l, CL:], AX.X, ALU.max).then_inc(s("mx_t"), 1)
            need(eng, base, l, "mx_t")
            v_.tensor_scalar(onehot[:, l], key[:, l, CL:], mx[:, l, 1:2], None, ALU.is_equal).then_inc(s("onehot"), 1)

    return {"sync": sync, "dve_setup": dve_setup, "pe_setup": pe_setup, "pe": pe, "dve": dve}


def route_tiles(net):
    route(net, "r1", T1, NB1, net.io["xf"].rearrange("b t d -> (b t) d"), ("order",), sign_scores, False)


def sorted_blocks(net, tag, nb, width, emit):
    nc, io, sem = net.nc, net.io, net.sem
    S = 2 * L
    with ExitStack() as ctx:
        ps = net.psum(ctx, tag)
        def sb(name, shape, dt=F32):
            return net.sb(ctx, f"{tag}_" + name, shape, dt)

        def s(name):
            return sem(f"{tag}_" + name)

        eb = sb("eb", [1, 256], I32)
        ident = sb("ident", [128, 128])
        x = sb("x", [128, S, D])
        w = sb("w", [128, S, width])
        xT = sb("xT", [D, L, 128])
        y = sb("y", [128, S, D])
        loaded = [s(f"loaded_{i}") for i in range(S)]
        y_stored = [s(f"y_stored_{i}") for i in range(S)]

        def need(eng, base, l, *which):
            for n in which:
                eng.wait_ge(s(n), base + (l + 1))

        def per_block(eng, body):
            with eng.Fori(0, nb // S) as it:
                for a in range(2):
                    body(S * it + L * a, L * a, it)
            if nb % S:
                body(nb - nb % S, 0, nb // S)

        env = dict(net=net, ps=ps, sb=sb, s=s, need=need, x=x, w=w, xT=xT, y=y, y_stored=y_stored)
        parts = emit(env)
        block = ctx.enter_context(nc.Block())

        @block.sync
        def _(sp):
            sp.dma_start(ident[:], io["ident"]).then_inc(s("ident_loaded"), 16)
            sp.dma_start(eb[:], io["eb"].rearrange("p g -> (p g)").unsqueeze(0)).then_inc(s("eb_loaded"), 16)
            parts.get("sync", lambda e: None)(sp)
            sp.wait_ge(s("eb_loaded"), 16)
            for i in range(S):
                sp.sem_inc(y_stored[i], 16)

            def load(base, slot0):
                for l in range(L):
                    e = sp.value_load(eb[0:1, bass.ds(base + l, 1)], min_val=0, max_val=io[f"{tag}_w"].shape[0] - 1)
                    sp.dma_start(w[:, slot0 + l], io[f"{tag}_w"][bass.ds(e, 1)].rearrange("o p n -> (o p) n")).then_inc(loaded[slot0 + l], 16)
                    sp.dma_start(x[:, slot0 + l], block_rows(io[f"sorted{tag[-1]}"], base + l)).then_inc(loaded[slot0 + l], 16)

            def store(base, slot0):
                for l in range(L):
                    need(sp, base, l, "y_ready")
                    sp.dma_start(block_rows(io[f"y{tag[-1]}"], base + l), y[:, slot0 + l]).then_inc(y_stored[slot0 + l], 16)

            load(0, 0)
            load(L, L)
            last = nb - 3 * L
            with sp.Fori(0, last // S) as it:
                for a in range(2):
                    store(S * it + L * a, L * a)
                    load(S * it + L * a + S, L * a)
            store(last, 0)
            load(last + S, 0)
            store(last + L, L)
            store(last + S, 0)
            for i in range(S):
                sp.wait_ge(y_stored[i], 16 * (nb // S + (i < nb % S)) + 16)

        @block.gpsimd
        def _(pool):
            parts.get("pool_setup", lambda e: None)(pool)

            def body(base, slot0, it):
                for l in range(L):
                    pool.wait_ge(loaded[slot0 + l], 32 * it + 32)
                parts["pool"](pool, base, slot0)

            if "pool" in parts:
                per_block(pool, body)

        @block.tensor
        def _(pe):
            pe.wait_ge(s("ident_loaded"), 16)

            def body(base, slot0, it):
                for l in range(L):
                    pe.wait_ge(loaded[slot0 + l], 32 * it + 32)
                    nc.tensor.transpose(ps[l][:, 0, :128], x[:, slot0 + l], ident[:]).then_inc(s("x_transposed"), 1)
                parts["pe"](pe, base, slot0)

            per_block(pe, body)

        @block.vector
        def _(dve):
            parts.get("dve_setup", lambda e: None)(dve)

            def body(base, slot0, it):
                for l in range(L):
                    need(dve, base, l, "x_transposed")
                    nc.vector.tensor_copy(xT[:, l], ps[l][:, 0, :128]).then_inc(s("xT"), 1)
                parts["dve"](dve, base, slot0, it)

            per_block(dve, body)

        @block.scalar
        def _(act):
            per_block(act, lambda base, slot0, it: parts["act"](act, base, slot0, it))


def expert_parts(env):
    net, sb, s, need = env["net"], env["sb"], env["s"], env["need"]
    nc, ps, w, xT, y, y_stored = net.nc, env["ps"], env["w"], env["xT"], env["y"], env["y_stored"]
    C = FF // 128
    hid = sb("hid", [128, L, C, 128])

    def pe(eng, base, slot0):
        mm = nc.tensor.matmul
        for l in range(L):
            need(eng, base, l, "xT")
            for c in range(C):
                ins = mm(ps[l][:, 1, 128 * c:128 * c + 128], w[:, slot0 + l, 128 * c:128 * c + 128], xT[:, l], start=True, stop=True)
            ins.then_inc(s("up_done"), 1)
        for l in range(L):
            need(eng, base, l, "hid")
            for c in range(C):
                ins = mm(ps[l][:, 2, :D], hid[:, l, c], w[:, slot0 + l, FF + 128 * c:FF + 128 * c + 128], start=(c == 0), stop=(c == C - 1))
            ins.then_inc(s("down_done"), 1)

    def act(eng, base, slot0, it):
        for l in range(L):
            need(eng, base, l, "up_done")
            for c in range(C):
                ins = nc.scalar.activation(hid[:, l, c], ps[l][:, 1, 128 * c:128 * c + 128], ACT.Gelu_apprx_tanh,
                                           bias=w[:, slot0 + l, 2 * FF + c:2 * FF + c + 1])
            ins.then_inc(s("hid"), 1)

    def dve(eng, base, slot0, it):
        for l in range(L):
            eng.wait_ge(y_stored[slot0 + l], 16 * it + 16)
            need(eng, base, l, "down_done")
            nc.vector.tensor_tensor(y[:, slot0 + l], ps[l][:, 2, :D], w[:, slot0 + l, 2 * FF + C:], ALU.add).then_inc(s("y_ready"), 1)

    return {"pe": pe, "act": act, "dve": dve}


def experts(net):
    sorted_blocks(net, "f0", NB0, W0C, expert_parts)


def spline_tiles(net):
    nc, io, sem = net.nc, net.io, net.sem
    GB, SLOTS, NG = 4, 4, NB1 // 4
    W = GB * 128
    ACT_BLOCKS = 2
    BASE, SLOPE = 2 * 128, 2 * 128 + GRID
    with ExitStack() as ctx:
        def sb(name, shape, dt=F32):
            return net.sb(ctx, "f1_" + name, shape, dt)

        def s(name):
            return sem("f1_" + name)

        ps = [[ctx.enter_context(nc.psum_tensor(f"f1_{name}{q}", [128, GB, 128], F32)) for q in range(2)]
              for name in ("xT_ps", "h_ps", "y_ps")]
        xT_ps, h_ps, y_ps = ps
        eb = sb("eb", [1, 256], I32)
        ident = sb("ident", [128, 128])
        gidx = sb("gidx", [DH, GRID])
        x = sb("x", [128, SLOTS, GB, D])
        w = sb("w", [128, SLOTS, GB, W1C])
        xT = sb("xT", [D, 2, GB, 128])
        hn = sb("hn", [DH, 2, GB, 128])
        slope = sb("slope", [DH, 2, GB, GRID])
        shift = sb("shift", [DH, 2, GB, GRID])
        pieces = sb("pieces", [DH, 2, GRID, GB, 128])
        mask = sb("mask", [DH, 2, GRID - 1, GB, 128], U8)
        y = sb("y", [128, 2, GB, D])
        sixteen = sb("sixteen", [DH, GRID])
        loaded = [s(f"loaded_{i}") for i in range(SLOTS)]
        y_stored = [s(f"y_stored_{q}") for q in range(2)]

        def groups(eng, body, last=None):
            body(0, 0)
            body(1, 1)
            with eng.Fori(0, (NG - 2) // SLOTS) as it:
                for j in range(SLOTS):
                    body(SLOTS * it + (j + 2), (j + 2) % SLOTS, it)
            if last:
                last(NG - 1)

        def times(i, j, it, n):
            return 16 * n if it is None else 16 * n * it + 16 * n * (1 + (j < 2))

        block = ctx.enter_context(nc.Block())

        @block.sync
        def _(sp):
            sp.dma_start(ident[:], io["ident"]).then_inc(s("consts_loaded"), 16)
            sp.dma_start(gidx[:], io["gidx"]).then_inc(s("consts_loaded"), 16)
            sp.dma_start(eb[:], io["eb"].rearrange("p g -> (p g)").unsqueeze(0)).then_inc(s("eb_loaded"), 16)
            sp.wait_ge(s("eb_loaded"), 16)

            def load(i, j):
                for b in range(GB):
                    e = sp.value_load(eb[0:1, bass.ds(GB * i + b, 1)], min_val=0, max_val=T1 - 1)
                    sp.dma_start(w[:, j, b], io["f1_w"][bass.ds(e, 1)].rearrange("o p n -> (o p) n")).then_inc(loaded[j], 16)
                sp.dma_start(x[:, j], io["sorted1"].rearrange("(i b p) d -> i p b d", b=GB, p=128)[bass.ds(i, 1)].rearrange(
                    "o p b d -> p (o b) d")).then_inc(loaded[j], 16)

            def store(i, q):
                sp.wait_ge(s("y_ready"), i + 1)
                sp.dma_start(io["y1"].rearrange("(i b p) d -> i p b d", b=GB, p=128)[bass.ds(i, 1)].rearrange(
                    "o p b d -> p (o b) d"), y[:, q]).then_inc(y_stored[q], 16)

            for q in range(2):
                sp.sem_inc(y_stored[q], 16)
            for i in range(SLOTS):
                load(i, i)
            with sp.Fori(0, (NG - 2 - SLOTS) // SLOTS) as it:
                for j in range(SLOTS):
                    store(SLOTS * it + j, j % 2)
                    load(SLOTS * it + j + SLOTS, j)
            done = NG - 2 - SLOTS
            for i in range(done, NG):
                store(i, i % 2)
                if i + SLOTS < NG:
                    load(i + SLOTS, i % SLOTS)
            for q in range(2):
                sp.wait_ge(y_stored[q], 16 * NG // 2 + 16)

        def make_pieces(op, eng, i, q, blocks, done):
            for b in blocks:
                for g in range(GRID):
                    ins = op(pieces[:, q, g, b], hn[:, q, b], slope[:, q, b, g:g + 1], shift[:, q, b, g:g + 1])
            ins.then_inc(s(done), 1)

        @block.gpsimd
        def _(pool):
            gp = nc.gpsimd
            pool.wait_ge(s("consts_loaded"), 32)

            def body(i, j, it=None):
                q = j % 2
                pool.wait_ge(loaded[j], times(i, j, it, GB + 1))
                if it is not None:
                    pool.wait_ge(s("act_pieces"), i - 1)
                    pool.wait_ge(s("picked"), i - 1)
                gp.tensor_tensor(shift[:, q], w[:, j, :, SLOPE:SLOPE + GRID], gidx[:].unsqueeze(1).broadcast_to([DH, GB, GRID]), ALU.mult).then_inc(s("gslope"), 1)
                gp.tensor_tensor(slope[:, q], w[:, j, :, SLOPE:SLOPE + GRID], sixteen[:].unsqueeze(1).broadcast_to([DH, GB, GRID]), ALU.mult)
                pool.wait_ge(s("gslope"), i + 1)
                gp.tensor_tensor(shift[:, q], w[:, j, :, BASE:BASE + GRID], shift[:, q], ALU.subtract).then_inc(s("tables"), 1)
                pool.wait_ge(s("tables"), i + 1)
                pool.wait_ge(s("hn"), i + 1)
                pool.sem_inc(s("settled"), 1)
                make_pieces(lambda dst, src, a, b: gp.tensor_scalar(dst, src, a, b, ALU.mult, ALU.add), pool, i, q, range(ACT_BLOCKS, GB), "pool_pieces")

            gp.memset(sixteen[:], float(GRID)).then_inc(s("sixteen"), 1)
            pool.wait_ge(s("sixteen"), 1)
            groups(pool, body)

        @block.scalar
        def _(act):
            a_ = nc.scalar.activation

            def body(i, j, it=None):
                q = j % 2
                act.wait_ge(s("x_transposed"), i + 1)
                a_(xT[:, q], xT_ps[q][:], ACT.Copy).then_inc(s("xT"), 1)
                act.wait_ge(s("h_done"), i + 1)
                if it is not None:
                    act.wait_ge(s("picked"), i - 1)
                    act.wait_ge(s("pool_pieces"), i - 1)
                a_(hn[:, q], h_ps[q][:], ACT.Sigmoid).then_inc(s("hn"), 1)
                act.wait_ge(s("hn"), i + 1)
                act.wait_ge(s("tables"), i + 1)
                make_pieces(lambda dst, src, a, b: a_(dst, src, ACT.Identity, scale=a, bias=b), act, i, q, range(ACT_BLOCKS), "act_pieces")

            groups(act, body)

        @block.tensor
        def _(pe):
            mm, tr = nc.tensor.matmul, nc.tensor.transpose
            pe.wait_ge(s("consts_loaded"), 32)

            def up(i, j):
                pe.wait_ge(s("picked"), i + 1)
                pe.sem_inc(s("settled_pe"), 1)
                for b in range(GB):
                    ins = mm(y_ps[j % 2][:, b], pieces[:, j % 2, 0, b], w[:, j, b, 128:256], start=True, stop=True)
                ins.then_inc(s("y_done"), 1)

            def body(i, j, it=None):
                q = j % 2
                pe.wait_ge(loaded[j], times(i, j, it, GB + 1))
                if it is not None:
                    pe.wait_ge(s("xT"), i - 1)
                    pe.wait_ge(s("hn"), i - 1)
                    pe.wait_ge(s("y_ready"), i - 1)
                for b in range(GB):
                    ins = tr(xT_ps[q][:, b], x[:, j, b], ident[:])
                ins.then_inc(s("x_transposed"), 1)
                pe.wait_ge(s("xT"), i + 1)
                for b in range(GB):
                    ins = mm(h_ps[q][:, b], w[:, j, b, :128], xT[:, q, b], start=True, stop=True)
                ins.then_inc(s("h_done"), 1)
                if not (it is None and i == 0):
                    up(i - 1, (j - 1) % SLOTS)

            groups(pe, body, lambda i: up(i, i % SLOTS))

        @block.vector
        def _(dve):
            v_ = nc.vector

            def finish(i, j):
                q = j % 2
                dve.wait_ge(s("y_done"), i + 1)
                v_.tensor_tensor(y[:, q], y_ps[q][:], w[:, j, :, W1C - 1:W1C].broadcast_to([128, GB, D]), ALU.mult).then_inc(s("y_ready"), 1)

            def body(i, j, it=None):
                q = j % 2

                def compare(g):
                    v_.tensor_scalar(mask[:, q, g - 1], hn[:, q], g / GRID, None, ALU.is_ge).then_inc(s("masked"), 1)

                dve.wait_ge(s("hn"), i + 1)
                compare(1)
                compare(2)
                if not (it is None and i == 0):
                    if it is not None:
                        dve.wait_ge(y_stored[(j - 1) % 2], 8 * SLOTS * it + 16 * (((j + 2) % SLOTS + 1) // 2 + 1))
                    finish(i - 1, (j - 1) % SLOTS)
                dve.wait_ge(s("act_pieces"), i + 1)
                dve.wait_ge(s("pool_pieces"), i + 1)
                for g in range(1, GRID):
                    dve.wait_ge(s("masked"), (GRID - 1) * i + g)
                    if g > 1:
                        dve.wait_ge(s("picks"), (GRID - 1) * i + g - 1)
                    dve.sem_inc(s("settled_dve"), 1)
                    ins = v_.copy_predicated(pieces[:, q, 0], mask[:, q, g - 1], pieces[:, q, g])
                    ins.then_inc(s("picks"), 1)
                    if g + 2 < GRID:
                        compare(g + 2)
                dve.wait_ge(s("picks"), (GRID - 1) * i + (GRID - 1))
                dve.sem_inc(s("picked"), 1)

            def last(i):
                dve.wait_ge(y_stored[i % 2], 16 * (NG // 2))
                finish(i, i % SLOTS)

            groups(dve, body, last)


def layer1(net):
    nc, io, sem = net.nc, net.io, net.sem
    EX = 2 * D
    with ExitStack() as ctx:
        ps = net.psum(ctx, "l1")
        def sb(name, shape, dt=F32):
            return net.sb(ctx, "l1_" + name, shape, dt)

        def s(name):
            return sem("l1_" + name)

        consts = {}
        for name in L1_CONSTS:
            src = io["c2_" + name]
            consts[name] = sb("c_" + name, list(src.shape), src.dtype)
        ident = consts["ident"]
        rows = sb("rows", [128, 2, TH])
        slot_i = sb("slot_i", [TH, 128], I32)
        gate = sb("gate", [TH, 128])
        cols = sb("cols", [TH, L, 2], I32)
        gcols = sb("gcols", [TH, L, 2])
        neg_half = sb("neg_half", [TH, 2])
        h1 = sb("h1", [TH, L, 2, D])
        y = sb("y", [TH, L, 2, D])
        h2 = sb("h2", [TH, L, 2, D])
        stats = sb("stats", [TH, L, 2, 6])
        mv = sb("mv", [TH, L, 2, 2])
        rstd = sb("rstd", [TH, L, 2])
        x = sb("x", [TH, L, 2, D])
        junk = sb("junk", [TH, L, 2, D])
        ms = sb("ms", [TH, L, 2])
        rms = sb("rms", [TH, L, 2])
        hb = sb("hb", [TH, L, 2, D])
        xr = sb("xr", [TH, L, 2, D])
        xrT = sb("xrT", [D, L, T])
        uT = sb("uT", [D, L, 2, T])
        bT = sb("bT", [D, L, T])
        qT, kT = sb("qT", [D, L, T]), sb("kT", [D, L, T])
        vb = sb("vb", [TH, L, 2, EX])
        v = sb("v", [TH, L, 2, EX])
        r1, r2 = sb("r1", [TH, L, 2, T]), sb("r2", [TH, L, 2, T])
        rot = sb("rot", [TH, L, 2, T])
        kern = sb("kern", [TH, L, 2, T])
        uo = sb("uo", [D, L, 2, T])
        h3 = sb("h3", [TH, L, 2, D])
        x2 = sb("x2", [TH, L, 2, D])
        r3 = sb("r3", [TH, L, 2, D])
        xf = sb("xf", [TH, L, 2, D])
        loaded = [s(f"h1_loaded_{l}") for l in range(L)]
        gathered = [s(f"gathered_{l}") for l in range(L)]
        r3_stored = [s(f"r3_stored_{l}") for l in range(L)]
        xf_stored = [s(f"xf_stored_{l}") for l in range(L)]
        STEPS = B // L
        nconst = 16 * len(L1_CONSTS)

        def need(eng, it, l, *names):
            for n in names:
                eng.wait_ge(s(n), L * it + l + 1)

        def settle(eng):
            eng.sem_inc(s("settled"), 1)

        block = ctx.enter_context(nc.Block())

        @block.sync
        def _(sp):
            for name in L1_CONSTS:
                sp.dma_start(consts[name][:], io["c2_" + name]).then_inc(s("consts_loaded"), 16)
            sp.dma_start(rows[:], io["slot_gate"].rearrange("g (r p) -> r g p", p=TH)).then_inc(s("rows_loaded"), 16)
            for l in range(L):
                sp.sem_inc(r3_stored[l], 16)
                sp.sem_inc(xf_stored[l], 16)

            def image(it, l):
                return bass.ds(L * it + l, 1)

            def load(it, l):
                sp.dma_start(h1[:, l], halves(io["h1"][image(it, l)])).then_inc(loaded[l], 16)

            def store(it, l, name, ready, tile, stored):
                need(sp, it, l, ready)
                sp.dma_start(halves(io[name][image(it, l)]), tile[:, l]).then_inc(stored[l], 16)

            for l in range(L):
                load(0, l)
            with sp.Fori(0, STEPS - 1) as it:
                for l in range(L):
                    need(sp, it, l, "h2")
                    load(it + 1, l)
                for l in range(L):
                    store(it, l, "r3", "r3", r3, r3_stored)
                for l in range(L):
                    store(it, l, "xf", "xf", xf, xf_stored)
            for l in range(L):
                store(STEPS - 1, l, "r3", "r3", r3, r3_stored)
                store(STEPS - 1, l, "xf", "xf", xf, xf_stored)
            for l in range(L):
                sp.wait_ge(r3_stored[l], 16 * STEPS + 16)
                sp.wait_ge(xf_stored[l], 16 * STEPS + 16)

        @block.gpsimd
        def _(pool):
            gp = nc.gpsimd
            gp.memset(neg_half[:], -0.5).then_inc(s("neg_half_ready"), 1)
            pool.wait_ge(s("neg_half_ready"), 1)
            pool.wait_ge(s("slot_i"), 1)
            pool.wait_ge(s("gate"), 1)

            def gather(it, l):
                pair = bass.ds(2 * (L * it + l), 2)
                gp.tensor_copy(cols[:, l], slot_i[:, pair]).then_inc(s("cols"), 1)
                gp.tensor_copy(gcols[:, l], gate[:, pair]).then_inc(s("gcols"), 1)
                need(pool, it, l, "cols")
                settle(pool)
                for u in range(2):
                    gp.indirect_dma_start(y[:, l, u], None, io["y0"], bass.IndirectOffsetOnAxis(cols[:, l, u:u + 1], 0)).then_inc(gathered[l], 16)

            def power(it, l, src, dst, before, after, eps):
                need(pool, it, l, before)
                settle(pool)
                gp.tensor_scalar(dst, src, 1.0, eps, ALU.mult, ALU.add).then_inc(s(after + "_sum"), 1)
                need(pool, it, l, after + "_sum")
                gp.tensor_tensor(dst, dst, neg_half[:], ALU.pow).then_inc(s(after), 1)

            def steps(it, last):
                for l in range(L):
                    power(it, l, mv[:, l, :, 1], rstd[:, l], "ln_a", "rstd_a", EPS_LN)
                for l in range(L):
                    power(it, l, ms[:, l], rms[:, l], "ms", "rms", EPS_RMS)
                if not last:
                    for l in range(L):
                        gather(it + 1, l)
                for l in range(L):
                    need(pool, it, l, "x")
                    gp.tensor_tensor(hb[:, l], h2[:, l], x[:, l], ALU.add).then_inc(s("hx"), 1)
                for l in range(L):
                    need(pool, it, l, "hx")
                    gp.tensor_tensor(hb[:, l], hb[:, l], consts["b2"][:], ALU.add).then_inc(s("hb"), 1)
                for l in range(L):
                    power(it, l, mv[:, l, :, 1], rstd[:, l], "ln_b", "rstd_b", EPS_LN)
                for l in range(L):
                    need(pool, it, l, "x2")
                    pool.wait_ge(r3_stored[l], 16 * it + 16)
                    gp.tensor_tensor(r3[:, l], h3[:, l], x2[:, l], ALU.add).then_inc(s("r3"), 1)
                for l in range(L):
                    power(it, l, mv[:, l, :, 1], rstd[:, l], "ln_c", "rstd_c", EPS_LN)
                for l in range(L):
                    need(pool, it, l, "x3")
                    pool.wait_ge(xf_stored[l], 16 * it + 16)
                    gp.tensor_tensor(xf[:, l], x2[:, l], consts["gamma"][:], ALU.mult).then_inc(s("xg"), 1)
                for l in range(L):
                    need(pool, it, l, "xg")
                    gp.tensor_tensor(xf[:, l], xf[:, l], consts["beta"][:], ALU.add).then_inc(s("xf"), 1)

            for l in range(L):
                gather(0, l)
            with pool.Fori(0, STEPS - 1) as it:
                steps(it, False)
            steps(STEPS - 1, True)

        def layer_norm(dve, it, l, src, tag):
            for u in range(2):
                nc.vector.bn_stats(stats[:, l, u], src[:, l, u]).then_inc(s("bn_" + tag), 1)
            dve.wait_ge(s("bn_" + tag), 2 * L * it + 2 * (l + 1))
            settle(dve)
            for u in range(2):
                ins = nc.vector.bn_aggr(mv[:, l, u], stats[:, l, u])
            ins.then_inc(s("ln_" + tag), 1)

        def normalise(dve, it, l, src, dst, tag, done):
            need(dve, it, l, "ln_" + tag, "rstd_" + tag)
            for u in range(2):
                ins = nc.vector.tensor_scalar(dst[:, l, u], src[:, l, u], mv[:, l, u, 0:1], rstd[:, l, u:u + 1],
                                              ALU.subtract, ALU.mult)
            ins.then_inc(s(done), 1)

        @block.vector
        def _(dve):
            v_ = nc.vector
            dve.wait_ge(s("consts_loaded"), nconst)
            dve.wait_ge(s("rows_transposed"), 1)
            v_.tensor_copy(slot_i[:], ps[0][:TH, 0, :128]).then_inc(s("slot_i"), 1)
            v_.tensor_copy(gate[:], ps[0][:TH, 0, 128:256]).then_inc(s("gate"), 1)
            with dve.Fori(0, STEPS) as it:
                for l in range(L):
                    dve.wait_ge(loaded[l], 16 * it + 16)
                    dve.wait_ge(gathered[l], 32 * it + 32)
                    need(dve, it, l, "gcols")
                    for u in range(2):
                        ins = v_.scalar_tensor_tensor(h2[:, l, u], y[:, l, u], gcols[:, l, u:u + 1], h1[:, l, u], ALU.mult, ALU.add)
                    ins.then_inc(s("h2"), 1)
                    need(dve, it, l, "h2")
                    layer_norm(dve, it, l, h2, "a")
                for l in range(L):
                    normalise(dve, it, l, h2, x, "a", "x")
                for l in range(L):
                    need(dve, it, l, "rms", "x")
                    for u in range(2):
                        ins = v_.tensor_scalar(xr[:, l, u], x[:, l, u], rms[:, l, u:u + 1], consts["ns"][:], ALU.mult, ALU.mult)
                    ins.then_inc(s("xr"), 1)
                for l in range(L):
                    need(dve, it, l, "v_done")
                    v_.tensor_tensor(vb[:, l], ps[l][:TH, 1, :].rearrange("p (u e) -> p u e", u=2), consts["b1v"][:], ALU.add).then_inc(s("vb"), 1)
                for l in range(L):
                    need(dve, it, l, "bT")
                    for j, dst in ((0, qT), (1, kT)):
                        ins = v_.tensor_scalar(dst[:, l], bT[:, l], consts["gb"][:, 2 * j:2 * j + 1], consts["gb"][:, 2 * j + 1:2 * j + 2], ALU.mult, ALU.add)
                    ins.then_inc(s("qk"), 1)
                for l in range(L):
                    need(dve, it, l, "s_done")
                    src = ps[l][:TH, 2, :2 * T].rearrange("p (u n) -> p u n", u=2)
                    v_.tensor_tensor(r1[:, l], src, consts["cosT"][:].unsqueeze(1).broadcast_to([TH, 2, T]), ALU.mult)
                    v_.tensor_tensor(r2[:, l], src, consts["sinT"][:].unsqueeze(1).broadcast_to([TH, 2, T]), ALU.mult).then_inc(s("r12"), 1)
                    need(dve, it, l, "r12")
                    v_.tensor_tensor(rot[:, l, 0], r1[:, l, 0], r2[:, l, 1], ALU.subtract)
                    v_.tensor_tensor(rot[:, l, 1], r1[:, l, 1], r2[:, l, 0], ALU.add).then_inc(s("rot"), 1)
                    need(dve, it, l, "rot")
                    v_.scalar_tensor_tensor(kern[:, l], rot[:, l], 0.0, rot[:, l], ALU.max, ALU.mult).then_inc(s("kern"), 1)
                for l in range(L):
                    need(dve, it, l, "o_done", "uT")
                    v_.tensor_tensor(uo[:, l], ps[l][:, 3, :2 * T].rearrange("p (c n) -> p c n", c=2), uT[:, l], ALU.mult).then_inc(s("uo"), 1)
                for l in range(L):
                    need(dve, it, l, "out_done", "hb")
                    v_.tensor_tensor(h3[:, l], ps[l][:TH, 0, :2 * D].rearrange("p (u d) -> p u d", u=2), hb[:, l], ALU.add).then_inc(s("h3"), 1)
                    need(dve, it, l, "h3")
                    layer_norm(dve, it, l, h3, "b")
                for l in range(L):
                    normalise(dve, it, l, h3, x2, "b", "x2")
                    need(dve, it, l, "x2")
                    layer_norm(dve, it, l, x2, "c")
                for l in range(L):
                    need(dve, it, l, "r3")
                    normalise(dve, it, l, x2, x2, "c", "x3")

        @block.scalar
        def _(act):
            a_ = nc.scalar.activation
            act.wait_ge(s("consts_loaded"), nconst)
            with act.Fori(0, STEPS) as it:
                for l in range(L):
                    need(act, it, l, "x")
                    for u in range(2):
                        ins = a_(junk[:, l, u], x[:, l, u], ACT.Square, scale=D ** -0.5, accum_out=ms[:, l, u:u + 1])
                    ins.then_inc(s("ms"), 1)
                for l in range(L):
                    need(act, it, l, "xr_transposed")
                    a_(xrT[:, l], ps[l][:, 0, :T], ACT.Copy).then_inc(s("xrT"), 1)
                for l in range(L):
                    need(act, it, l, "ub_done")
                    a_(bT[:, l], ps[l][:, 3, 2 * T:3 * T], ACT.Silu, bias=consts["b1c"][:, 2:3]).then_inc(s("bT"), 1)
                    for c in range(2):
                        ins = a_(uT[:, l, c], ps[l][:, 3, T * c:T * c + T], ACT.Silu, bias=consts["b1c"][:, c:c + 1])
                    ins.then_inc(s("uT"), 1)
                for l in range(L):
                    need(act, it, l, "vb")
                    a_(v[:, l], vb[:, l], ACT.Silu).then_inc(s("v"), 1)

        @block.tensor
        def _(pe):
            mm, tr = nc.tensor.matmul, nc.tensor.transpose
            pe.wait_ge(s("consts_loaded"), nconst)
            pe.wait_ge(s("rows_loaded"), 16)
            for g in range(2):
                ins = tr(ps[0][:TH, 0, 128 * g:128 * g + 128], rows[:, g], ident[:])
            ins.then_inc(s("rows_transposed"), 1)
            pe.wait_ge(s("gate"), 1)
            with pe.Fori(0, STEPS) as it:
                for l in range(L):
                    need(pe, it, l, "xr")
                    for u in range(2):
                        ins = tr(ps[l][:, 0, TH * u:TH * u + TH], xr[:, l, u], ident[:TH, :TH])
                    ins.then_inc(s("xr_transposed"), 1)
                for l in range(L):
                    need(pe, it, l, "xrT")
                    for c in (2, 0, 1):
                        ins = mm(ps[l][:, 3, T * c:T * c + T], consts["w1"][:, (2 * EX if c == 2 else D * c):(2 * EX if c == 2 else D * c) + D], xrT[:, l], start=True, stop=True)
                    ins.then_inc(s("ub_done"), 1)
                    for u in range(2):
                        ins = mm(ps[l][:TH, 1, EX * u:EX * u + EX], xrT[:, l, TH * u:TH * u + TH], consts["w1"][:, EX:2 * EX], start=True, stop=True)
                    ins.then_inc(s("v_done"), 1)
                for l in range(L):
                    need(pe, it, l, "qk")
                    for u in range(2):
                        ins = mm(ps[l][:TH, 2, T * u:T * u + T], kT[:, l, TH * u:TH * u + TH], qT[:, l], start=True, stop=True)
                    ins.then_inc(s("s_done"), 1)
                for l in range(L):
                    need(pe, it, l, "kern", "v", "uT")
                    for c in range(2):
                        for u in range(2):
                            ins = mm(ps[l][:, 3, T * c:T * c + T], v[:, l, u, D * c:D * c + D], kern[:, l, u], start=(u == 0), stop=(u == 1))
                    ins.then_inc(s("o_done"), 1)
                for l in range(L):
                    need(pe, it, l, "uo")
                    for u in range(2):
                        for c in range(2):
                            ins = mm(ps[l][:TH, 0, D * u:D * u + D], uo[:, l, c, TH * u:TH * u + TH], consts["w2"][:, c], start=(c == 0), stop=(c == 1))
                    ins.then_inc(s("out_done"), 1)


def gather_out(net):
    nc, io, sem, slots = net.nc, net.io, net.sem, net.slots
    with ExitStack() as ctx:
        def s(name):
            return sem("g_" + name)

        cols = net.sb(ctx, "g_cols", [128, L], I32)
        y = net.sb(ctx, "g_y", [128, L, D])
        r3 = net.sb(ctx, "g_r3", [128, L, D])
        out = net.sb(ctx, "g_out", [128, L, D])
        gathered = [s(f"gathered_{l}") for l in range(L)]
        r3_loaded = [s(f"r3_loaded_{l}") for l in range(L)]
        stored = [s(f"out_stored_{l}") for l in range(L)]
        r3_rows = io["r3"].rearrange("b t d -> (b t) d")
        out_rows = io["out"].rearrange("b t d -> (b t) d")
        block = ctx.enter_context(nc.Block())

        def per_block(eng, body):
            with eng.Fori(0, NT // L) as it:
                body(L * it, range(L))
            body(NT - NT % L, range(NT % L))

        @block.sync
        def _(sp):
            def body(base, lanes):
                for l in lanes:
                    sp.wait_ge(s("sum"), base + (l + 1))
                    sp.dma_start(r3[:, l], block_rows(r3_rows, base + l)).then_inc(r3_loaded[l], 16)

            per_block(sp, body)

        @block.gpsimd
        def _(pool):
            def body(base, lanes):
                for l in lanes:
                    pool.wait_ge(s("sum"), base + (l + 1))
                    pool.sem_inc(s("settled"), 1)
                    nc.gpsimd.tensor_copy(cols[:, l:l + 1], slots[:, bass.ds(base + l, 1)]).then_inc(s("cols"), 1)
                for l in lanes:
                    pool.wait_ge(s("cols"), base + (l + 1))
                    pool.sem_inc(s("settled"), 1)
                    nc.gpsimd.indirect_dma_start(y[:, l], None, io["y1"], bass.IndirectOffsetOnAxis(cols[:, l:l + 1], 0)).then_inc(gathered[l], 16)

            per_block(pool, body)

        @block.vector
        def _(dve):
            dve.sem_inc(s("sum"), L)

            def body(base, lanes):
                for l in lanes:
                    dve.wait_ge(gathered[l], 8 * base + 16)
                    dve.wait_ge(r3_loaded[l], 8 * base + 16)
                    dve.wait_ge(stored[l], 8 * base + 16)
                    nc.vector.tensor_tensor(out[:, l], y[:, l], r3[:, l], ALU.add).then_inc(s("sum"), 1)

            per_block(dve, body)

        @block.scalar
        def _(act):
            for l in range(L):
                act.sem_inc(stored[l], 16)

            def body(base, lanes):
                for l in lanes:
                    act.wait_ge(s("sum"), base + (l + 1 + L))
                    act.dma_start(block_rows(out_rows, base + l), out[:, l]).then_inc(stored[l], 16)

            per_block(act, body)
            for l in range(L):
                act.wait_ge(stored[l], 16 * ((NT - l + L - 1) // L) + 16)


def host_arrays(inp):
    f = np.float32
    c = np.ascontiguousarray
    a = {}
    x = inp["x"].reshape(B // XG // 2, 2, XG, CH, 8, PATCH, 8, PATCH)
    x = x.transpose(0, 1, 3, 5, 7, 2, 4, 6).reshape(B // XG, 3, 7, KP, XG * PATCHES)
    a["x"] = c(x.transpose(0, 1, 3, 2, 4))
    a["tok_w"] = c(inp["L0_tok_W"].T.reshape(KC, KP, D).transpose(1, 0, 2))
    a["tok_b"] = c(inp["L0_tok_b"].reshape(D, 1))
    pos = inp["L0_tok_pos_embed"]
    a["tok_posT"] = c(pos[1:].T)
    a["tok_cls"] = c(np.broadcast_to(inp["L0_tok_class_token"], (B, D)))
    a["tok_pos0"] = c(np.broadcast_to(pos[:1], (B, D)))
    a["txt"] = c(inp["txt"])
    a["ident"] = np.eye(128, dtype=f)

    ang = np.outer(np.arange(T, dtype=f), 1.0 / 500000.0 ** (np.arange(0, DR, 2, dtype=f) / DR))
    emb = np.concatenate([ang, ang], -1).astype(f)
    cos, sin = np.cos(emb).astype(f), np.sin(emb).astype(f)
    sin = sin * np.where(np.arange(DR) < DR // 2, -1, 1).astype(f)
    rot = np.r_[DR // 2:DR, 0:DR // 2]
    one_head = lambda r, n: np.concatenate([n, r], 1).T
    p = {}
    p["ident"] = np.eye(128, dtype=f)
    p["identb"] = np.eye(128, dtype=f).astype(np.dtype("bfloat16"))
    row = np.arange(RW).reshape(NCH, CR).T[:, :, None]
    key = np.arange(T)[None, None]
    hidden = (key > row % T) & (row < G * T)
    p["maskb"] = np.where(hidden, NEG, 0.0).astype(f).astype(np.dtype("bfloat16"))
    p["cosq"] = np.tile(one_head(cos, np.ones((T, HD - DR), f)), (2, 1))
    p["sinq"] = np.tile(one_head(sin, np.zeros((T, HD - DR), f)), (2, 1))
    p["cosk"] = np.tile(cos.reshape(2, TH, DR).transpose(1, 0, 2), (1, 1, KVH))
    p["sink"] = np.tile(sin.reshape(2, TH, DR).transpose(1, 0, 2), (1, 1, KVH))
    g = lambda n: inp["L0_attn_" + n]
    kr = g("W_KR").reshape(D, KVH, DR)
    p["wlat"] = np.concatenate([g("W_DQ"), g("W_DKV"), kr.reshape(D, -1), kr[:, :, rot].reshape(D, -1)], 1)
    p["wkv"] = np.concatenate([g("W_UK"), g("W_UV")], 1)
    uq, qr = g("W_UQ").reshape(64, H, HD - DR), g("W_QR").reshape(64, H, DR)
    pack = lambda n, r: np.concatenate([n, r], 2).reshape(64, KVH, G, HD).transpose(0, 2, 1, 3).reshape(64, G, 128)
    p["wqa"] = pack(uq, qr)
    p["wqp"] = pack(uq, qr[:, :, rot])
    p["qln"] = g("q_ln_w").reshape(64, 1)
    p["kvln"] = g("kv_ln_w").reshape(D, 1)
    p["qhn"] = np.tile(g("q_head_norm_w"), 2).reshape(D, 1)
    p["khn"] = np.tile(g("k_head_norm_w"), 2).reshape(D, 1)
    p["half_sum"] = np.kron(np.eye(2, dtype=f), np.ones((64, 1), f))
    p["wo2"] = g("W_O").reshape(KVH, G, HD, D).transpose(0, 2, 1, 3).reshape(D, G, D)
    p["wvrT"] = g("W_VR").T.reshape(KVH, G, HD, D).transpose(0, 2, 1, 3).reshape(D, G, D)
    g = lambda n: inp["L0_ffn_" + n]
    rows = lambda w: np.broadcast_to(w, (TH, 2, D))
    p["wq"], p["wk"], p["wv"], p["wproj"] = g("Wq"), g("Wk"), g("Wv"), g("Wo")
    p["bq"], p["bk"] = g("bq").reshape(D, 1), g("bk").reshape(D, 1)
    p["bv"] = np.broadcast_to(g("bv")[:, None], (D, TH))
    for k, n in (("bo", "bo"), ("lng", "ln1_g"), ("lnb", "ln1_b")):
        p[k] = np.broadcast_to(g(n), (TH, D))
    p["hmask"] = np.kron(np.eye(H, dtype=f), np.ones((16, 1), f)) * f(0.25)
    a.update({"c0_" + k: c(p[k]) for k in L0_CONSTS})

    bf = np.dtype("bfloat16")
    for tag, ne in (("cr0_", E0), ("cr1_", T1)):
        a[tag + "ident"] = np.eye(128, dtype=f)
        a[tag + "upper"] = np.triu(np.ones((128, 128), f), 1).astype(bf)
        a[tag + "onesb"] = np.ones((128, 128), bf)
        k, e = np.arange(ne)[:, None], np.arange(ne)[None]
        a[tag + "scan"] = np.concatenate([(k <= e) * 1.0, (k < e) * 128.0], 1).astype(bf)
        a[tag + "jcol"] = (2 * np.arange(128)[:, None] + np.arange(2)[None]).astype(f)
    a["cr0_gw"] = c(g("gate_W"))
    a["cr0_gb"] = c(np.broadcast_to(g("gate_b"), (128, E0)))
    a["cr0_order"] = c(np.broadcast_to(np.arange(E0, 0, -1, dtype=f), (128, E0)))
    a["cr1_order"] = c(np.broadcast_to(np.concatenate([np.arange(CL - 1, -1, -1), np.arange(T1 - 1, -1, -1)]).astype(f), (128, CL + T1)))

    a["f0_w"] = np.concatenate([
        g("W1"), g("W2").reshape(E0, FF // 128, 128, D).transpose(0, 2, 1, 3).reshape(E0, 128, FF),
        g("b1").reshape(E0, FF // 128, 128).transpose(0, 2, 1), np.broadcast_to(g("b2")[:, None], (E0, 128, D))], 2)

    g = lambda n: inp["L1_attn_" + n]
    p = {"ident": np.eye(128, dtype=f)}
    half = T // 2
    inv = (f(10000.0) ** (-np.arange(half, dtype=f) / f(half))).astype(f)
    ang = np.arange(T, dtype=f)[None] * inv[:, None]
    p["cosT"], p["sinT"] = np.cos(ang).astype(f) / 128, np.sin(ang).astype(f) / 128
    p["w1"] = g("W1")
    b1 = g("b1")
    p["b1c"] = np.stack([b1[:D], b1[D:2 * D], b1[4 * D:]], 1)
    p["b1v"] = np.broadcast_to(b1[2 * D:4 * D], (TH, 2, 2 * D))
    p["gb"] = np.stack([g("gamma")[0], g("beta")[0], g("gamma")[1], g("beta")[1]], 1)
    p["w2"] = g("W2").reshape(2, D, D).transpose(1, 0, 2)
    p["b2"] = rows(g("b2"))
    p["ns"] = np.broadcast_to(g("norm_scale"), (TH, 1))
    g = lambda n: inp["L1_ffn_" + n]
    p["gamma"], p["beta"] = rows(g("gamma")), rows(g("beta"))
    a.update({"c2_" + k: c(p[k]) for k in L1_CONSTS})
    a["wdT"] = c(g("Wd").transpose(2, 0, 1))
    a["f1_w"] = np.concatenate([g("Wd").transpose(0, 2, 1), g("Wu").transpose(0, 2, 1), g("spline_bases"), g("spline_slopes"),
                                np.broadcast_to(g("scale")[:, None, None], (T1, 128, 1))], 2)
    a["gidx"] = c(np.broadcast_to(np.arange(GRID, dtype=f), (DH, GRID)))
    return a


SCRATCH = {"r3": (B, T, D), "xf": (B, T, D), "y0": (NB0 * 128, D), "y1": (NB1 * 128, D), "slot_gate": (2, N), "h1": (B, T, D), "t": (B, T, D), "h0": (B, T, D), "sorted0": (NB0 * 128, D), "sorted1": (NB1 * 128, D)}


def build(nc, arrays, phases, debug=False, given=()):
    io = {}
    for k, v in arrays.items():
        io[k] = nc.dram_tensor(f"in_{k}", v.shape, mybir.dt.from_np(v.dtype), kind="ExternalInput").ap()
    for k, shape in SCRATCH.items():
        io[k] = nc.dram_tensor(k, shape, F32, **({"kind": "ExternalInput" if k in given else "ExternalOutput"} if debug else {})).ap()
    io["eb"] = nc.dram_tensor("eb", (128, 2), I32, **({"kind": "ExternalOutput"} if debug else {})).ap()
    io["out"] = nc.dram_tensor("out_0", (B, T, D), F32, kind="ExternalOutput").ap()
    with ExitStack() as ctx:
        net = Net(nc, ctx, io)
        net.slots = net.sb(ctx, "slots", [128, NT], I32)
        for phase in phases:
            phase(net)
            net.end_phase()


PHASES = (patch_tokens, layer0, route_experts, experts, layer1, route_tiles, spline_tiles, gather_out)


def kernel(**inputs):
    from concourse import bacc
    from concourse.bass_utils import run_bass_kernel_spmd

    arrays = host_arrays({k: np.asarray(v) for k, v in inputs.items()})
    nc = bacc.Bacc("TRN2", target_bir_lowering=False, num_devices=1)
    build(nc, arrays, PHASES)
    r = run_bass_kernel_spmd(nc, [{f"in_{k}": v for k, v in arrays.items()}], core_ids=[0])
    return r.results[0]["out_0"]
```

```python
from contextlib import ExitStack

import numpy as np

import concourse.bass as bass
from concourse import mybir

F32 = mybir.dt.float32
BF16 = mybir.dt.bfloat16
I32 = mybir.dt.int32
U8 = mybir.dt.uint8
ALU = mybir.AluOpType
ACT = mybir.ActivationFunctionType
AX = mybir.AxisListType

B, T, D = 64, 142, 128
TH = T // 2
N = B * T
NT = N // 128
PATCHES, PATCH, CH = 64, 28, 3
KP = 112
KC = CH * PATCH * PATCH // KP
XG = 8
H, KVH, HD, DR = 8, 2, 64, 32
G = H // KVH
CR = 114
NCH = 5
RW = NCH * CR
E0, FF = 8, 512
T1, DH, GRID, CL = 64, 128, 16, 8
NB0 = -(-(NT + E0 - 1) // 8) * 8
NB1 = -(-(NT + T1 - 1) // 4) * 4
W0C = FF + FF + FF // 128 + D
W1C = 2 * 128 + 2 * GRID + 1
EPS_LN, EPS_RMS = 1e-5, 1e-6
RL = 4
EL = 4
SC = 8
GL = 8
LA = 4
L1N = 4
NEG = -1e30


L0_CONSTS = ("ident", "wlat", "qln", "kvln", "wkv", "cosk", "sink", "wqa", "wqp", "cosq", "sinq", "qhn", "khn",
             "half_sum", "identb", "maskb", "wvrT", "wo2", "wq", "wk", "wv", "bq", "bk", "bv", "bo", "hmask",
             "wproj", "lng", "lnb")


L1_CONSTS = ("ident", "w1", "b1c", "b1v", "gb", "cosT", "sinT", "w2", "b2", "ns", "gamma", "beta")


class Net:

    def __init__(self, nc, io):
        self.nc, self.io = nc, io
        self.sems = {}

    def sb(self, ctx, name, shape, dt=F32):
        return ctx.enter_context(self.nc.sbuf_tensor(name, shape, dt))

    def sem(self, name):
        if name not in self.sems:
            self.sems[name] = self.nc.alloc_semaphore(name=name)
        return self.sems[name]

    def end_phase(self):
        self.nc.all_engine_barrier()
        self.nc.clear_and_free_semaphores(list(self.sems.values()))
        self.nc.all_engine_barrier()
        self.sems = {}


FIRST, SECOND = (0, 1), (2, 3)


def in_turns(eng, steps, first, second):
    def merge(*programs):
        at = [[next(p), n, p] for n, p in enumerate(programs)]
        while at:
            now = min(at, key=lambda e: e[:2])
            now[0] = next(now[2], None)
            at = [e for e in at if e[0] is not None]

    def step(it):
        merge(second(it - 1, SECOND), first(it, FIRST))
        merge(second(it, FIRST), first(it, SECOND))

    merge(first(0, FIRST))
    merge(second(0, FIRST), first(0, SECOND))
    with eng.Fori(1, steps - 1) as it:
        step(it)
    step(steps - 1)
    merge(second(steps - 1, SECOND))


def idle(it, lanes):
    yield 0


def halves(ap):
    return ap.rearrange("o (u p) d -> p (o u) d", u=2)


def patch_tokens(net):
    nc, io, sem = net.nc, net.io, net.sem
    with ExitStack() as ctx:
        ps = [ctx.enter_context(nc.psum_tensor(f"pt_ps{i}", [128, 4, 512], F32)) for i in range(2)]
        wt = net.sb(ctx, "pt_w", [KP, KC, D])
        bcol = net.sb(ctx, "pt_b", [D, 1])
        posT = net.sb(ctx, "pt_posT", [D, PATCHES])
        cls = net.sb(ctx, "pt_cls", [B, 2, D])
        ident = net.sb(ctx, "pt_ident", [128, 128])
        x = net.sb(ctx, "pt_x", [KP, 2, 3, 7, 512])
        tokT = net.sb(ctx, "pt_tokT", [D, 2, 512])
        tok = net.sb(ctx, "pt_tok", [128, 2, 4, D])
        h0 = io["h0"]
        x_loaded = [[sem(f"pt_x_loaded_{g}{s}") for s in range(3)] for g in range(2)]
        consts_loaded, x_used = sem("pt_consts_loaded"), sem("pt_x_used")
        tokT_ready = sem("pt_tokT_ready")
        transposed, tok_ready = sem("pt_transposed"), sem("pt_tok_ready")
        tok_stored = [sem("pt_tok_stored_0"), sem("pt_tok_stored_1")]
        cls_ready, rows_stored = sem("pt_cls_ready"), sem("pt_rows_stored")
        zero_ready = sem("pt_zero_ready")
        zeros = net.sb(ctx, "pt_zeros", [128, 2048])
        block = ctx.enter_context(nc.Block())

        @block.sync
        def _(sp):
            sp.dma_start(wt[:], io["tok_w"]).then_inc(consts_loaded, 16)
            for g in range(2):
                for s in range(3):
                    sp.dma_start(x[:, g, s], io["x"][g, s]).then_inc(x_loaded[g][s], 16)
            with sp.Fori(1, B // XG // 2) as it:
                for g in range(2):
                    for s in range(3):
                        sp.wait_ge(x_used, 6 * it + (3 * g + s + 1 - 6))
                        sp.dma_start(x[:, g, s], io["x"][bass.ds(2 * it + g, 1), s].rearrange(
                            "o p k n -> (o p) k n")).then_inc(x_loaded[g][s], 16)

        @block.gpsimd
        def _(pool):
            nc.gpsimd.memset(zeros[:], 0.0).then_inc(zero_ready, 1)

        @block.scalar
        def _(act):
            for dst, src in ((bcol[:], io["tok_b"]), (posT[:], io["tok_posT"]), (cls[:, 0], io["tok_cls"]),
                             (cls[:, 1], io["tok_pos0"]), (ident[:], io["ident"])):
                act.dma_start(dst, src).then_inc(consts_loaded, 16)
            act.dma_start(h0[:, 1 + PATCHES:, :], io["txt"]).then_inc(rows_stored, 16)
            act.wait_ge(cls_ready, 1)
            act.dma_start(h0[:, 0, :], cls[:, 0]).then_inc(rows_stored, 16)
            act.wait_ge(zero_ready, 1)
            nz = 0
            for name in ("sorted0", "sorted1"):
                flat = io[name].rearrange("(p r) d -> p (r d)", p=128)
                for c in range(0, flat.shape[1], 2048):
                    w = min(2048, flat.shape[1] - c)
                    act.dma_start(flat[:, c:c + w], zeros[:, :w]).then_inc(rows_stored, 16)
                    nz += 1
            act.sem_inc(tok_ready, 2)
            with act.Fori(0, B // XG // 2) as it:
                for g in range(2):
                    act.wait_ge(transposed, 2 * it + g + 1)
                    nc.scalar.activation(tok[:, g], ps[1][:, 2 + g, :].rearrange("p (a d) -> p a d", a=4),
                                         ACT.Copy).then_inc(tok_ready, 1)
                    act.wait_ge(tok_ready, 2 * it + g + 3)
                    for i in range(2):
                        dst = h0[bass.ds(16 * it + 8 * g, 8), 1:1 + PATCHES, :].rearrange(
                            "(a i) p d -> i p a d", i=2)
                        act.dma_start(dst[i], tok[64 * i:64 * i + 64, g]).then_inc(tok_stored[g], 16)
                for g in range(2):
                    act.wait_ge(tok_stored[g], 32 * it + 32)
            act.wait_ge(rows_stored, 16 * (2 + nz))

        @block.vector
        def _(dve):
            dve.wait_ge(consts_loaded, 96)
            nc.vector.tensor_tensor(cls[:, 0], cls[:, 0], cls[:, 1], ALU.mult).then_inc(cls_ready, 1)
            with dve.Fori(0, B // XG // 2) as it:
                for g in range(2):
                    dve.wait_ge(x_used, 6 * it + 3 * g + 3)
                    nc.vector.scalar_tensor_tensor(
                        tokT[:, g].rearrange("p (b n) -> p b n", b=XG), ps[0][:, g, :].rearrange("p (b n) -> p b n", b=XG),
                        bcol[:], posT[:].unsqueeze(1).broadcast_to([D, XG, PATCHES]), ALU.add, ALU.mult).then_inc(tokT_ready, 1)

        @block.tensor
        def _(pe):
            pe.wait_ge(consts_loaded, 96)
            with pe.Fori(0, B // XG // 2) as it:
                for g in range(2):
                    for s in range(3):
                        pe.wait_ge(x_loaded[g][s], 16 * it + 16)
                        for k in range(7):
                            mm = nc.tensor.matmul(ps[0][:, g, :], wt[:, 7 * s + k], x[:, g, s, k],
                                                  start=(s + k == 0), stop=(s == 2 and k == 6))
                        mm.then_inc(x_used, 1)
                    pe.wait_ge(tokT_ready, 2 * it + g + 1)
                    pe.wait_ge(tok_ready, 2 * it + g + 1)
                    for a in range(4):
                        mm = nc.tensor.transpose(ps[1][:, 2 + g, 128 * a:128 * a + 128], tokT[:, g, 128 * a:128 * a + 128], ident[:])
                    mm.then_inc(transposed, 1)



def layer0(net):
    nc, io, sem = net.nc, net.io, net.sem
    LL = LA
    with ExitStack() as ctx:
        def sb(name, shape, dt=F32):
            return net.sb(ctx, "l0_" + name, shape, dt)

        ps = [ctx.enter_context(nc.psum_tensor(f"l0_ps{l}", [128, 2, 512], F32)) for l in range(LL)]
        X, Y = 0, 1
        consts = {}
        for name in L0_CONSTS:
            src = io["c0_" + name]
            consts[name] = sb("c_" + name, list(src.shape), src.dtype)
        ident, identb, maskb = consts["ident"], consts["identb"], consts["maskb"]
        wvro = sb("wvro", [D, D])
        wqk = sb("wqk", [D, 1])
        bo2 = sb("bo2", [TH, D])
        h = sb("h", [TH, LL, 2, D])
        stats = sb("stats", [TH, LL, 2, 6])
        mv = sb("mv", [TH, LL, 2, 2])
        rstd = sb("rstd", [TH, LL, 2])
        xn = sb("xn", [TH, LL, 2, D])
        xT = sb("xT", [D, LL, T])
        cms = sb("cms", [TH, LL, 2, 2])
        crs = sb("crs", [TH, LL, 2, 2])
        cn = sb("cn", [TH, LL, 2, 192])
        cqT = sb("cqT", [64, LL, T])
        ckvT = sb("ckvT", [D, LL, T])
        kt = sb("kt", [TH, LL, 2, KVH, HD])
        kr2 = sb("kr2", [TH, LL, 2, KVH * DR])
        ksq = sb("ksq", [TH, LL, 4, HD])
        kss = sb("kss", [TH, LL, 4])
        krs = sb("krs", [TH, LL, 4])
        kT = sb("kT", [D, LL, T])
        v = sb("v", [TH, LL, 2, KVH * HD])
        q = sb("q", [D, LL, RW])
        q1 = sb("q1", [D, LL, 2 * T])
        qsq = sb("qsq", [D, LL, RW])
        rq = sb("rq", [CR, LL, NCH, KVH])
        nb = sb("nb", [CR, LL, KVH, NCH])
        P = sb("P", [CR, LL, NCH, T])
        PT = sb("PT", [TH, LL, 2, 2 * RW])
        h1 = sb("h1", [TH, LL, 2, D])
        xmb = sb("xmb", [TH, LL, 2, D])
        q2T = sb("q2T", [D, LL, T])
        qbd = sb("qbd", [D, LL, 2 * RW])
        k2T = sb("k2T", [D, LL, T])
        v2 = sb("v2", [TH, LL, 2, H, D + 16])
        rsum = sb("rsum", [CR, LL, 2, NCH])
        z = sb("z", [TH, LL, 2, D])
        t = sb("t", [TH, LL, 2, D])
        oT = qsq
        o2T = q2T
        neg_half = sb("neg_half", [CR, 10])

        h_loaded = [sem(f"l0_h_loaded_{l}") for l in range(LL)]
        h1_stored = [sem(f"l0_h1_stored_{l}") for l in range(LL)]
        t_stored = [sem(f"l0_t_stored_{l}") for l in range(LL)]
        consts_loaded = sem("l0_consts_loaded")

        def s(name):
            return sem("l0_" + name)

        block = ctx.enter_context(nc.Block())
        STEPS = B // LL
        PARTS = ((X, 0, 3), (Y, 3, 2))

        def need(eng, it, l, *names):
            for n in names:
                eng.wait_ge(s(n), LL * it + l + 1)

        def settle(eng):
            eng.sem_inc(s("settled"), 1)

        @block.sync
        def _(sp):
            for name in L0_CONSTS:
                sp.dma_start(consts[name][:], io["c0_" + name]).then_inc(consts_loaded, 16)
            for l in range(LL):
                sp.sem_inc(h1_stored[l], 16)
                sp.sem_inc(t_stored[l], 16)

            def image(it, l):
                return bass.ds(LL * it + l, 1)

            def load(it, l):
                sp.dma_start(h[:, l], halves(io["h0"][image(it, l)])).then_inc(h_loaded[l], 16)

            def store_h1(it, l):
                need(sp, it, l, "h1_ready")
                sp.dma_start(halves(io["h1"][image(it, l)]), h1[:, l]).then_inc(h1_stored[l], 16)

            def store_t(it, l):
                need(sp, it, l, "t_ready")
                sp.dma_start(halves(io["t"][image(it, l)]), t[:, l]).then_inc(t_stored[l], 16)

            def h1_then_t(it, lanes, loads):
                for l in lanes:
                    store_h1(it, l)
                    if loads:
                        load(it + 1, l)
                for l in lanes:
                    store_t(it, l)

            for l in range(LL):
                load(0, l)
            h1_then_t(0, FIRST, True)
            with sp.Fori(1, STEPS - 1) as it:
                h1_then_t(it - 1, SECOND, True)
                h1_then_t(it, FIRST, True)
            h1_then_t(STEPS - 2, SECOND, True)
            h1_then_t(STEPS - 1, FIRST, False)
            h1_then_t(STEPS - 1, SECOND, False)
            for l in range(LL):
                sp.wait_ge(h1_stored[l], 16 * STEPS + 16)
                sp.wait_ge(t_stored[l], 16 * STEPS + 16)

        @block.gpsimd
        def _(pool):
            gp = nc.gpsimd
            gp.memset(neg_half[:], -0.5).then_inc(s("neg_half_ready"), 1)
            gp.memset(q[:, :, G * T:], 0.0).then_inc(s("pad_ready"), 1)
            gp.memset(qsq[:, :, G * T:], 0.0).then_inc(s("pad_ready"), 1)
            gp.memset(qbd[:, :, H * T:], 0.0).then_inc(s("pad_ready"), 1)
            for l in range(LL):
                gp.memset(v2[:, l], 0.0).then_inc(s("pad_ready"), 1)
            pool.wait_ge(s("neg_half_ready"), 1)
            pool.wait_ge(consts_loaded, 16 * len(L0_CONSTS))
            pool.wait_ge(s("bo2_ready"), 1)

            def power(it, l, src, dst, n, before, after, scale, eps):
                rows = src.shape[0]
                need(pool, it, l, before)
                settle(pool)
                gp.tensor_scalar(dst, src, scale, eps, ALU.mult, ALU.add).then_inc(s(after + "_sum"), 1)
                need(pool, it, l, after + "_sum")
                gp.tensor_tensor(dst, dst, neg_half[:rows, :n], ALU.pow).then_inc(s(after), 1)

            def first(it, lanes):
                yield 1
                for l in lanes:
                    power(it, l, mv[:, l, :, 1], rstd[:, l], 2, "ln_a", "rstd_a", 1.0, EPS_LN)
                yield 7
                for l in lanes:
                    power(it, l, cms[:, l].rearrange("p a b -> p (a b)"), crs[:, l].rearrange("p a b -> p (a b)"), 4, "cms", "crs", 1.0, EPS_RMS)
                yield 16
                for l in lanes:
                    power(it, l, kss[:, l], krs[:, l], 4, "kss", "krs", 1.0 / HD, EPS_RMS)
                for a in range(2):
                    yield 21 + 3 * a
                    for l in lanes:
                        power(it, l, rq[:, l, :, a], rq[:, l, :, a], 5, "qss", f"rq_{a}", 1.0, HD * EPS_RMS)

            def second(it, lanes):
                yield 3
                for l in lanes:
                    power(it, l, mv[:, l, :, 1], rstd[:, l], 2, "ln_b", "rstd_b", 1.0, EPS_LN)
                yield 17
                for l in lanes:
                    need(pool, it, l, "q2T")
                    gp.tensor_tensor(qbd[:, l, :H * T].rearrange("p (h n) -> p h n", h=H),
                                     q2T[:, l].unsqueeze(1).broadcast_to([D, H, T]),
                                     consts["hmask"][:].unsqueeze(2).broadcast_to([D, H, T]), ALU.mult).then_inc(s("qbd"), 1)
                yield 13
                for l in lanes:
                    need(pool, it, l, "xn_b")
                    gp.tensor_tensor(xmb[:, l], xn[:, l], bo2[:].unsqueeze(1).broadcast_to([TH, 2, D]), ALU.add).then_inc(s("xmb"), 1)
                yield 43
                for l in lanes:
                    power(it, l, mv[:, l, :, 1], rstd[:, l], 2, "ln_c", "rstd_c", 1.0, EPS_LN)
                yield 45
                for l in lanes:
                    need(pool, it, l, "zn")
                    pool.wait_ge(t_stored[l], 16 * it + 16)
                    gp.tensor_tensor(t[:, l], z[:, l], consts["lng"][:].unsqueeze(1).broadcast_to([TH, 2, D]), ALU.mult).then_inc(s("t_scaled"), 1)
                yield 45
                for l in lanes:
                    need(pool, it, l, "t_scaled")
                    gp.tensor_tensor(t[:, l], t[:, l], consts["lnb"][:].unsqueeze(1).broadcast_to([TH, 2, D]), ALU.add).then_inc(s("t_ready"), 1)

            in_turns(pool, STEPS, first, second)

        def layer_norm(dve, it, l, src, tag):
            for u in range(2):
                nc.vector.bn_stats(stats[:, l, u], src[:, l, u]).then_inc(s("bn_" + tag), 1)
            dve.wait_ge(s("bn_" + tag), 2 * LL * it + 2 * (l + 1))
            settle(dve)
            for u in range(2):
                ins = nc.vector.bn_aggr(mv[:, l, u], stats[:, l, u])
            ins.then_inc(s("ln_" + tag), 1)

        def normalise(dve, it, l, src, dst, tag, done):
            need(dve, it, l, "ln_" + tag, "rstd_" + tag)
            for u in range(2):
                ins = nc.vector.tensor_scalar(dst[:, l, u], src[:, l, u], mv[:, l, u, 0:1], rstd[:, l, u:u + 1],
                                              ALU.subtract, ALU.mult)
            ins.then_inc(s(done), 1)

        def score_max(dve, it, l, tag, a):
            need(dve, it, l, f"s_done_{tag}{a}")
            for bank, c0, n in PARTS:
                ins = nc.vector.tensor_reduce(nb[:, l, a, c0:c0 + n], ps[l][:CR, bank, :n * T].rearrange("p (i k) -> p i k", k=T),
                                              AX.X, ALU.max, negate=True)
            ins.then_inc(s(f"max_{tag}{a}"), 1)

        def rows_over_sums(it, l, tag, a):
            need(nc.vector, it, l, f"exp_{tag}{a}")
            nc.vector.reciprocal(rsum[:, l, a], rsum[:, l, a]).then_inc(s(f"rsum_{tag}{a}"), 1)
            need(nc.vector, it, l, f"rsum_{tag}{a}")
            nc.vector.tensor_tensor(P[:, l], P[:, l], rsum[:, l, a].unsqueeze(2).broadcast_to([CR, NCH, T]), ALU.mult).then_inc(s(f"P_{tag}{a}"), 1)

        def keep_PT(op, eng, it, l, tag, a, khalf, *func):
            need(eng, it, l, f"pt_done_{tag}{a}{khalf}")
            for bank, c0, n in PARTS:
                ins = op(PT[:, l, khalf, RW * a + CR * c0:RW * a + CR * (c0 + n)], ps[l][:TH, bank, :CR * n], *func)
            ins.then_inc(s(f"PT_{tag}{a}{khalf}"), 1)

        @block.vector
        def _(dve):
            v_ = nc.vector
            dve.wait_ge(consts_loaded, 16 * len(L0_CONSTS))
            dve.wait_ge(s("setup_done"), 2)
            v_.tensor_copy(wvro[:], ps[0][:, X, :D])
            v_.tensor_tensor(bo2[:], ps[0][:TH, Y, :D], consts["bo"][:], ALU.add).then_inc(s("bo2_ready"), 1)
            v_.tensor_tensor(wqk[:], consts["qhn"][:], consts["khn"][:], ALU.mult).then_inc(s("wqk_ready"), 1)
            dve.wait_ge(s("pad_ready"), 3 + LL)
            def first(it, lanes):
                yield 0
                for l in lanes:
                    dve.wait_ge(h_loaded[l], 16 * it + 16)
                    layer_norm(dve, it, l, h, "a")
                yield 2
                for l in lanes:
                    normalise(dve, it, l, h, xn, "a", "xn_a")
                yield 7
                for l in lanes:
                    need(dve, it, l, "cms")
                    kr1 = kt[:, l, :, :, DR:]
                    v_.tensor_tensor(kr1, ps[l][:TH, :, 192:256].rearrange("p u (k d) -> p u k d", k=KVH),
                                     consts["cosk"][:].rearrange("p u (k d) -> p u k d", k=KVH), ALU.mult).then_inc(s("kr1"), 1)
                    v_.tensor_tensor(kr2[:, l], ps[l][:TH, :, 256:320], consts["sink"][:], ALU.mult).then_inc(s("kr2"), 1)
                    need(dve, it, l, "kr1", "kr2")
                    v_.tensor_tensor(kr1, kr1, kr2[:, l].rearrange("p u (k d) -> p u k d", k=KVH), ALU.add).then_inc(s("kr"), 1)
                yield 8
                for l in lanes:
                    need(dve, it, l, "crs")
                    v_.tensor_tensor(cn[:, l, :, :64], ps[l][:TH, :, :64], crs[:, l, :, 0:1].broadcast_to([TH, 2, 64]), ALU.mult)
                    v_.tensor_tensor(cn[:, l, :, 64:], ps[l][:TH, :, 64:192], crs[:, l, :, 1:2].broadcast_to([TH, 2, 128]), ALU.mult).then_inc(s("cn"), 1)
                yield 13
                for l in lanes:
                    need(dve, it, l, "kv_kept", "kr")
                    k4 = kt[:, l].rearrange("p u k d -> p (u k) d")
                    v_.tensor_tensor(ksq[:, l], k4, k4, ALU.mult).then_inc(s("ksq"), 1)
                yield 13
                for l in lanes:
                    need(dve, it, l, "ksq")
                    v_.tensor_reduce(kss[:, l], ksq[:, l], AX.X, ALU.add).then_inc(s("kss"), 1)
                for r in range(2):
                    yield 14 + 3 * r
                    for l in lanes:
                        need(dve, it, l, f"q_done_{r}")
                        cosq = consts["cosq"][:].unsqueeze(1).broadcast_to([D, 2, T])
                        sinq = consts["sinq"][:].unsqueeze(1).broadcast_to([D, 2, T])
                        qp = ps[l][:, Y, :2 * T].rearrange("p (c n) -> p c n", n=T)
                        q1v = q1[:, l].rearrange("p (c n) -> p c n", n=T)
                        v_.tensor_tensor(q1v, ps[l][:, X, :2 * T].rearrange("p (c n) -> p c n", n=T), cosq, ALU.mult).then_inc(s(f"q1_{r}"), 1)
                        v_.tensor_tensor(qp, qp, sinq, ALU.mult).then_inc(s(f"q2_{r}"), 1)
                        need(dve, it, l, f"q1_{r}", f"q2_{r}")
                        v_.tensor_tensor(q[:, l, 2 * T * r:2 * T * r + 2 * T], ps[l][:, Y, :2 * T], q1[:, l], ALU.add).then_inc(s(f"q_{r}"), 1)
                yield 18
                for l in lanes:
                    need(dve, it, l, "krs")
                    k4 = kt[:, l].rearrange("p u k d -> p (u k) d")
                    v_.tensor_tensor(k4, k4, krs[:, l].unsqueeze(2).broadcast_to([TH, 4, HD]), ALU.mult).then_inc(s("kn"), 1)
                yield 20
                for l in lanes:
                    need(dve, it, l, "qss_done")
                    v_.tensor_copy(rq[:, l].rearrange("p c k -> p (c k)"), ps[l][:CR, Y, :10]).then_inc(s("qss"), 1)
                for a in range(2):
                    yield 23 + 10 * a
                    for l in lanes:
                        score_max(dve, it, l, "a", a)
                        need(dve, it, l, f"max_a{a}", f"rq_{a}")
                        v_.tensor_tensor(nb[:, l, a], nb[:, l, a], rq[:, l, :, a], ALU.mult).then_inc(s(f"nb_a{a}"), 1)
                    yield 26 + 10 * a
                    for l in lanes:
                        rows_over_sums(it, l, "a", a)
                    yield 31 + 10 * a
                    for l in lanes:
                        keep_PT(v_.tensor_copy, dve, it, l, "a", a, 1)

            def second(it, lanes):
                yield 3
                for l in lanes:
                    need(dve, it, l, "out_done")
                    dve.wait_ge(h1_stored[l], 16 * it + 16)
                    v_.tensor_tensor(h1[:, l], ps[l][:TH, X, :2 * D].rearrange("p (u d) -> p u d", u=2), h[:, l], ALU.add).then_inc(s("h1_ready"), 1)
                    need(dve, it, l, "h1_ready")
                    layer_norm(dve, it, l, h1, "b")
                yield 7
                for l in lanes:
                    normalise(dve, it, l, h1, xn, "b", "xn_b")
                for a in range(2):
                    yield 20 + 8 * a
                    for l in lanes:
                        score_max(dve, it, l, "b", a)
                    yield 22 + 10 * a
                    for l in lanes:
                        rows_over_sums(it, l, "b", a)
                    yield 26 + 10 * a
                    for l in lanes:
                        keep_PT(v_.tensor_copy, dve, it, l, "b", a, 1)
                yield 42
                for l in lanes:
                    need(dve, it, l, "proj_done", "xmb")
                    v_.tensor_tensor(z[:, l], ps[l][:TH, X, :2 * D].rearrange("p (u d) -> p u d", u=2), xmb[:, l], ALU.add).then_inc(s("z"), 1)
                    need(dve, it, l, "z")
                    layer_norm(dve, it, l, z, "c")
                yield 44
                for l in lanes:
                    normalise(dve, it, l, z, z, "c", "zn")

            in_turns(dve, STEPS, first, second)

        @block.scalar
        def _(act):
            a_ = nc.scalar.activation
            act.wait_ge(consts_loaded, 16 * len(L0_CONSTS))
            act.wait_ge(s("pad_ready"), 3 + LL)
            act.wait_ge(s("wqk_ready"), 1)
            def first(it, lanes):
                yield 4
                for l in lanes:
                    need(act, it, l, "xt_done_a")
                    a_(xT[:, l], ps[l][:, X, :T], ACT.Copy).then_inc(s("xT_a"), 1)
                yield 6
                for l in lanes:
                    need(act, it, l, "lat_done")
                    for u in range(2):
                        for j, (c0, n) in enumerate(((0, 64), (64, 128))):
                            ins = a_(cn[:, l, u, c0:c0 + n], ps[l][:TH, u, c0:c0 + n], ACT.Square, scale=n ** -0.5,
                                     accum_out=cms[:, l, u, j:j + 1])
                    ins.then_inc(s("cms"), 1)
                yield 10
                for l in lanes:
                    need(act, it, l, "cT_done")
                    a_(cqT[:, l], ps[l][:64, X, :T], ACT.Copy, scale=consts["qln"][:])
                    a_(ckvT[:, l], ps[l][:, X, T:2 * T], ACT.Copy, scale=consts["kvln"][:]).then_inc(s("cT"), 1)
                yield 12
                for l in lanes:
                    need(act, it, l, "kv_done")
                    kv = ps[l][:TH, Y, :384].rearrange("p (u n) -> p u n", u=2)
                    a_(kt[:, l, :, :, :DR], kv[:, :, :64].rearrange("p u (k d) -> p u k d", k=KVH), ACT.Copy)
                    a_(v[:, l], kv[:, :, 64:], ACT.Copy).then_inc(s("kv_kept"), 1)
                for r in range(2):
                    yield 15 + 3 * r
                    for l in lanes:
                        need(act, it, l, f"q_{r}")
                        a_(qsq[:, l, 2 * T * r:2 * T * r + 2 * T], q[:, l, 2 * T * r:2 * T * r + 2 * T], ACT.Square).then_inc(s(f"qsq_{r}"), 1)
                yield 20
                for l in lanes:
                    need(act, it, l, "kT_done")
                    a_(kT[:, l], ps[l][:, X, :T], ACT.Copy, scale=wqk[:]).then_inc(s("kT"), 1)
                for a in range(2):
                    yield 25 + 10 * a
                    for l in lanes:
                        need(act, it, l, f"nb_a{a}")
                        for bank, c0, n in PARTS:
                            for i in range(n):
                                ins = a_(P[:, l, c0 + i], ps[l][:CR, bank, T * i:T * i + T], ACT.Exp,
                                         bias=nb[:, l, a, c0 + i:c0 + i + 1], scale=rq[:, l, c0 + i, a:a + 1],
                                         accum_out=rsum[:, l, a, c0 + i:c0 + i + 1])
                        ins.then_inc(s(f"exp_a{a}"), 1)
                    yield 29 + 10 * a
                    for l in lanes:
                        keep_PT(a_, act, it, l, "a", a, 0, ACT.Copy)

            def second(it, lanes):
                yield 2
                for l in lanes:
                    need(act, it, l, "o_done")
                    for r in range(2):
                        ins = a_(oT[:, l, 2 * T * r:2 * T * r + 2 * T], ps[l][:, r, :2 * T], ACT.Copy)
                    ins.then_inc(s("oT"), 1)
                yield 9
                for l in lanes:
                    need(act, it, l, "xt_done_b")
                    a_(xT[:, l], ps[l][:, Y, :T], ACT.Copy).then_inc(s("xT_b"), 1)
                yield 15
                for l in lanes:
                    need(act, it, l, "qk2_done")
                    a_(q2T[:, l], ps[l][:, X, :T], ACT.Identity, bias=consts["bq"][:]).then_inc(s("q2T"), 1)
                    a_(k2T[:, l], ps[l][:, X, T:2 * T], ACT.Identity, bias=consts["bk"][:]).then_inc(s("k2T"), 1)
                yield 15
                for l in lanes:
                    need(act, it, l, "v2_done")
                    a_(v2[:, l, :, :, :16], ps[l][:TH, Y, :2 * D].rearrange("p (u h e) -> p u h e", u=2, e=16), ACT.Copy).then_inc(s("v2"), 1)
                for a in range(2):
                    yield 21 + 10 * a
                    for l in lanes:
                        need(act, it, l, f"max_b{a}")
                        for bank, c0, n in PARTS:
                            for i in range(n):
                                ins = a_(P[:, l, c0 + i], ps[l][:CR, bank, T * i:T * i + T], ACT.Exp, bias=nb[:, l, a, c0 + i:c0 + i + 1],
                                         accum_out=rsum[:, l, a, c0 + i:c0 + i + 1])
                        ins.then_inc(s(f"exp_b{a}"), 1)
                    yield 24 + 10 * a
                    for l in lanes:
                        keep_PT(a_, act, it, l, "b", a, 0, ACT.Copy)
                yield 40
                for l in lanes:
                    need(act, it, l, "o2_done")
                    a_(o2T[:, l], ps[l][:, Y, :T], ACT.Copy).then_inc(s("o2T"), 1)

            in_turns(act, STEPS, first, second)

        @block.tensor
        def _(pe):
            mm, tr = nc.tensor.matmul, nc.tensor.transpose

            def scores(it, l, tag, a, keys, queries, masked):
                for bank, c0, n in PARTS:
                    for i in range(n):
                        ins = mm(ps[l][:CR, bank, T * i:T * i + T], queries(c0 + i), keys,
                                 start=(i == 0 or not masked), stop=not masked, skip_group_check=masked)
                if masked:
                    for bank, c0, n in PARTS:
                        ins = mm(ps[l][:CR, bank, :n * T], identb[:CR, :CR], maskb[:, c0:c0 + n], start=False, stop=True, skip_group_check=True)
                ins.then_inc(s(f"s_done_{tag}{a}"), 1)

            def transposes_P(it, l, tag, a, khalf):
                for bank, c0, n in PARTS:
                    for i in range(n):
                        ins = tr(ps[l][:TH, bank, CR * i:CR * i + CR], P[:, l, c0 + i, TH * khalf:TH * khalf + TH], ident[:CR, :CR])
                ins.then_inc(s(f"pt_done_{tag}{a}{khalf}"), 1)

            def attend(it, lanes, tag, turns, scores_of, before):
                for a in range(2):
                    yield turns[a][0]
                    for l in lanes:
                        need(pe, it, l, *(before if a == 0 else (f"PT_{tag}01",)))
                        settle(pe)
                        scores_of(l, a)
                    yield turns[a][1]
                    for l in lanes:
                        need(pe, it, l, f"P_{tag}{a}")
                        transposes_P(it, l, tag, a, 0)
                    yield turns[a][2]
                    for l in lanes:
                        need(pe, it, l, f"PT_{tag}{a}0")
                        transposes_P(it, l, tag, a, 1)

            pe.wait_ge(consts_loaded, 16 * len(L0_CONSTS))
            for c in range(4):
                ins = mm(ps[0][:, X, :D], consts["wvrT"][:, c], consts["wo2"][:, c], start=(c == 0), stop=(c == 3))
            ins.then_inc(s("setup_done"), 1)
            mm(ps[0][:TH, Y, :D], consts["bv"][:], consts["wproj"][:], start=True, stop=True).then_inc(s("setup_done"), 1)
            pe.wait_ge(s("bo2_ready"), 1)
            pe.wait_ge(s("pad_ready"), 3 + LL)
            def first(it, lanes):
                yield 3
                for l in lanes:
                    need(pe, it, l, "xn_a")
                    for u in range(2):
                        ins = tr(ps[l][:, X, TH * u:TH * u + TH], xn[:, l, u], ident[:TH, :TH])
                    ins.then_inc(s("xt_done_a"), 1)
                yield 5
                for l in lanes:
                    need(pe, it, l, "xT_a")
                    for u in range(2):
                        ins = mm(ps[l][:TH, u, :320], xT[:, l, TH * u:TH * u + TH], consts["wlat"][:], start=True, stop=True)
                    ins.then_inc(s("lat_done"), 1)
                yield 9
                for l in lanes:
                    need(pe, it, l, "cn", "kr")
                    settle(pe)
                    for u in range(2):
                        tr(ps[l][:64, X, TH * u:TH * u + TH], cn[:, l, u, :64], ident[:TH, :TH])
                        ins = tr(ps[l][:, X, T + TH * u:T + TH * u + TH], cn[:, l, u, 64:], ident[:TH, :TH])
                    ins.then_inc(s("cT_done"), 1)
                yield 11
                for l in lanes:
                    need(pe, it, l, "cT")
                    for u in range(2):
                        ins = mm(ps[l][:TH, Y, 192 * u:192 * u + 192], ckvT[:, l, TH * u:TH * u + TH], consts["wkv"][:], start=True, stop=True)
                    ins.then_inc(s("kv_done"), 1)
                for r in range(2):
                    yield 13 + 3 * r
                    for l in lanes:
                        need(pe, it, l, "kv_kept" if r == 0 else "q_0")
                        for w, bank in (("wqa", X), ("wqp", Y)):
                            for c in range(2):
                                ins = mm(ps[l][:, bank, T * c:T * c + T], consts[w][:, 2 * r + c], cqT[:, l], start=True, stop=True)
                        ins.then_inc(s(f"q_done_{r}"), 1)
                yield 19
                for l in lanes:
                    need(pe, it, l, "q_1", "kn")
                    for u in range(2):
                        ins = tr(ps[l][:, X, TH * u:TH * u + TH], kt[:, l, u].rearrange("p k d -> p (k d)"), ident[:TH, :TH])
                    ins.then_inc(s("kT_done"), 1)
                yield 19
                for l in lanes:
                    need(pe, it, l, "qsq_1")
                    settle(pe)
                    for i in range(NCH):
                        ins = mm(ps[l][:CR, Y, 2 * i:2 * i + 2], qsq[:, l, CR * i:CR * i + CR], consts["half_sum"][:], start=True, stop=True)
                    ins.then_inc(s("qss_done"), 1)
                yield from attend(it, lanes, "a", ((22, 28, 30), (32, 38, 40)), lambda l, a: scores(it, l, "a", a, kT[HD * a:HD * a + HD, l],
                                                    lambda i: q[HD * a:HD * a + HD, l, CR * i:CR * i + CR], True), ("kT", "qss"))

            def second(it, lanes):
                yield 0
                for l in lanes:
                    need(pe, it, l, "PT_a11")
                    for r in range(2):
                        for u in range(2):
                            for k in range(KVH):
                                def cut(columns):
                                    return columns if u == 0 else columns.rearrange("p (h u n) -> p h u n", h=2, u=2)[:, :, 1]

                                c = RW * k + 2 * T * r
                                ins = mm(cut(ps[l][HD * k:HD * k + HD, r, :2 * T]), v[:, l, u, HD * k:HD * k + HD], cut(PT[:, l, u, c:c + 2 * T]),
                                         start=(u == 0), stop=(u == 1), skip_group_check=True)
                    ins.then_inc(s("o_done"), 1)
                yield 3
                for l in lanes:
                    need(pe, it, l, "oT")
                    for u in range(2):
                        out = ps[l][:TH, X, D * u:D * u + D]
                        mm(out, xT[:, l, TH * u:TH * u + TH], wvro[:], start=True, stop=False)
                        for g in range(G):
                            ins = mm(out, oT[:, l, T * g + TH * u:T * g + TH * u + TH], consts["wo2"][:, g], start=False, stop=(g == G - 1))
                    ins.then_inc(s("out_done"), 1)
                yield 9
                for l in lanes:
                    need(pe, it, l, "xn_b")
                    for u in range(2):
                        ins = tr(ps[l][:, Y, TH * u:TH * u + TH], xn[:, l, u], ident[:TH, :TH])
                    ins.then_inc(s("xt_done_b"), 1)
                yield 14
                for l in lanes:
                    need(pe, it, l, "xT_b")
                    mm(ps[l][:, X, :T], consts["wq"][:], xT[:, l], start=True, stop=True)
                    mm(ps[l][:, X, T:2 * T], consts["wk"][:], xT[:, l], start=True, stop=True).then_inc(s("qk2_done"), 1)
                    for u in range(2):
                        ins = mm(ps[l][:TH, Y, D * u:D * u + D], xT[:, l, TH * u:TH * u + TH], consts["wv"][:], start=True, stop=True)
                    ins.then_inc(s("v2_done"), 1)
                yield from attend(it, lanes, "b", ((19, 23, 25), (27, 33, 35)), lambda l, a: scores(it, l, "b", a, k2T[:, l],
                                                    lambda i: qbd[:, l, RW * a + CR * i:RW * a + CR * i + CR], False), ("qbd", "k2T", "v2"))
                yield 38
                for l in lanes:
                    need(pe, it, l, "PT_b11")
                    for odd in range(2):
                        for u in range(2):
                            for j in range(4):
                                hh = 2 * j + odd
                                wide = v2[:, l, u].rearrange("p h e -> p (h e)")
                                ins = mm(ps[l][32 * j:32 * j + 32, Y, :T], wide[:, D * hh + 32 * j:D * hh + 32 * j + 32], PT[:, l, u, T * hh:T * hh + T],
                                         start=(odd + u == 0), stop=(odd + u == 2), skip_group_check=True)
                    ins.then_inc(s("o2_done"), 1)
                yield 41
                for l in lanes:
                    need(pe, it, l, "o2T")
                    for u in range(2):
                        ins = mm(ps[l][:TH, X, D * u:D * u + D], o2T[:, l, TH * u:TH * u + TH], consts["wproj"][:], start=True, stop=True)
                    ins.then_inc(s("proj_done"), 1)

            in_turns(pe, STEPS, first, second)


def block_rows(ap, j):
    return ap.rearrange("(j p) d -> j p d", p=128)[bass.ds(j, 1)].rearrange("o p d -> (o p) d")


def route(net, tag, ne, nb, source, score_consts, score_stage, wide_gate):
    nc, io, sem = net.nc, net.io, net.sem
    with ExitStack() as ctx:
        ps = [ctx.enter_context(nc.psum_tensor(f"{tag}_ps{l}", [128, 2, 512], F32)) for l in range(RL)]
        def sb(name, shape, dt=F32):
            return net.sb(ctx, f"{tag}_" + name, shape, dt)

        def s(name):
            return sem(f"{tag}_" + name)

        names = score_consts + ("ident", "upper", "onesb", "scan", "jcol")
        consts = {}
        for name in names:
            src = io[f"c{tag}_" + name]
            consts[name] = sb("c_" + name, list(src.shape), src.dtype)
        nconst = 16 * len(names)
        ident = consts["ident"]
        x = sb("x", [128, 2, RL, D])
        xT = sb("xT", [D, RL, 128], F32 if wide_gate else BF16)
        onehot = sb("onehot", [128, RL, ne], BF16)
        onehot_all = sb("onehot_all", [128, NT, ne], BF16)
        acc = sb("acc", [128, RL, ne], BF16)
        res = sb("res", [128, RL, 2])
        res_all = sb("res_all", [128, NT, 2])
        weighted = sb("weighted", [128, RL, ne])
        blocks_f = sb("blocks_f", [ne, 1])
        blocks_i = sb("blocks_i", [ne, 2], I32)
        blocks_b = sb("blocks_b", [ne, 128], BF16)
        ends = sb("ends", [128, 2 * ne])
        eb_f = sb("eb_f", [128, 2])
        eb_i = sb("eb_i", [128, 2], I32)
        eb_junk = sb("eb_junk", [128, 2, ne])
        base_of = sb("base_of", [128, NT, ne])
        slot_f = sb("slot_f", [128, NT])
        gate = sb("gate", [128, NT])
        rows_f = sb("rows_f", [NT, 2, 128])
        slots = net.slots
        slot_cols = sb("slot_cols", [128, 2, SC], I32)
        x_chunk = sb("x_chunk", [128, 2, SC, D])
        x_loaded = [s(f"x_loaded_{q}") for q in range(2)]
        x_again = [s(f"x_again_{q}") for q in range(2)]
        scattered = [s(f"scattered_{q}") for q in range(2)]
        env = dict(net=net, ps=ps, sb=sb, s=s, consts=consts, x=x, xT=xT, onehot=onehot, res=res, x_loaded=x_loaded)

        def need(eng, base, l, *which):
            for n in which:
                eng.wait_ge(s(n), base + (l + 1))

        env["need"] = need
        score = score_stage(env)

        FULL, REST = divmod(NT, 2 * RL)

        def per_block(eng, body):
            with eng.Fori(0, FULL) as it:
                for q in range(2):
                    body(2 * RL * it + RL * q, range(RL), q, it)
            for q in range(-(-REST // RL)):
                body(2 * RL * FULL + RL * q, range(min(RL, REST - RL * q)), q, FULL)

        block = ctx.enter_context(nc.Block())

        @block.sync
        def _(sp):
            for name in names:
                sp.dma_start(consts[name][:], io[f"c{tag}_" + name]).then_inc(s("consts_loaded"), 16)
            score.get("sync", lambda e: None)(sp)

            def load(base, n, q):
                sp.dma_start(x[:, q, :n], source.rearrange("(j p) d -> p j d", p=128)[:, bass.ds(base, n)]).then_inc(x_loaded[q], 16)

            for q in range(2):
                load(RL * q, RL, q)
            with sp.Fori(0, FULL - 1) as it:
                for q in range(2):
                    sp.wait_ge(s("x_free"), 2 * RL * it + (RL * q + 2 * RL))
                    load(2 * RL * it + RL * (q + 2), RL, q)
            for q in range(-(-REST // RL)):
                sp.wait_ge(s("x_free"), 2 * RL * (FULL - 1) + RL * q + 2 * RL)
                load(2 * RL * FULL + RL * q, min(RL, REST - RL * q), q)

            def load_chunk(c, q):
                sp.dma_start(x_chunk[:, q], source.rearrange("(j p) d -> p j d", p=128)[:, bass.ds(SC * c, SC)]).then_inc(x_again[q], 16)

            for q in range(2):
                load_chunk(q, q)
            sp.wait_ge(s("eb_ready"), 1)
            sp.dma_start(io["eb"], eb_i[:]).then_inc(s("tables_stored"), 16)
            sp.wait_ge(s("rows_ready"), 1)
            sp.dma_start(io["slot_gate"].rearrange("g (j p) -> j g p", p=128), rows_f[:]).then_inc(s("tables_stored"), 16)

            with sp.Fori(0, NT // SC // 2 - 1) as it:
                for q in range(2):
                    sp.wait_ge(scattered[q], 16 * SC * it + 16 * SC)
                    load_chunk(2 * it + q + 2, q)
            sp.wait_ge(scattered[0], 16 * SC * (NT // SC // 2))
            sp.dma_start(x_chunk[:, 0, :NT % SC], source.rearrange("(j p) d -> p j d", p=128)[:, NT - NT % SC:]).then_inc(x_again[0], 16)
            sp.wait_ge(s("tables_stored"), 32)

        @block.tensor
        def _(pe):
            mm, tr = nc.tensor.matmul, nc.tensor.transpose
            pe.wait_ge(s("consts_loaded"), nconst)
            score.get("pe_setup", lambda e: None)(pe)
            pe.sem_inc(s("x_free"), RL)

            def body(base, lanes, q, it):
                pe.wait_ge(x_loaded[q], 16 * it + 16)
                for l in lanes:
                    tr(ps[l][:, 0, :128], x[:, q, l], ident[:]).then_inc(s("x_free"), 1)
                score["pe"](pe, base, lanes)
                for l in lanes:
                    need(pe, base, l, "onehot", "acc")
                    mm(ps[l][:, 1, 256:256 + ne], consts["upper"][:], onehot[:, l], start=True, stop=False)
                    mm(ps[l][:, 1, 256:256 + ne], consts["onesb"][:], acc[:, l], start=False, stop=True).then_inc(s("rank_done"), 1)

            per_block(pe, body)
            pe.wait_ge(s("acc"), NT + 1)
            mm(ps[0][:ne, 0, :1], acc[:, NT % RL], consts["onesb"][:, :1], start=True, stop=True).then_inc(s("count_done"), 1)
            pe.wait_ge(s("blocks_b"), 1)
            mm(ps[0][:, 1, :2 * ne], blocks_b[:], consts["scan"][:], start=True, stop=True).then_inc(s("ends_done"), 1)
            pe.wait_ge(s("slot_f"), 1)
            tr(ps[0][:NT, 1, 256:384], slot_f[:], ident[:])
            tr(ps[0][:NT, 1, 384:], gate[:], ident[:]).then_inc(s("rows_done"), 1)

        @block.vector
        def _(dve):
            v_ = nc.vector
            dve.wait_ge(s("consts_loaded"), nconst)
            dve.sem_inc(s("rank"), RL)
            v_.memset(acc[:], 0.0).then_inc(s("acc"), 1)
            if not wide_gate:
                v_.memset(res[:], 1.0).then_inc(s("res_set"), 1)
                dve.wait_ge(s("res_set"), 1)
            score.get("dve_setup", lambda e: None)(dve)

            def body(base, lanes, q, it):
                score["dve"](dve, base, lanes)
                for l in lanes:
                    need(dve, base, l, "onehot", "acc", "rank_done")
                    v_.tensor_tensor(acc[:, (l + 1) % RL], acc[:, l], onehot[:, l], ALU.add).then_inc(s("acc"), 1)
                    v_.tensor_copy(onehot_all[:, bass.ds(base + l, 1)].rearrange("p o e -> p (o e)"), onehot[:, l])
                    v_.scalar_tensor_tensor(weighted[:, l], ps[l][:, 1, 256:256 + ne], 1.0, onehot[:, l], ALU.mult, ALU.mult,
                                            accum_out=res[:, l, 0:1]).then_inc(s("rank"), 1)
                for l in lanes:
                    dve.wait_ge(s("rank"), base + (l + 1 + RL))
                    v_.tensor_copy(res_all[:, bass.ds(base + l, 1)].rearrange("p o e -> p (o e)"), res[:, l]).then_inc(s("res_kept"), 1)

            per_block(dve, body)
            dve.wait_ge(s("count_done"), 1)
            v_.tensor_scalar(blocks_i[:, 0:1], ps[0][:ne, 0, :1], 127.0, None, ALU.add).then_inc(s("b1"), 1)
            dve.wait_ge(s("b1"), 1)
            v_.tensor_scalar(blocks_i[:, 1:2], blocks_i[:, 0:1], 7, None, ALU.arith_shift_right).then_inc(s("b2"), 1)
            dve.wait_ge(s("b2"), 1)
            v_.tensor_copy(blocks_f[:], blocks_i[:, 1:2]).then_inc(s("b3"), 1)
            dve.wait_ge(s("b3"), 1)
            v_.tensor_scalar(blocks_b[:], consts["onesb"][:ne], blocks_f[:], None, ALU.mult).then_inc(s("blocks_b"), 1)
            dve.wait_ge(s("ends_done"), 1)
            v_.tensor_copy(ends[:], ps[0][:, 1, :2 * ne]).then_inc(s("ends"), 1)
            dve.wait_ge(s("ends"), 1)
            for i in range(2):
                ins = v_.tensor_scalar(eb_junk[:, i], ends[:, :ne], consts["jcol"][:, i:i + 1], None, ALU.is_le, ALU.add,
                                       accum_out=eb_f[:, i:i + 1])
            ins.then_inc(s("eb_f"), 1)
            dve.wait_ge(s("eb_f"), 1)
            v_.tensor_scalar(eb_i[:], eb_f[:], float(ne - 1), None, ALU.min).then_inc(s("eb_ready"), 1)
            dve.wait_ge(s("res_kept"), NT)
            v_.tensor_tensor(base_of[:], onehot_all[:], ends[:, ne:].unsqueeze(1).broadcast_to([128, NT, ne]), ALU.mult).then_inc(s("base_of"), 1)
            dve.wait_ge(s("base_of"), 1)
            v_.tensor_reduce(slot_f[:], base_of[:], AX.X, ALU.add).then_inc(s("base_sum"), 1)
            v_.reciprocal(gate[:], res_all[:, :, 1])
            dve.wait_ge(s("base_sum"), 1)
            v_.tensor_tensor(slot_f[:], slot_f[:], res_all[:, :, 0], ALU.add).then_inc(s("slot_f"), 1)
            dve.wait_ge(s("slot_f"), 1)
            v_.tensor_copy(slots[:], slot_f[:]).then_inc(s("slots"), 1)
            dve.wait_ge(s("rows_done"), 1)
            v_.tensor_copy(rows_f[:], ps[0][:NT, 1, 256:].rearrange("p (g n) -> p g n", g=2)).then_inc(s("rows_ready"), 1)

        @block.scalar
        def _(act):
            act.wait_ge(s("consts_loaded"), nconst)
            if "act" in score:
                per_block(act, lambda base, lanes, q, it: score["act"](act, base, lanes))

        @block.gpsimd
        def _(pool):
            pool.wait_ge(s("slots"), 1)

            def scatter(c, q, times, n):
                pool.wait_ge(x_again[q], 16 * times + 16)
                pool.sem_inc(s("settled"), 1)
                nc.gpsimd.tensor_copy(slot_cols[:, q, :n], slots[:, bass.ds(SC * c, n)]).then_inc(s("slot_cols"), 1)
                pool.wait_ge(s("slot_cols"), c + 1)
                pool.sem_inc(s("settled"), 1)
                for b in range(n):
                    nc.gpsimd.indirect_dma_start(io[f"sorted{tag[-1]}"], bass.IndirectOffsetOnAxis(slot_cols[:, q, b:b + 1], 0),
                                                 x_chunk[:, q, b], None).then_inc(scattered[q], 16)

            with pool.Fori(0, NT // SC // 2) as it:
                for q in range(2):
                    scatter(2 * it + q, q, it, SC)
            scatter(NT // SC, 0, NT // SC // 2, NT % SC)
            pool.wait_ge(scattered[0], 16 * (SC * (NT // SC // 2) + NT % SC))
            pool.wait_ge(scattered[1], 16 * SC * (NT // SC // 2))


def gate_scores(env):
    net, sb, s, need = env["net"], env["sb"], env["s"], env["need"]
    nc, ps, consts = net.nc, env["ps"], env["consts"]
    xT, onehot, res = env["xT"], env["onehot"], env["res"]
    lg, nmx, ex, first, mx2 = sb("lg", [128, RL, E0]), sb("nmx", [128, RL]), sb("ex", [128, RL, E0]), sb("first", [128, RL, E0]), sb("mx2", [128, RL])

    def pe(eng, base, lanes):
        for l in lanes:
            need(eng, base, l, "xT", "rank")
            eng.sem_inc(s("settled"), 1)
            nc.tensor.matmul(ps[l][:, 1, :E0], xT[:, l], consts["gw"][:], start=True, stop=True).then_inc(s("scores_done"), 1)

    def act(eng, base, lanes):
        for l in lanes:
            eng.wait_ge(s("x_free"), base + (l + 1 + RL))
            nc.scalar.activation(xT[:, l], ps[l][:, 0, :128], ACT.Copy).then_inc(s("xT"), 1)
        for l in lanes:
            need(eng, base, l, "lg0")
            nc.scalar.activation(ex[:, l], lg[:, l], ACT.Exp, accum_out=res[:, l, 1:2]).then_inc(s("gate_sum"), 1)

    def dve(eng, base, lanes):
        v_ = nc.vector
        for l in lanes:
            need(eng, base, l, "scores_done")
            v_.tensor_tensor(lg[:, l], ps[l][:, 1, :E0], consts["gb"][:], ALU.add).then_inc(s("lg"), 1)
        for l in lanes:
            need(eng, base, l, "lg")
            v_.tensor_reduce(nmx[:, l:l + 1], lg[:, l], AX.X, ALU.max, negate=True).then_inc(s("nmx"), 1)
        for l in lanes:
            need(eng, base, l, "nmx")
            v_.tensor_scalar(lg[:, l], lg[:, l], nmx[:, l:l + 1], None, ALU.add).then_inc(s("lg0"), 1)
        for l in lanes:
            need(eng, base, l, "lg0")
            v_.scalar_tensor_tensor(first[:, l], lg[:, l], 0.0, consts["order"][:], ALU.is_equal, ALU.mult).then_inc(s("first"), 1)
        for l in lanes:
            need(eng, base, l, "first")
            v_.tensor_reduce(mx2[:, l:l + 1], first[:, l], AX.X, ALU.max).then_inc(s("mx2"), 1)
        for l in lanes:
            need(eng, base, l, "mx2", "gate_sum")
            v_.tensor_scalar(onehot[:, l], first[:, l], mx2[:, l:l + 1], None, ALU.is_equal).then_inc(s("onehot"), 1)

    return {"pe": pe, "act": act, "dve": dve}


def route_experts(net):
    route(net, "r0", E0, NB0, net.io["t"].rearrange("b t d -> (b t) d"), ("gw", "gb", "order"), gate_scores, True)


def sign_scores(env):
    net, sb, s, need = env["net"], env["sb"], env["s"], env["need"]
    nc, ps, consts = net.nc, env["ps"], env["consts"]
    xT, onehot = env["xT"], env["onehot"]
    wd = sb("wd", [D, T1, DH])
    sums, pos = sb("sums", [D, T1]), sb("pos", [D, T1])
    nsig = sb("nsig", [D, T1])
    csum, cpos, csig = sb("csum", [D, CL]), sb("cpos", [D, CL]), sb("csig", [D, CL])
    sig = sb("sig", [D, CL + T1], BF16)
    key, mx = sb("key", [128, RL, CL + T1]), sb("mx", [128, RL, 2])
    big = sb("big", [128, RL, CL])

    def sync(eng):
        eng.dma_start(wd[:], net.io["wdT"]).then_inc(s("wd_loaded"), 16)

    def dve_setup(eng):
        v_ = nc.vector
        eng.wait_ge(s("wd_loaded"), 16)
        v_.tensor_reduce(sums[:], wd[:], AX.X, ALU.add).then_inc(s("sums"), 1)
        eng.wait_ge(s("sums"), 1)
        v_.tensor_scalar(pos[:], sums[:], 0.0, None, ALU.is_gt).then_inc(s("pos"), 1)
        eng.wait_ge(s("pos"), 1)
        v_.scalar_tensor_tensor(nsig[:], sums[:], 0.0, pos[:], ALU.is_lt, ALU.subtract).then_inc(s("nsig"), 1)
        eng.wait_ge(s("nsig"), 1)
        v_.tensor_scalar(sig[:, CL:], nsig[:], float(T1), None, ALU.mult)
        v_.tensor_reduce(csum[:], nsig[:].rearrange("p (c t) -> p c t", c=CL), AX.X, ALU.add).then_inc(s("csum"), 1)
        eng.wait_ge(s("csum"), 1)
        v_.tensor_scalar(cpos[:], csum[:], 0.0, None, ALU.is_lt).then_inc(s("cpos"), 1)
        eng.wait_ge(s("cpos"), 1)
        v_.scalar_tensor_tensor(csig[:], csum[:], 0.0, cpos[:], ALU.is_gt, ALU.subtract).then_inc(s("csig"), 1)
        eng.wait_ge(s("csig"), 1)
        v_.tensor_scalar(sig[:, :CL], csig[:], float(CL), None, ALU.mult).then_inc(s("sig"), 1)

    def pe_setup(eng):
        eng.wait_ge(s("sig"), 1)

    def act(eng, base, lanes):
        for l in lanes:
            eng.wait_ge(s("x_free"), base + (l + 1 + RL))
            nc.scalar.activation(xT[:, l], ps[l][:, 0, :128], ACT.Sign, scale=-1.0).then_inc(s("xT"), 1)

    def pe(eng, base, lanes):
        for l in lanes:
            need(eng, base, l, "xT", "rank")
            nc.tensor.matmul(ps[l][:, 1, :CL + T1], xT[:, l], sig[:], start=True, stop=True).then_inc(s("scores_done"), 1)

    def dve(eng, base, lanes):
        v_ = nc.vector
        for l in lanes:
            need(eng, base, l, "scores_done")
            v_.tensor_tensor(key[:, l], ps[l][:, 1, :CL + T1], consts["order"][:], ALU.add).then_inc(s("key"), 1)
        for l in lanes:
            need(eng, base, l, "key")
            v_.tensor_reduce(mx[:, l, 0:1], key[:, l, :CL], AX.X, ALU.max).then_inc(s("mx_c"), 1)
        for l in lanes:
            need(eng, base, l, "mx_c")
            v_.tensor_scalar(big[:, l], key[:, l, :CL], mx[:, l, 0:1], float(1 << 15), ALU.is_equal, ALU.mult).then_inc(s("big"), 1)
        for l in lanes:
            need(eng, base, l, "big")
            kt = key[:, l, CL:].rearrange("p (c t) -> p c t", c=CL)
            v_.tensor_tensor(kt, kt, big[:, l].unsqueeze(2).broadcast_to([128, CL, T1 // CL]), ALU.add).then_inc(s("key_t"), 1)
        for l in lanes:
            need(eng, base, l, "key_t")
            v_.tensor_reduce(mx[:, l, 1:2], key[:, l, CL:], AX.X, ALU.max).then_inc(s("mx_t"), 1)
        for l in lanes:
            need(eng, base, l, "mx_t")
            v_.tensor_scalar(onehot[:, l], key[:, l, CL:], mx[:, l, 1:2], None, ALU.is_equal).then_inc(s("onehot"), 1)

    return {"sync": sync, "dve_setup": dve_setup, "pe_setup": pe_setup, "pe": pe, "act": act, "dve": dve}


def route_tiles(net):
    route(net, "r1", T1, NB1, net.io["xf"].rearrange("b t d -> (b t) d"), ("order",), sign_scores, False)


def sorted_blocks(net, tag, nb, width, emit):
    nc, io, sem = net.nc, net.io, net.sem
    S = 2 * EL
    with ExitStack() as ctx:
        ps = [ctx.enter_context(nc.psum_tensor(f"{tag}_ps{l}", [128, 2, 512], F32)) for l in range(EL)]
        def sb(name, shape, dt=F32):
            return net.sb(ctx, f"{tag}_" + name, shape, dt)

        def s(name):
            return sem(f"{tag}_" + name)

        eb = sb("eb", [1, 256], I32)
        ident = sb("ident", [128, 128])
        x = sb("x", [128, S, D])
        w_all = sb("w_all", [128, E0, width])
        w = sb("w", [128, S, width])
        xT = sb("xT", [D, EL, 128])
        y = sb("y", [128, S, D])
        loaded = [s(f"loaded_{i}") for i in range(S)]
        y_stored = [s(f"y_stored_{i}") for i in range(S)]

        def need(eng, base, l, *which):
            for n in which:
                eng.wait_ge(s(n), base + (l + 1))

        def per_block(eng, body):
            with eng.Fori(0, nb // S) as it:
                for a in range(2):
                    body(S * it + EL * a, EL * a, it)

        env = dict(net=net, ps=ps, sb=sb, s=s, need=need, x=x, w=w, xT=xT, y=y, y_stored=y_stored)
        parts = emit(env)
        block = ctx.enter_context(nc.Block())

        @block.sync
        def _(sp):
            sp.dma_start(ident[:], io["ident"]).then_inc(s("ident_loaded"), 16)
            sp.dma_start(eb[:], io["eb"].rearrange("p g -> (p g)").unsqueeze(0)).then_inc(s("eb_loaded"), 16)
            for i in range(S):
                sp.sem_inc(y_stored[i], 16)

            def load(base, slot0):
                for l in range(EL):
                    sp.dma_start(x[:, slot0 + l], block_rows(io[f"sorted{tag[-1]}"], base + l)).then_inc(loaded[slot0 + l], 16)

            def store(base, slot0):
                for l in range(EL):
                    sp.wait_ge(s("y_ready"), base + (l + 1 + EL))
                    sp.dma_start(block_rows(io[f"y{tag[-1]}"], base + l), y[:, slot0 + l]).then_inc(y_stored[slot0 + l], 16)

            load(0, 0)
            load(EL, EL)
            for e in range(E0):
                sp.dma_start(w_all[:, e], io[f"{tag}_w"][e]).then_inc(s("w_loaded"), 16)
            with sp.Fori(0, nb // S - 1) as it:
                for a in range(2):
                    store(S * it + EL * a, EL * a)
                    load(S * it + EL * a + S, EL * a)
            for a in range(2):
                store(nb - S + EL * a, EL * a)
            for i in range(S):
                sp.wait_ge(y_stored[i], 16 * (nb // S) + 16)

        @block.tensor
        def _(pe):
            pe.wait_ge(s("ident_loaded"), 16)

            def body(base, slot0, it):
                for l in range(EL):
                    pe.wait_ge(loaded[slot0 + l], 16 * it + 16)
                    need(pe, base, l, "y_ready")
                    nc.tensor.transpose(ps[l][:, 0, :128], x[:, slot0 + l], ident[:]).then_inc(s("x_transposed"), 1)
                parts["pe"](pe, base, slot0)

            per_block(pe, body)

        @block.vector
        def _(dve):
            def take_weights(base, slot0):
                for l in range(EL):
                    e = dve.value_load(eb[0:1, bass.ds(base + l, 1)], min_val=0, max_val=E0 - 1)
                    nc.vector.tensor_copy(w[:, slot0 + l], w_all[:, bass.ds(e, 1)].rearrange("p o n -> p (o n)")).then_inc(s("w_taken"), 1)

            dve.sem_inc(s("y_ready"), EL)
            dve.wait_ge(s("eb_loaded"), 16)
            dve.wait_ge(s("w_loaded"), 16 * E0)
            take_weights(0, 0)

            def body(base, slot0, it):
                for l in range(EL):
                    need(dve, base, l, "x_transposed")
                    nc.vector.tensor_copy(xT[:, l], ps[l][:, 0, :128]).then_inc(s("xT"), 1)
                for l in range(EL):
                    dve.wait_ge(y_stored[(slot0 + EL) % S + l], 16 * it + (32 if slot0 else 16))
                take_weights(base + EL, (slot0 + EL) % S)
                parts["dve"](dve, base, slot0, it)

            per_block(dve, body)

        @block.scalar
        def _(act):
            per_block(act, lambda base, slot0, it: parts["act"](act, base, slot0, it))


def expert_parts(env):
    net, sb, s, need = env["net"], env["sb"], env["s"], env["need"]
    nc, ps, w, xT, y, y_stored = net.nc, env["ps"], env["w"], env["xT"], env["y"], env["y_stored"]
    C = FF // 128
    hid = sb("hid", [128, EL, C, 128])

    def pe(eng, base, slot0):
        mm = nc.tensor.matmul
        for l in range(EL):
            need(eng, base, l, "xT", "w_taken")
            for c in range(C):
                ins = mm(ps[l][:, 1, 128 * c:128 * c + 128], w[:, slot0 + l, 128 * c:128 * c + 128], xT[:, l], start=True, stop=True)
            ins.then_inc(s("up_done"), 1)
        for l in range(EL):
            need(eng, base, l, "hid")
            for c in range(C):
                ins = mm(ps[l][:, 0, 128:128 + D], hid[:, l, c], w[:, slot0 + l, FF + 128 * c:FF + 128 * c + 128], start=(c == 0), stop=(c == C - 1))
            ins.then_inc(s("down_done"), 1)

    def act(eng, base, slot0, it):
        for l in range(EL):
            need(eng, base, l, "up_done")
            for c in range(C):
                ins = nc.scalar.activation(hid[:, l, c], ps[l][:, 1, 128 * c:128 * c + 128], ACT.Gelu_apprx_tanh,
                                           bias=w[:, slot0 + l, 2 * FF + c:2 * FF + c + 1])
            ins.then_inc(s("hid"), 1)

    def dve(eng, base, slot0, it):
        for l in range(EL):
            eng.wait_ge(y_stored[slot0 + l], 16 * it + 16)
            need(eng, base, l, "down_done")
            nc.vector.tensor_tensor(y[:, slot0 + l], ps[l][:, 0, 128:128 + D], w[:, slot0 + l, 2 * FF + C:], ALU.add).then_inc(s("y_ready"), 1)

    return {"pe": pe, "act": act, "dve": dve}


def experts(net):
    sorted_blocks(net, "f0", NB0, W0C, expert_parts)


def spline_tiles(net):
    nc, io, sem = net.nc, net.io, net.sem
    GB, SLOTS, NG = 4, 4, NB1 // 4
    W = GB * 128
    OF_ACT = 34
    BASE, SLOPE = 2 * 128, 2 * 128 + GRID
    with ExitStack() as ctx:
        def sb(name, shape, dt=F32):
            return net.sb(ctx, "f1_" + name, shape, dt)

        def s(name):
            return sem("f1_" + name)

        ps = [[ctx.enter_context(nc.psum_tensor(f"f1_{name}{q}", [128, GB, 128], F32)) for q in range(2)]
              for name in ("xT_ps", "h_ps", "y_ps")]
        xT_ps, h_ps, y_ps = ps
        eb = sb("eb", [1, 256], I32)
        ident = sb("ident", [128, 128])
        gidx = sb("gidx", [DH, GRID])
        x = sb("x", [128, SLOTS, GB, D])
        w = sb("w", [128, SLOTS, GB, W1C])
        xT = sb("xT", [D, 2, GB, 128])
        hn = sb("hn", [DH, SLOTS, GB, 128])
        slope = sb("slope", [DH, 2, GB, GRID])
        shift = sb("shift", [DH, 2, GB, GRID])
        hs = sb("hs", [DH, SLOTS, GB, 128])
        pieces = sb("pieces", [DH, 2, GRID - 1, GB, 128])
        mask = sb("mask", [DH, 2, GRID - 1, GB, 128], U8)
        y = sb("y", [128, 2, GB, D])
        sixteen = sb("sixteen", [DH, GRID])
        loaded = [s(f"loaded_{i}") for i in range(SLOTS)]
        y_stored = [s(f"y_stored_{q}") for q in range(2)]

        def groups(eng, body, last=None):
            body(0, 0)
            body(1, 1)
            with eng.Fori(0, (NG - 2) // SLOTS) as it:
                for j in range(SLOTS):
                    body(SLOTS * it + (j + 2), (j + 2) % SLOTS, it)
            if last:
                last(NG - 1)

        def times(i, j, it, n):
            return 16 * n if it is None else 16 * n * it + 16 * n * (1 + (j < 2))

        block = ctx.enter_context(nc.Block())

        @block.sync
        def _(sp):
            sp.dma_start(ident[:], io["ident"]).then_inc(s("consts_loaded"), 16)
            sp.dma_start(gidx[:], io["gidx"]).then_inc(s("consts_loaded"), 16)
            sp.dma_start(eb[:], io["eb"].rearrange("p g -> (p g)").unsqueeze(0)).then_inc(s("eb_loaded"), 16)
            sp.wait_ge(s("eb_loaded"), 16)

            def load(i, j):
                for b in range(GB):
                    e = sp.value_load(eb[0:1, bass.ds(GB * i + b, 1)], min_val=0, max_val=T1 - 1)
                    sp.dma_start(w[:, j, b], io["f1_w"][bass.ds(e, 1)].rearrange("o p n -> (o p) n")).then_inc(loaded[j], 16)
                sp.dma_start(x[:, j], io["sorted1"].rearrange("(i b p) d -> i p b d", b=GB, p=128)[bass.ds(i, 1)].rearrange(
                    "o p b d -> p (o b) d")).then_inc(loaded[j], 16)

            def store(i, q):
                sp.wait_ge(s("y_ready"), i + 3)
                sp.dma_start(io["y1"].rearrange("(i b p) d -> i p b d", b=GB, p=128)[bass.ds(i, 1)].rearrange(
                    "o p b d -> p (o b) d"), y[:, q]).then_inc(y_stored[q], 16)

            for q in range(2):
                sp.sem_inc(y_stored[q], 16)
            for i in range(SLOTS):
                load(i, i)
            with sp.Fori(0, (NG - 2 - SLOTS) // SLOTS) as it:
                for j in range(SLOTS):
                    store(SLOTS * it + j, j % 2)
                    load(SLOTS * it + j + SLOTS, j)
            done = NG - 2 - SLOTS
            for i in range(done, NG):
                store(i, i % 2)
                if i + SLOTS < NG:
                    load(i + SLOTS, i % SLOTS)
            for q in range(2):
                sp.wait_ge(y_stored[q], 16 * NG // 2 + 16)

        def make_pieces(op, i, j, which, done):
            for n in which:
                b, g = n // GRID, n % GRID
                dst = pieces[:, j % 2, g - 1, b] if g else hs[:, j, b]
                ins = op(dst, hn[:, j, b], slope[:, j % 2, b, g:g + 1], shift[:, j % 2, b, g:g + 1])
            ins.then_inc(s(done), 1)

        @block.gpsimd
        def _(pool):
            gp = nc.gpsimd
            pool.wait_ge(s("consts_loaded"), 32)

            def body(i, j, it=None):
                q = j % 2
                pool.wait_ge(loaded[j], times(i, j, it, GB + 1))
                if it is not None:
                    pool.wait_ge(s("act_pieces"), i - 1)
                gp.tensor_tensor(shift[:, q], w[:, j, :, SLOPE:SLOPE + GRID], gidx[:].unsqueeze(1).broadcast_to([DH, GB, GRID]), ALU.mult).then_inc(s("gslope"), 1)
                gp.tensor_tensor(slope[:, q], w[:, j, :, SLOPE:SLOPE + GRID], sixteen[:].unsqueeze(1).broadcast_to([DH, GB, GRID]), ALU.mult)
                pool.wait_ge(s("gslope"), i + 1)
                gp.tensor_tensor(shift[:, q], w[:, j, :, BASE:BASE + GRID], shift[:, q], ALU.subtract).then_inc(s("tables"), 1)
                pool.wait_ge(s("tables"), i + 1)
                pool.wait_ge(s("hn"), i + 1)
                pool.wait_ge(s("picked"), i + 1)
                pool.sem_inc(s("settled"), 1)
                make_pieces(lambda dst, src, a, b: gp.tensor_scalar(dst, src, a, b, ALU.mult, ALU.add), i, j, range(OF_ACT, GB * GRID), "pool_pieces")

            gp.memset(sixteen[:], float(GRID)).then_inc(s("sixteen"), 1)
            pool.wait_ge(s("sixteen"), 1)
            groups(pool, body)

        @block.scalar
        def _(act):
            a_ = nc.scalar.activation

            def own_pieces(i, j, which, done):
                act.wait_ge(s("hn"), i + 1)
                act.wait_ge(s("tables"), i + 1)
                act.wait_ge(s("picked"), i + 1)
                make_pieces(lambda dst, src, a, b: a_(dst, src, ACT.Identity, scale=a, bias=b), i, j, which, done)

            def body(i, j, it=None):
                cuts = (0, OF_ACT // 3, 2 * OF_ACT // 3, OF_ACT)

                def third(n):
                    if not (it is None and i == 0):
                        own_pieces(i - 1, (j - 1) % SLOTS, range(cuts[n], cuts[n + 1]), ("act_third", "act_two_thirds", "act_pieces")[n])

                third(0)
                act.wait_ge(s("x_transposed"), i + 1)
                a_(xT[:, j % 2], xT_ps[j % 2][:], ACT.Copy).then_inc(s("xT"), 1)
                third(1)
                act.wait_ge(s("h_done"), i + 1)
                a_(hn[:, j], h_ps[j % 2][:], ACT.Sigmoid).then_inc(s("hn"), 1)
                third(2)

            def last(i):
                own_pieces(i, i % SLOTS, range(OF_ACT), "act_pieces")

            groups(act, body, last)

        @block.tensor
        def _(pe):
            mm, tr = nc.tensor.matmul, nc.tensor.transpose
            pe.wait_ge(s("consts_loaded"), 32)

            def up(i, j):
                pe.wait_ge(s("picked"), i + 3)
                pe.wait_ge(s("y_ready"), i + 1)
                pe.sem_inc(s("settled_pe"), 1)
                for b in range(GB):
                    ins = mm(y_ps[j % 2][:, b], hs[:, j, b], w[:, j, b, 128:256], start=True, stop=True)
                ins.then_inc(s("y_done"), 1)

            def body(i, j, it=None):
                q = j % 2
                pe.wait_ge(loaded[j], times(i, j, it, GB + 1))
                if it is not None:
                    pe.wait_ge(s("xT"), i - 1)
                    pe.wait_ge(s("hn"), i - 1)
                for b in range(GB):
                    ins = tr(xT_ps[q][:, b], x[:, j, b], ident[:])
                ins.then_inc(s("x_transposed"), 1)
                pe.wait_ge(s("xT"), i + 1)
                for b in range(GB):
                    ins = mm(h_ps[q][:, b], w[:, j, b, :128], xT[:, q, b], start=True, stop=True)
                ins.then_inc(s("h_done"), 1)
                if it is not None:
                    up(i - 2, (j - 2) % SLOTS)

            def last(i):
                up(i - 1, (i - 1) % SLOTS)
                up(i, i % SLOTS)

            groups(pe, body, last)

        @block.vector
        def _(dve):
            v_ = nc.vector
            dve.sem_inc(s("picked"), 2)
            dve.sem_inc(s("y_ready"), 2)

            def finish(i, j):
                q = j % 2
                dve.wait_ge(s("y_done"), i + 1)
                v_.tensor_tensor(y[:, q], y_ps[q][:], w[:, j, :, W1C - 1:W1C].broadcast_to([128, GB, D]), ALU.mult).then_inc(s("y_ready"), 1)

            def body(i, j, it=None):
                q = j % 2

                def compare(g):
                    v_.tensor_scalar(mask[:, q, g - 1], hn[:, j], g / GRID, None, ALU.is_ge).then_inc(s("masked"), 1)

                dve.wait_ge(s("hn"), i + 1)
                compare(1)
                compare(2)
                dve.wait_ge(s("act_pieces"), i + 1)
                dve.wait_ge(s("pool_pieces"), i + 1)
                for g in range(1, GRID):
                    dve.wait_ge(s("masked"), (GRID - 1) * i + g)
                    if g > 1:
                        dve.wait_ge(s("picks"), (GRID - 1) * i + g - 1)
                    dve.sem_inc(s("settled_dve"), 1)
                    ins = v_.copy_predicated(hs[:, j], mask[:, q, g - 1], pieces[:, q, g - 1])
                    ins.then_inc(s("picks"), 1)
                    if g + 2 < GRID:
                        compare(g + 2)
                    if g == 4 and not (it is None and i == 0):
                        if it is not None:
                            dve.wait_ge(y_stored[(j - 1) % 2], 8 * SLOTS * it + 16 * (((j + 2) % SLOTS + 1) // 2 + 1))
                        finish(i - 1, (j - 1) % SLOTS)
                dve.wait_ge(s("picks"), (GRID - 1) * i + (GRID - 1))
                dve.sem_inc(s("picked"), 1)

            def last(i):
                dve.wait_ge(y_stored[i % 2], 16 * (NG // 2))
                finish(i, i % SLOTS)

            groups(dve, body, last)


def layer1(net):
    nc, io, sem = net.nc, net.io, net.sem
    EX = 2 * D
    with ExitStack() as ctx:
        ps = [ctx.enter_context(nc.psum_tensor(f"l1_ps{l}", [128, 2, 512], F32)) for l in range(L1N)]
        def sb(name, shape, dt=F32):
            return net.sb(ctx, "l1_" + name, shape, dt)

        def s(name):
            return sem("l1_" + name)

        consts = {}
        for name in L1_CONSTS:
            src = io["c2_" + name]
            consts[name] = sb("c_" + name, list(src.shape), src.dtype)
        ident = consts["ident"]
        rows = sb("rows", [128, 2, TH])
        slot_i = sb("slot_i", [TH, 128], I32)
        gate = sb("gate", [TH, 128])
        cols = sb("cols", [TH, L1N, 2], I32)
        gcols = sb("gcols", [TH, L1N, 2])
        neg_half = sb("neg_half", [TH, 2, 2])
        h1 = sb("h1", [TH, L1N, 2, D])
        y = sb("y", [TH, L1N, 2, D])
        h2 = sb("h2", [TH, L1N, 2, D])
        stats = sb("stats", [TH, L1N, 2, 6])
        mv = sb("mv", [TH, L1N, 2, 2])
        rstd = sb("rstd", [TH, L1N, 2])
        x = sb("x", [TH, L1N, 2, D])
        rstd_b = sb("rstd_b", [TH, L1N, 2])
        rstd_c = sb("rstd_c", [TH, L1N, 2])
        xg = sb("xg", [TH, L1N, 2, D])
        rms = sb("rms", [TH, L1N, 2])
        hb = sb("hb", [TH, L1N, 2, D])
        xr = sb("xr", [TH, L1N, 2, D])
        xrT = sb("xrT", [D, L1N, T])
        uT = sb("uT", [D, L1N, 2, T])
        bT = sb("bT", [D, L1N, T])
        qT, kT = sb("qT", [D, L1N, T]), sb("kT", [D, L1N, T])
        vb = sb("vb", [TH, L1N, 2, EX])
        v = sb("v", [TH, L1N, 2, EX])
        r1, r2 = sb("r1", [TH, L1N, 2, T]), sb("r2", [TH, L1N, 2, T])
        rot = sb("rot", [TH, L1N, 2, T])
        kern = sb("kern", [TH, L1N, 2, T])
        uo = sb("uo", [D, L1N, 2, T])
        h3 = sb("h3", [TH, L1N, 2, D])
        x2 = sb("x2", [TH, L1N, 2, D])
        r3 = sb("r3", [TH, L1N, 2, D])
        xf = sb("xf", [TH, L1N, 2, D])
        loaded = [s(f"h1_loaded_{l}") for l in range(L1N)]
        gathered = [s(f"gathered_{l}") for l in range(L1N)]
        r3_stored = [s(f"r3_stored_{l}") for l in range(L1N)]
        xf_stored = [s(f"xf_stored_{l}") for l in range(L1N)]
        STEPS = B // L1N
        nconst = 16 * len(L1_CONSTS)

        def need(eng, it, l, *names):
            for n in names:
                eng.wait_ge(s(n), L1N * it + l + 1)

        def need_pair(eng, it, lanes, *names):
            for n in names:
                eng.wait_ge(s(n), 2 * it + lanes[0] // 2 + 1)

        def settle(eng):
            eng.sem_inc(s("settled"), 1)

        def last_step(it):
            return isinstance(it, int) and it == STEPS - 1

        block = ctx.enter_context(nc.Block())

        @block.sync
        def _(sp):
            for name in L1_CONSTS:
                sp.dma_start(consts[name][:], io["c2_" + name]).then_inc(s("consts_loaded"), 16)
            sp.dma_start(rows[:], io["slot_gate"].rearrange("g (r p) -> r g p", p=TH)).then_inc(s("rows_loaded"), 16)
            for l in range(L1N):
                sp.sem_inc(r3_stored[l], 16)
                sp.sem_inc(xf_stored[l], 16)

            def image(it, l):
                return bass.ds(L1N * it + l, 1)

            def load(it, l):
                sp.dma_start(h1[:, l], halves(io["h1"][image(it, l)])).then_inc(loaded[l], 16)

            def store(it, l, name, ready, tile, stored):
                need(sp, it, l, ready)
                sp.dma_start(halves(io[name][image(it, l)]), tile[:, l]).then_inc(stored[l], 16)

            for l in range(L1N):
                load(0, l)

            def first(it, lanes):
                yield 1
                for l in lanes:
                    need(sp, it, l, "h2")
                    if not last_step(it):
                        load(it + 1, l)

            def second(it, lanes):
                yield 9
                for l in lanes:
                    store(it, l, "r3", "r3", r3, r3_stored)
                yield 13
                for l in lanes:
                    store(it, l, "xf", "xf", xf, xf_stored)

            in_turns(sp, STEPS, first, second)
            for l in range(L1N):
                sp.wait_ge(r3_stored[l], 16 * STEPS + 16)
                sp.wait_ge(xf_stored[l], 16 * STEPS + 16)

        @block.gpsimd
        def _(pool):
            gp = nc.gpsimd
            gp.memset(neg_half[:], -0.5).then_inc(s("neg_half_ready"), 1)
            pool.wait_ge(s("neg_half_ready"), 1)
            pool.wait_ge(s("slot_i"), 1)
            pool.wait_ge(s("gate"), 1)

            def gather(it, l):
                pair = bass.ds(2 * (L1N * it + l), 2)
                gp.tensor_copy(cols[:, l], slot_i[:, pair]).then_inc(s("cols"), 1)
                gp.tensor_copy(gcols[:, l], gate[:, pair]).then_inc(s("gcols"), 1)
                need(pool, it, l, "cols")
                settle(pool)
                for u in range(2):
                    gp.indirect_dma_start(y[:, l, u], None, io["y0"], bass.IndirectOffsetOnAxis(cols[:, l, u:u + 1], 0)).then_inc(gathered[l], 16)

            def power(it, lanes, src, dst, after, eps):
                settle(pool)
                gp.tensor_scalar(dst, src, 1.0, eps, ALU.mult, ALU.add).then_inc(s(after + "_sum"), 1)
                need_pair(pool, it, lanes, after + "_sum")
                gp.tensor_tensor(dst, dst, neg_half[:], ALU.pow).then_inc(s(after), 1)

            def inverse_deviations(it, lanes, tag, first_r, second_r, eps):
                p = slice(lanes[0], lanes[0] + 2)
                need(pool, it, lanes[1], "ln_" + tag)
                power(it, lanes, mv[:, p, :, 1], first_r[:, p], "rstd_" + tag, EPS_LN)
                need_pair(pool, it, lanes, "rstd_" + tag)
                gp.tensor_tensor(second_r[:, p], first_r[:, p], first_r[:, p], ALU.mult).then_inc(s("square_" + tag), 1)
                need_pair(pool, it, lanes, "square_" + tag)
                gp.tensor_tensor(second_r[:, p], second_r[:, p], mv[:, p, :, 1], ALU.mult).then_inc(s("ms_" + tag), 1)
                need_pair(pool, it, lanes, "ms_" + tag)
                power(it, lanes, second_r[:, p], second_r[:, p], "again_" + tag, eps)

            for l in range(L1N):
                gather(0, l)

            def first(it, lanes):
                yield 1
                inverse_deviations(it, lanes, "a", rstd, rms, EPS_RMS)
                yield 7
                for l in lanes:
                    if not last_step(it):
                        gather(it + 1, l)
                yield 5
                for l in lanes:
                    need(pool, it, l, "x")
                    gp.tensor_tensor(hb[:, l], h2[:, l], x[:, l], ALU.add).then_inc(s("hx"), 1)
                yield 6
                for l in lanes:
                    need(pool, it, l, "hx")
                    gp.tensor_tensor(hb[:, l], hb[:, l], consts["b2"][:], ALU.add).then_inc(s("hb"), 1)

            def second(it, lanes):
                yield 6
                inverse_deviations(it, lanes, "b", rstd_b, rstd_c, EPS_LN)
                yield 7
                for l in lanes:
                    need(pool, it, l, "x2")
                    pool.wait_ge(r3_stored[l], 16 * it + 16)
                    gp.tensor_tensor(r3[:, l], h3[:, l], x2[:, l], ALU.add).then_inc(s("r3"), 1)
                yield 10
                for l in lanes:
                    need(pool, it, l, "xg")
                    pool.wait_ge(xf_stored[l], 16 * it + 16)
                    gp.tensor_tensor(xf[:, l], xg[:, l], consts["beta"][:], ALU.add).then_inc(s("xf"), 1)

            in_turns(pool, STEPS, first, second)

        def layer_norm(dve, it, l, src, tag):
            for u in range(2):
                nc.vector.bn_stats(stats[:, l, u], src[:, l, u]).then_inc(s("bn_" + tag), 1)
            dve.wait_ge(s("bn_" + tag), 2 * L1N * it + 2 * (l + 1))
            settle(dve)
            for u in range(2):
                ins = nc.vector.bn_aggr(mv[:, l, u], stats[:, l, u])
            ins.then_inc(s("ln_" + tag), 1)

        def normalise(it, l, src, dst, inverse, done):
            for u in range(2):
                ins = nc.vector.tensor_scalar(dst[:, l, u], src[:, l, u], mv[:, l, u, 0:1], inverse[:, l, u:u + 1],
                                              ALU.subtract, ALU.mult)
            ins.then_inc(s(done), 1)

        @block.vector
        def _(dve):
            v_ = nc.vector
            dve.wait_ge(s("consts_loaded"), nconst)
            dve.wait_ge(s("rows_transposed"), 1)
            v_.tensor_copy(slot_i[:], ps[0][:TH, 0, :128]).then_inc(s("slot_i"), 1)
            v_.tensor_copy(gate[:], ps[0][:TH, 0, 128:256]).then_inc(s("gate"), 1)
            def first(it, lanes):
                yield 0
                for l in lanes:
                    dve.wait_ge(loaded[l], 16 * it + 16)
                    dve.wait_ge(gathered[l], 32 * it + 32)
                    need(dve, it, l, "gcols")
                    for u in range(2):
                        ins = v_.scalar_tensor_tensor(h2[:, l, u], y[:, l, u], gcols[:, l, u:u + 1], h1[:, l, u], ALU.mult, ALU.add)
                    ins.then_inc(s("h2"), 1)
                    need(dve, it, l, "h2")
                    layer_norm(dve, it, l, h2, "a")
                yield 2
                need_pair(dve, it, lanes, "rstd_a")
                settle(dve)
                for l in lanes:
                    normalise(it, l, h2, x, rstd, "x")
                yield 3
                for l in lanes:
                    need_pair(dve, it, lanes, "again_a")
                    need(dve, it, l, "x")
                    for u in range(2):
                        ins = v_.tensor_scalar(xr[:, l, u], x[:, l, u], rms[:, l, u:u + 1], consts["ns"][:], ALU.mult, ALU.mult)
                    ins.then_inc(s("xr"), 1)
                yield 8
                for l in lanes:
                    need(dve, it, l, "v_done")
                    v_.tensor_tensor(vb[:, l], ps[l][:TH, 0, :].rearrange("p (u e) -> p u e", u=2), consts["b1v"][:], ALU.add).then_inc(s("vb"), 1)
                yield 8
                for l in lanes:
                    need(dve, it, l, "bT")
                    for j, dst in ((0, qT), (1, kT)):
                        ins = v_.tensor_scalar(dst[:, l], bT[:, l], consts["gb"][:, 2 * j:2 * j + 1], consts["gb"][:, 2 * j + 1:2 * j + 2], ALU.mult, ALU.add)
                    ins.then_inc(s("qk"), 1)

            def second(it, lanes):
                yield 0
                for l in lanes:
                    need(dve, it, l, "s_done")
                    src = ps[l][:TH, 0, :2 * T].rearrange("p (u n) -> p u n", u=2)
                    v_.tensor_tensor(r1[:, l], src, consts["cosT"][:].unsqueeze(1).broadcast_to([TH, 2, T]), ALU.mult)
                    v_.tensor_tensor(r2[:, l], src, consts["sinT"][:].unsqueeze(1).broadcast_to([TH, 2, T]), ALU.mult).then_inc(s("r12"), 1)
                    need(dve, it, l, "r12")
                    v_.tensor_tensor(rot[:, l, 0], r1[:, l, 0], r2[:, l, 1], ALU.subtract)
                    v_.tensor_tensor(rot[:, l, 1], r1[:, l, 1], r2[:, l, 0], ALU.add).then_inc(s("rot"), 1)
                    need(dve, it, l, "rot")
                    v_.scalar_tensor_tensor(kern[:, l], rot[:, l], 0.0, rot[:, l], ALU.max, ALU.mult).then_inc(s("kern"), 1)
                yield 1
                for l in lanes:
                    need(dve, it, l, "o_done", "uT")
                    v_.tensor_tensor(uo[:, l], ps[l][:, 1, :2 * T].rearrange("p (c n) -> p c n", c=2), uT[:, l], ALU.mult).then_inc(s("uo"), 1)
                yield 4
                for l in lanes:
                    need(dve, it, l, "out_done", "hb")
                    v_.tensor_tensor(h3[:, l], ps[l][:TH, 0, :2 * D].rearrange("p (u d) -> p u d", u=2), hb[:, l], ALU.add).then_inc(s("h3"), 1)
                    need(dve, it, l, "h3")
                    layer_norm(dve, it, l, h3, "b")
                yield 6
                need_pair(dve, it, lanes, "rstd_b")
                settle(dve)
                for l in lanes:
                    normalise(it, l, h3, x2, rstd_b, "x2")
                yield 9
                for l in lanes:
                    need_pair(dve, it, lanes, "again_b")
                    need(dve, it, l, "x2")
                    for u in range(2):
                        ins = v_.scalar_tensor_tensor(xg[:, l, u], x2[:, l, u], rstd_c[:, l, u:u + 1], consts["gamma"][:, u], ALU.mult, ALU.mult)
                    ins.then_inc(s("xg"), 1)

            in_turns(dve, STEPS, first, second)

        @block.scalar
        def _(act):
            a_ = nc.scalar.activation
            act.wait_ge(s("consts_loaded"), nconst)
            def first(it, lanes):
                yield 5
                for l in lanes:
                    need(act, it, l, "xr_transposed")
                    a_(xrT[:, l], ps[l][:, 0, :T], ACT.Copy).then_inc(s("xrT"), 1)
                yield 7
                for l in lanes:
                    need(act, it, l, "ub_done")
                    a_(bT[:, l], ps[l][:, 1, 2 * T:3 * T], ACT.Silu, bias=consts["b1c"][:, 2:3]).then_inc(s("bT"), 1)
                    for c in range(2):
                        ins = a_(uT[:, l, c], ps[l][:, 1, T * c:T * c + T], ACT.Silu, bias=consts["b1c"][:, c:c + 1])
                    ins.then_inc(s("uT"), 1)
                yield 9
                for l in lanes:
                    need(act, it, l, "vb")
                    a_(v[:, l], vb[:, l], ACT.Silu).then_inc(s("v"), 1)

            in_turns(act, STEPS, first, idle)

        @block.tensor
        def _(pe):
            mm, tr = nc.tensor.matmul, nc.tensor.transpose
            pe.wait_ge(s("consts_loaded"), nconst)
            pe.wait_ge(s("rows_loaded"), 16)
            for g in range(2):
                ins = tr(ps[0][:TH, 0, 128 * g:128 * g + 128], rows[:, g], ident[:])
            ins.then_inc(s("rows_transposed"), 1)
            pe.wait_ge(s("gate"), 1)
            def first(it, lanes):
                yield 4
                for l in lanes:
                    need(pe, it, l, "xr")
                    for u in range(2):
                        ins = tr(ps[l][:, 0, TH * u:TH * u + TH], xr[:, l, u], ident[:TH, :TH])
                    ins.then_inc(s("xr_transposed"), 1)
                yield 6
                for l in lanes:
                    need(pe, it, l, "xrT")
                    for c in (2, 0, 1):
                        ins = mm(ps[l][:, 1, T * c:T * c + T], consts["w1"][:, (2 * EX if c == 2 else D * c):(2 * EX if c == 2 else D * c) + D], xrT[:, l], start=True, stop=True)
                    ins.then_inc(s("ub_done"), 1)
                    for u in range(2):
                        ins = mm(ps[l][:TH, 0, EX * u:EX * u + EX], xrT[:, l, TH * u:TH * u + TH], consts["w1"][:, EX:2 * EX], start=True, stop=True)
                    ins.then_inc(s("v_done"), 1)

            def second(it, lanes):
                yield 0
                for l in lanes:
                    need(pe, it, l, "qk", "vb")
                    for u in range(2):
                        ins = mm(ps[l][:TH, 0, T * u:T * u + T], kT[:, l, TH * u:TH * u + TH], qT[:, l], start=True, stop=True)
                    ins.then_inc(s("s_done"), 1)
                yield 1
                for l in lanes:
                    need(pe, it, l, "kern", "v", "uT")
                    for c in range(2):
                        for u in range(2):
                            ins = mm(ps[l][:, 1, T * c:T * c + T], v[:, l, u, D * c:D * c + D], kern[:, l, u], start=(u == 0), stop=(u == 1))
                    ins.then_inc(s("o_done"), 1)
                yield 3
                for l in lanes:
                    need(pe, it, l, "uo")
                    for u in range(2):
                        for c in range(2):
                            ins = mm(ps[l][:TH, 0, D * u:D * u + D], uo[:, l, c, TH * u:TH * u + TH], consts["w2"][:, c], start=(c == 0), stop=(c == 1))
                    ins.then_inc(s("out_done"), 1)

            in_turns(pe, STEPS, first, second)


def gather_out(net):
    nc, io, sem, slots = net.nc, net.io, net.sem, net.slots
    with ExitStack() as ctx:
        def s(name):
            return sem("g_" + name)

        cols = net.sb(ctx, "g_cols", [128, GL], I32)
        y = net.sb(ctx, "g_y", [128, GL, D])
        r3 = net.sb(ctx, "g_r3", [128, GL, D])
        out = net.sb(ctx, "g_out", [128, GL, D])
        gathered = [s(f"gathered_{l}") for l in range(GL)]
        r3_loaded = [s(f"r3_loaded_{l}") for l in range(GL)]
        stored = [s(f"out_stored_{l}") for l in range(GL)]
        r3_rows = io["r3"].rearrange("b t d -> (b t) d")
        out_rows = io["out"].rearrange("b t d -> (b t) d")
        block = ctx.enter_context(nc.Block())

        def per_block(eng, body):
            with eng.Fori(0, NT // GL) as it:
                body(GL * it, range(GL))
            body(NT - NT % GL, range(NT % GL))

        @block.sync
        def _(sp):
            def body(base, lanes):
                for l in lanes:
                    sp.wait_ge(s("sum"), base + (l + 1))
                    sp.dma_start(r3[:, l], block_rows(r3_rows, base + l)).then_inc(r3_loaded[l], 16)

            per_block(sp, body)

        @block.gpsimd
        def _(pool):
            def body(base, lanes):
                for l in lanes:
                    pool.wait_ge(s("sum"), base + (l + 1))
                    pool.sem_inc(s("settled"), 1)
                    nc.gpsimd.tensor_copy(cols[:, l:l + 1], slots[:, bass.ds(base + l, 1)]).then_inc(s("cols"), 1)
                for l in lanes:
                    pool.wait_ge(s("cols"), base + (l + 1))
                    pool.sem_inc(s("settled"), 1)
                    nc.gpsimd.indirect_dma_start(y[:, l], None, io["y1"], bass.IndirectOffsetOnAxis(cols[:, l:l + 1], 0)).then_inc(gathered[l], 16)

            per_block(pool, body)

        @block.vector
        def _(dve):
            dve.sem_inc(s("sum"), GL)

            def body(base, lanes):
                for l in lanes:
                    dve.wait_ge(gathered[l], 16 // GL * base + 16)
                    dve.wait_ge(r3_loaded[l], 16 // GL * base + 16)
                    dve.wait_ge(stored[l], 16 // GL * base + 16)
                    nc.vector.tensor_tensor(out[:, l], y[:, l], r3[:, l], ALU.add).then_inc(s("sum"), 1)

            per_block(dve, body)

        @block.scalar
        def _(act):
            for l in range(GL):
                act.sem_inc(stored[l], 16)

            def body(base, lanes):
                for l in lanes:
                    act.wait_ge(s("sum"), base + (l + 1 + GL))
                    act.dma_start(block_rows(out_rows, base + l), out[:, l]).then_inc(stored[l], 16)

            per_block(act, body)
            for l in range(GL):
                act.wait_ge(stored[l], 16 * ((NT - l + GL - 1) // GL) + 16)


def host_arrays(inp):
    f = np.float32
    c = np.ascontiguousarray
    a = {}
    x = inp["x"].reshape(B // XG // 2, 2, XG, CH, 8, PATCH, 8, PATCH)
    x = x.transpose(0, 1, 3, 5, 7, 2, 4, 6).reshape(B // XG, 3, 7, KP, XG * PATCHES)
    a["x"] = c(x.transpose(0, 1, 3, 2, 4))
    a["tok_w"] = c(inp["L0_tok_W"].T.reshape(KC, KP, D).transpose(1, 0, 2))
    a["tok_b"] = c(inp["L0_tok_b"].reshape(D, 1))
    pos = inp["L0_tok_pos_embed"]
    a["tok_posT"] = c(pos[1:].T)
    a["tok_cls"] = c(np.broadcast_to(inp["L0_tok_class_token"], (B, D)))
    a["tok_pos0"] = c(np.broadcast_to(pos[:1], (B, D)))
    a["txt"] = c(inp["txt"])
    a["ident"] = np.eye(128, dtype=f)

    ang = np.outer(np.arange(T, dtype=f), 1.0 / 500000.0 ** (np.arange(0, DR, 2, dtype=f) / DR))
    emb = np.concatenate([ang, ang], -1).astype(f)
    cos, sin = np.cos(emb).astype(f), np.sin(emb).astype(f)
    sin = sin * np.where(np.arange(DR) < DR // 2, -1, 1).astype(f)
    rot = np.r_[DR // 2:DR, 0:DR // 2]
    one_head = lambda r, n: np.concatenate([n, r], 1).T
    p = {}
    p["ident"] = np.eye(128, dtype=f)
    p["identb"] = np.eye(128, dtype=f).astype(np.dtype("bfloat16"))
    row = np.arange(RW).reshape(NCH, CR).T[:, :, None]
    key = np.arange(T)[None, None]
    hidden = (key > row % T) & (row < G * T)
    p["maskb"] = np.where(hidden, NEG, 0.0).astype(f).astype(np.dtype("bfloat16"))
    p["cosq"] = np.tile(one_head(cos, np.ones((T, HD - DR), f)), (2, 1))
    p["sinq"] = np.tile(one_head(sin, np.zeros((T, HD - DR), f)), (2, 1))
    p["cosk"] = np.tile(cos.reshape(2, TH, DR).transpose(1, 0, 2), (1, 1, KVH))
    p["sink"] = np.tile(sin.reshape(2, TH, DR).transpose(1, 0, 2), (1, 1, KVH))
    g = lambda n: inp["L0_attn_" + n]
    kr = g("W_KR").reshape(D, KVH, DR)
    p["wlat"] = np.concatenate([g("W_DQ"), g("W_DKV"), kr.reshape(D, -1), kr[:, :, rot].reshape(D, -1)], 1)
    p["wkv"] = np.concatenate([g("W_UK"), g("W_UV")], 1)
    uq, qr = g("W_UQ").reshape(64, H, HD - DR), g("W_QR").reshape(64, H, DR)
    pack = lambda n, r: np.concatenate([n, r], 2).reshape(64, KVH, G, HD).transpose(0, 2, 1, 3).reshape(64, G, 128)
    p["wqa"] = pack(uq, qr)
    p["wqp"] = pack(uq, qr[:, :, rot])
    p["qln"] = g("q_ln_w").reshape(64, 1)
    p["kvln"] = g("kv_ln_w").reshape(D, 1)
    p["qhn"] = np.tile(g("q_head_norm_w"), 2).reshape(D, 1)
    p["khn"] = np.tile(g("k_head_norm_w"), 2).reshape(D, 1)
    p["half_sum"] = np.kron(np.eye(2, dtype=f), np.ones((64, 1), f))
    p["wo2"] = g("W_O").reshape(KVH, G, HD, D).transpose(0, 2, 1, 3).reshape(D, G, D)
    p["wvrT"] = g("W_VR").T.reshape(KVH, G, HD, D).transpose(0, 2, 1, 3).reshape(D, G, D)
    g = lambda n: inp["L0_ffn_" + n]
    rows = lambda w: np.broadcast_to(w, (TH, 2, D))
    p["wq"], p["wk"], p["wv"], p["wproj"] = g("Wq"), g("Wk"), g("Wv"), g("Wo")
    p["bq"], p["bk"] = g("bq").reshape(D, 1), g("bk").reshape(D, 1)
    p["bv"] = np.broadcast_to(g("bv")[:, None], (D, TH))
    for k, n in (("bo", "bo"), ("lng", "ln1_g"), ("lnb", "ln1_b")):
        p[k] = np.broadcast_to(g(n), (TH, D))
    p["hmask"] = np.kron(np.eye(H, dtype=f), np.ones((16, 1), f)) * f(0.25)
    a.update({"c0_" + k: c(p[k]) for k in L0_CONSTS})

    bf = np.dtype("bfloat16")
    for tag, ne in (("cr0_", E0), ("cr1_", T1)):
        a[tag + "ident"] = np.eye(128, dtype=f)
        a[tag + "upper"] = np.triu(np.ones((128, 128), f), 1).astype(bf)
        a[tag + "onesb"] = np.ones((128, 128), bf)
        k, e = np.arange(ne)[:, None], np.arange(ne)[None]
        a[tag + "scan"] = np.concatenate([(k <= e) * 1.0, (k < e) * 128.0], 1).astype(bf)
        a[tag + "jcol"] = (2 * np.arange(128)[:, None] + np.arange(2)[None]).astype(f)
    a["cr0_gw"] = c(g("gate_W"))
    a["cr0_gb"] = c(np.broadcast_to(g("gate_b"), (128, E0)))
    a["cr0_order"] = c(np.broadcast_to(np.arange(E0, 0, -1, dtype=f), (128, E0)))
    a["cr1_order"] = c(np.broadcast_to(np.concatenate([np.arange(CL - 1, -1, -1), np.arange(T1 - 1, -1, -1)]).astype(f), (128, CL + T1)))

    a["f0_w"] = np.concatenate([
        g("W1"), g("W2").reshape(E0, FF // 128, 128, D).transpose(0, 2, 1, 3).reshape(E0, 128, FF),
        g("b1").reshape(E0, FF // 128, 128).transpose(0, 2, 1), np.broadcast_to(g("b2")[:, None], (E0, 128, D))], 2)

    g = lambda n: inp["L1_attn_" + n]
    p = {"ident": np.eye(128, dtype=f)}
    half = T // 2
    inv = (f(10000.0) ** (-np.arange(half, dtype=f) / f(half))).astype(f)
    ang = np.arange(T, dtype=f)[None] * inv[:, None]
    p["cosT"], p["sinT"] = np.cos(ang).astype(f) / 128, np.sin(ang).astype(f) / 128
    p["w1"] = g("W1")
    b1 = g("b1")
    p["b1c"] = np.stack([b1[:D], b1[D:2 * D], b1[4 * D:]], 1)
    p["b1v"] = np.broadcast_to(b1[2 * D:4 * D], (TH, 2, 2 * D))
    p["gb"] = np.stack([g("gamma")[0], g("beta")[0], g("gamma")[1], g("beta")[1]], 1)
    p["w2"] = g("W2").reshape(2, D, D).transpose(1, 0, 2)
    p["b2"] = rows(g("b2"))
    p["ns"] = np.broadcast_to(g("norm_scale"), (TH, 1))
    g = lambda n: inp["L1_ffn_" + n]
    p["gamma"], p["beta"] = rows(g("gamma")), rows(g("beta"))
    a.update({"c2_" + k: c(p[k]) for k in L1_CONSTS})
    a["wdT"] = c(g("Wd").transpose(2, 0, 1))
    a["f1_w"] = np.concatenate([g("Wd").transpose(0, 2, 1), g("Wu").transpose(0, 2, 1), g("spline_bases"), g("spline_slopes"),
                                np.broadcast_to(g("scale")[:, None, None], (T1, 128, 1))], 2)
    a["gidx"] = c(np.broadcast_to(np.arange(GRID, dtype=f), (DH, GRID)))
    return a


SCRATCH = {"r3": (B, T, D), "xf": (B, T, D), "y0": (NB0 * 128, D), "y1": (NB1 * 128, D), "slot_gate": (2, N), "h1": (B, T, D), "t": (B, T, D), "h0": (B, T, D), "sorted0": (NB0 * 128, D), "sorted1": (NB1 * 128, D)}


def build(nc, arrays, phases, debug=False, given=()):
    io = {}
    for k, v in arrays.items():
        io[k] = nc.dram_tensor(f"in_{k}", v.shape, mybir.dt.from_np(v.dtype), kind="ExternalInput").ap()
    for k, shape in SCRATCH.items():
        io[k] = nc.dram_tensor(k, shape, F32, **({"kind": "ExternalInput" if k in given else "ExternalOutput"} if debug else {})).ap()
    io["eb"] = nc.dram_tensor("eb", (128, 2), I32, **({"kind": "ExternalOutput"} if debug else {})).ap()
    io["out"] = nc.dram_tensor("out_0", (B, T, D), F32, kind="ExternalOutput").ap()
    with ExitStack() as ctx:
        net = Net(nc, io)
        net.slots = net.sb(ctx, "slots", [128, NT], I32)
        for phase in phases:
            phase(net)
            net.end_phase()


PHASES = (patch_tokens, layer0, route_experts, experts, layer1, route_tiles, spline_tiles, gather_out)


def kernel(**inputs):
    from concourse import bacc
    from concourse.bass_utils import run_bass_kernel_spmd

    arrays = host_arrays({k: np.asarray(v) for k, v in inputs.items()})
    nc = bacc.Bacc("TRN2", target_bir_lowering=False, num_devices=1)
    build(nc, arrays, PHASES)
    r = run_bass_kernel_spmd(nc, [{f"in_{k}": v for k, v in arrays.items()}], core_ids=[0])
    return r.results[0]["out_0"]
```
